# Optimizing a Trainium2 kernel written in Bass

```python
import numpy as np
import jax
import jax.numpy as jnp

def _softmax(x, axis=-1):
    return jax.nn.softmax(x, axis=axis)

def _gelu(x):
    return jax.nn.gelu(x, approximate=True)

def _silu(x):
    return jax.nn.silu(x)

def _sigmoid(x):
    return jax.nn.sigmoid(x)

def _layernorm(x, axis=-1, eps=1e-05):
    m = jnp.mean(x, axis=axis, keepdims=True)
    v = jnp.var(x, axis=axis, keepdims=True)
    return (x - m) / jnp.sqrt(v + eps)

def _scatter_add(tgt, idx, src, axis=0):
    return tgt.at[idx].add(src)

def _segment_sum(src, seg, n):
    return jax.ops.segment_sum(src, seg, n)
kernel_name = 'mk_hybrid_d1_jaxref_r8_1c411d'

def setup_inputs(seed: int=0):
    np.random.seed(seed)
    _w = jnp.asarray

    def _L0_attn_a_setup():
        import jax, jax.numpy as jnp
        import numpy as np
        EPS = 1e-12

        def _l2norm(t):
            n = jnp.linalg.norm(t, axis=-1, keepdims=True)
            return t / jnp.maximum(n, EPS)
        key = jax.random.key(seed)
        kx, kq, kk, kv = jax.random.split(key, 4)
        B, N, D = (8, 512, 128)
        s = 1.0 / np.sqrt(D)
        return {'x': jax.random.normal(kx, (B, N, D), dtype=jnp.float32), 'W_q': jax.random.normal(kq, (D, D), dtype=jnp.float32) * s, 'W_k': jax.random.normal(kk, (D, D), dtype=jnp.float32) * s, 'W_v': jax.random.normal(kv, (D, D), dtype=jnp.float32) * s}
    _L0_attn_a_in = _L0_attn_a_setup()

    def _L0_attn_b_setup():
        import jax, jax.numpy as jnp
        import numpy as np
        DIM = 128
        N_HEADS = 16
        HEAD_DIM = DIM // N_HEADS
        SCALE = HEAD_DIM ** (-0.5)
        key = jax.random.key(seed)
        ks = jax.random.split(key, 5)
        x = jax.random.normal(ks[0], (4, 256, DIM), dtype=jnp.float32)
        bound = 1.0 / np.sqrt(DIM)
        qkv_w = jax.random.uniform(ks[1], (3 * DIM, DIM), minval=-bound, maxval=bound, dtype=jnp.float32)
        qkv_b = jax.random.uniform(ks[2], (3 * DIM,), minval=-bound, maxval=bound, dtype=jnp.float32)
        out_w = jax.random.uniform(ks[3], (DIM, DIM), minval=-bound, maxval=bound, dtype=jnp.float32)
        out_b = jax.random.uniform(ks[4], (DIM,), minval=-bound, maxval=bound, dtype=jnp.float32)
        return {'x': x, 'qkv_w': qkv_w, 'qkv_b': qkv_b, 'out_w': out_w, 'out_b': out_b}
    _L0_attn_b_in = _L0_attn_b_setup()

    def _L0_ffn_setup():
        import jax, jax.numpy as jnp
        import numpy as np
        TOP_K = 2

        def _mlp(x, w1, b1, w2, b2):
            h = jax.nn.gelu(jnp.einsum('bsd,di->bsi', x, w1) + b1)
            return jnp.einsum('bsi,id->bsd', h, w2) + b2
        key = jax.random.key(seed)
        ks = jax.random.split(key, 8)
        B, S, D, I, E = (2, 256, 128, 512, 8)
        s_in = 1.0 / np.sqrt(D)
        s_mid = 1.0 / np.sqrt(I)
        return {'x': jax.random.normal(ks[0], (B, S, D), jnp.float32), 'gate_w': jax.random.normal(ks[1], (D, E), jnp.float32) * s_in, 'gate_b': jnp.zeros((E,), jnp.float32), 'sh_w1': jax.random.normal(ks[2], (D, I), jnp.float32) * s_in, 'sh_b1': jnp.zeros((I,), jnp.float32), 'sh_w2': jax.random.normal(ks[3], (I, D), jnp.float32) * s_mid, 'sh_b2': jnp.zeros((D,), jnp.float32), 'ew1': jax.random.normal(ks[4], (E, D, I), jnp.float32) * s_in, 'eb1': jnp.zeros((E, I), jnp.float32), 'ew2': jax.random.normal(ks[5], (E, I, D), jnp.float32) * s_mid, 'eb2': jnp.zeros((E, D), jnp.float32)}
    _L0_ffn_in = _L0_ffn_setup()
    _d = {'L0_attn_a_x': _L0_attn_a_in['x'], 'L0_attn_a_W_q': _L0_attn_a_in['W_q'], 'L0_attn_a_W_k': _L0_attn_a_in['W_k'], 'L0_attn_a_W_v': _L0_attn_a_in['W_v'], 'L0_attn_b_qkv_w': _L0_attn_b_in['qkv_w'], 'L0_attn_b_qkv_b': _L0_attn_b_in['qkv_b'], 'L0_attn_b_out_w': _L0_attn_b_in['out_w'], 'L0_attn_b_out_b': _L0_attn_b_in['out_b'], 'L0_ffn_gate_w': _L0_ffn_in['gate_w'], 'L0_ffn_gate_b': _L0_ffn_in['gate_b'], 'L0_ffn_sh_w1': _L0_ffn_in['sh_w1'], 'L0_ffn_sh_b1': _L0_ffn_in['sh_b1'], 'L0_ffn_sh_w2': _L0_ffn_in['sh_w2'], 'L0_ffn_sh_b2': _L0_ffn_in['sh_b2'], 'L0_ffn_ew1': _L0_ffn_in['ew1'], 'L0_ffn_eb1': _L0_ffn_in['eb1'], 'L0_ffn_ew2': _L0_ffn_in['ew2'], 'L0_ffn_eb2': _L0_ffn_in['eb2']}
    _x0 = _d['L0_attn_a_x']
    _d['L0_attn_a_x'] = jax.random.normal(jax.random.fold_in(jax.random.key(seed), 1), (16, 256, 128), dtype=_x0.dtype)
    del _x0
    return _d

def reference(L0_attn_a_x, L0_attn_a_W_q, L0_attn_a_W_k, L0_attn_a_W_v, L0_attn_b_qkv_w, L0_attn_b_qkv_b, L0_attn_b_out_w, L0_attn_b_out_b, L0_ffn_gate_w, L0_ffn_gate_b, L0_ffn_sh_w1, L0_ffn_sh_b1, L0_ffn_sh_w2, L0_ffn_sh_b2, L0_ffn_ew1, L0_ffn_eb1, L0_ffn_ew2, L0_ffn_eb2):

    def _L0_attn_a_ref(x, W_q, W_k, W_v):
        import jax, jax.numpy as jnp
        import numpy as np
        EPS = 1e-12

        def _l2norm(t):
            n = jnp.linalg.norm(t, axis=-1, keepdims=True)
            return t / jnp.maximum(n, EPS)
        Q = _l2norm(jnp.einsum('bnd,ed->bne', x, W_q))
        K = _l2norm(jnp.einsum('bnd,ed->bne', x, W_k))
        V = jnp.einsum('bnd,ed->bne', x, W_v)
        C = x.shape[1]
        global_feat = jnp.sum(K * V, axis=1, keepdims=True) / C
        return Q * global_feat

    def _L0_attn_b_ref(x, qkv_w, qkv_b, out_w, out_b):
        import jax, jax.numpy as jnp
        import numpy as np
        DIM = 128
        N_HEADS = 16
        HEAD_DIM = DIM // N_HEADS
        SCALE = HEAD_DIM ** (-0.5)
        b, n, dim = x.shape
        qkv = x @ qkv_w.T + qkv_b
        qkv = qkv.reshape(b, n, 3, N_HEADS, HEAD_DIM)
        qkv = jnp.transpose(qkv, (2, 0, 3, 1, 4))
        q, k, v = (qkv[0], qkv[1], qkv[2])
        attn = jnp.einsum('bhqd,bhkd->bhqk', q, k) * SCALE
        attn = jax.nn.softmax(attn, axis=-1)
        out = jnp.einsum('bhqk,bhkd->bhqd', attn, v)
        out = jnp.transpose(out, (0, 2, 1, 3)).reshape(b, n, dim)
        return out @ out_w.T + out_b

    def _L0_ffn_ref(x, gate_w, gate_b, sh_w1, sh_b1, sh_w2, sh_b2, ew1, eb1, ew2, eb2):
        import jax, jax.numpy as jnp
        import numpy as np
        TOP_K = 2

        def _mlp(x, w1, b1, w2, b2):
            h = jax.nn.gelu(jnp.einsum('bsd,di->bsi', x, w1) + b1)
            return jnp.einsum('bsi,id->bsd', h, w2) + b2
        E = ew1.shape[0]
        router_probs = jax.nn.softmax(jnp.einsum('bsd,de->bse', x, gate_w) + gate_b, axis=-1)
        expert_values, expert_indices = jax.lax.top_k(router_probs, k=TOP_K)
        expert_values = expert_values / (jnp.sum(expert_values, axis=-1, keepdims=True) + 1e-09)
        h = jax.nn.gelu(jnp.einsum('bsd,edi->bsei', x, ew1) + eb1)
        all_outputs = jnp.einsum('bsei,eid->bsed', h, ew2) + eb2
        one_hot = jax.nn.one_hot(expert_indices, E, dtype=x.dtype)
        weights_E = (one_hot * expert_values[..., None]).sum(axis=2)
        moe_out = jnp.einsum('bse,bsed->bsd', weights_E, all_outputs)
        return x + _mlp(x, sh_w1, sh_b1, sh_w2, sh_b2) + moe_out
    x = L0_attn_a_x
    x = x + _L0_attn_a_ref(_layernorm(x, axis=-1), L0_attn_a_W_q, L0_attn_a_W_k, L0_attn_a_W_v)
    x = x + _L0_ffn_ref(_layernorm(x, axis=-1), L0_ffn_gate_w, L0_ffn_gate_b, L0_ffn_sh_w1, L0_ffn_sh_b1, L0_ffn_sh_w2, L0_ffn_sh_b2, L0_ffn_ew1, L0_ffn_eb1, L0_ffn_ew2, L0_ffn_eb2)
    x = x + _L0_attn_b_ref(_layernorm(x, axis=-1), L0_attn_b_qkv_w, L0_attn_b_qkv_b, L0_attn_b_out_w, L0_attn_b_out_b)
    x = x + _L0_ffn_ref(_layernorm(x, axis=-1), L0_ffn_gate_w, L0_ffn_gate_b, L0_ffn_sh_w1, L0_ffn_sh_b1, L0_ffn_sh_w2, L0_ffn_sh_b2, L0_ffn_ew1, L0_ffn_eb1, L0_ffn_ew2, L0_ffn_eb2)
    return x

_drawn_inputs = setup_inputs


def setup_inputs(seed=0):
    import zlib

    import numpy as np

    out = dict(_drawn_inputs(seed))
    spreads = {'L0_ffn_gate_b': (0.0, 0.1),
     'L0_ffn_sh_b1': (0.0, 0.1),
     'L0_ffn_sh_b2': (0.0, 0.1),
     'L0_ffn_eb1': (0.0, 0.1),
     'L0_ffn_eb2': (0.0, 0.1)}
    factors = {'L0_attn_a_W_q': 26.22,
     'L0_attn_a_W_k': 27.651,
     'L0_attn_a_W_v': 27.262,
     'L0_attn_b_qkv_b': 3.123}
    for name, (base, spread) in spreads.items():
        noise = np.random.default_rng([zlib.crc32(name.encode()), seed]).standard_normal(out[name].shape)
        drawn = base * np.exp(spread * noise) if base else spread * noise
        out[name] = jnp.asarray(drawn.astype(out[name].dtype))
    for name, factor in factors.items():
        out[name] = (out[name] * factor).astype(out[name].dtype)
    return out
```

```python
from contextlib import ExitStack

import concourse.bass as bass
from concourse import mybir

F32 = mybir.dt.float32
F16 = mybir.dt.float16
I32 = mybir.dt.int32
ALU = mybir.AluOpType
ACT = mybir.ActivationFunctionType
AX_X = mybir.AxisListType.X
ds = bass.ds


def build(nc, x, W_q, W_k, W_v, qkv_w, qkv_b, out_w, out_b, gate_w, gate_b, sh_w1, sh_b1, sh_w2,
          sh_b2, ew1, eb1, ew2, eb2, out):
    NBATCH, SEQ, D = x.shape
    P = 128
    T = NBATCH * SEQ // P
    CB = SEQ // P
    E, _, I = ew1.shape
    NE = E + 1
    CH = I // P
    TOPK = 2
    NBLK = TOPK * T + E
    NHEAD, HD = 16, D // 16
    HG = NHEAD // 4
    assert (D, CB, HD) == (128, 2, 8) and NBLK % 8 == 0 and T % 4 == 0

    XS = 8.0
    WS = 64.0
    PS = XS * WS
    KX = 16384.0
    RND = 12582912.0
    HALF = 63.5 / 128

    B1, B2 = 0, NE * I
    BG = B2 + NE * D
    BQKV = BG + E
    BO = BQKV + 3 * D
    BQS = BO + D
    BKS = BQS + 4 * P
    BN = BKS + 4 * P

    ctx = ExitStack()
    with ctx:
        def sb(name, shape, dt):
            return ctx.enter_context(nc.sbuf_tensor(name, shape, dt))

        def sem(name):
            return ctx.enter_context(nc.semaphore(name))

        xres = sb("xres", [P, T, D], F32)
        xn = sb("xn", [P, T, D], F32)
        hl = sb("hl", [P, T, 2 * D], F16)
        xT = sb("xT", [P, T, 2 * P], F16)
        w1s = sb("w1s", [P, NE, 2, I], F16)
        w2s = sb("w2s", [P, NE, 2, CH * D], F16)
        bt = sb("bt", [P, BN], F16)
        gws = sb("gws", [P, 2, E], F16)
        waT = sb("waT", [P, 2, 3 * D], F16)
        wbT = sb("wbT", [P, 2, 4 * D], F16)
        wqk = sb("wqk", [P, 2, 2, 4 * P], F16)
        scratch = sb("scratch", [P, 4096], F32)
        ident16 = sb("ident16", [P, P], F16)
        ident32 = sb("ident32", [P, P], F32)
        upper16 = sb("upper16", [P, P], F16)
        ones16 = sb("ones16", [P, P], F16)
        cXS = sb("cXS", [P, SEQ], F16)
        zero16 = sb("zero16", [P, P], F16)
        onesC = sb("onesC", [P, P], F32)
        iota_i = sb("iota_i", [P, P], I32)
        iota_f = sb("iota_f", [P, P], F32)
        ids_i = sb("ids_i", [P, T], I32)
        ids_f = sb("ids_f", [P, T], F32)
        part_i = sb("part_i", [P, 4], I32)
        nsel = sb("nsel", [P, 2], F32)
        eps = sb("eps", [P, 1], F32)
        cWS = sb("cWS", [P, 1], F32)
        reset = sb("reset", [P, E, T], F32)
        stats = sb("stats", [P, T, 6], F32)
        mean = sb("mean", [P, T], F32)
        var = sb("var", [P, T], F32)
        gap = sb("gap", [P, T], F32)
        rstd = sb("rstd", [P, T], F32)
        bnat = sb("bnat", [P, 56], F32)
        bhi = sb("bhi", [P, 56], F16)
        blo = sb("blo", [P, 56], F16)
        ssq = sb("ssq", [P, 2, CB, 2], F32)
        rnorm = sb("rnorm", [P, 2, CB, 2], F32)
        h32 = sb("h32", [P, 4, I], F32)
        hhi = sb("hhi", [P, 4, I], F16)
        hlo = sb("hlo", [P, 4, I], F16)
        xg = sb("xg", [P, 4, 2 * P], F16)
        yst = sb("yst", [P, 4, D], F32)
        gidx = sb("gidx", [P, 4, 4], I32)
        yidx = sb("yidx", [P, 4, 4], I32)
        prob = sb("prob", [P, T, E], F32)
        rt = [sb(f"rt{i}", [P, T, E], F32) for i in range(3)]
        mask = [sb(f"mask{k}", [P, T, E], F32) for k in range(TOPK)]
        mask16 = sb("mask16", [P, E, T], F16)
        rs = [sb(f"rs{i}", [P, T], F32) for i in range(3)]
        topp = sb("topp", [P, TOPK, T], F32)
        wtop = sb("wtop", [P, TOPK, T], F32)
        cum = sb("cum", [P, E, T], F32)
        slotb = sb("slotb", [P, E, T], F32)
        e8 = [sb(f"e8_{i}", [P, E], F32) for i in range(4)]
        slot = sb("slot", [P, TOPK, T], F32)
        blk = sb("blk", [P, TOPK, T], F32)
        row = sb("row", [P, TOPK, T], F32)
        slot_i = sb("slot_i", [P, TOPK, T], I32)
        bexp = sb("bexp", [P, NBLK, E], F32)
        bexpf = sb("bexpf", [P, NBLK], F32)
        bexp_i = sb("bexp_i", [P, NBLK], I32)
        tok_i = sb("tok_i", [P, NBLK], I32)
        onerow = sb("onerow", [P, 2, TOPK, P], F32)
        oneblk = sb("oneblk", [P, 2, TOPK, NBLK], F32)

        ps = ctx.enter_context(nc.psum_tensor("ps", [P, 8, 512], F32))

        rows_dram = [nc.dram_tensor(f"rows{r}", [T * P, 2 * D], F16, kind="Internal").ap()
                     for r in range(2)]
        y_dram = [nc.dram_tensor(f"ysorted{r}", [NBLK * P, D], F32, kind="Internal").ap()
                  for r in range(2)]

        qst = sb("qst", [P, 2, HG, SEQ], F16)
        kst = sb("kst", [P, 2, HG, SEQ], F16)
        vx = sb("vx", [P, 2, CB, NHEAD, 32], F32)
        mx = sb("mx", [P, CB, NHEAD], F32)
        rsum = sb("rsum", [P, CB, NHEAD], F32)
        prb = scratch[:, :].rearrange("p (n k) -> p n k", n=8)
        qkhi = hhi[:, 0:2, :]
        negmax = hlo[:, 0:2, :]
        qst2 = hlo[:, 2:4, :].rearrange("p a (b n) -> p (a b) n", b=2)
        oT = h32[:, 0:2, :]
        attn = h32[:, 2, 0:CB * D].rearrange("p (c d) -> p c d", c=CB)
        ahi, alo = xg[:, 0, :], xg[:, 1, :]

        def part(at, n, dt=F32):
            return scratch[:, at:at + n].bitcast(dt) if dt != F32 else scratch[:, at:at + n]

        junk = part(0, 4 * D).rearrange("p (n d) -> p n d", n=4)
        kn = part(4 * D, 4 * D).rearrange("p (u c d) -> p u c d", u=2, c=CB)
        kv = part(8 * D, 4 * D).rearrange("p (u c d) -> p u c d", u=2, c=CB)
        qg = part(12 * D, 4 * D).rearrange("p (u c d) -> p u c d", u=2, c=CB)
        gf = part(16 * D, 2 * D).rearrange("p (u d) -> p u d", u=2)
        grow = part(0, 8 * D, F16).rearrange("p (u n) -> p u n", u=8)
        gy = part(8 * D, 8 * D).rearrange("p (s u d) -> p s u d", s=2, u=4)

        wstage = h32[:, :, :].rearrange("p (u w) n -> p u w n", u=2)
        wnat = xn[:, 0:7, :]
        gstage = xn[:, 7, 0:E]

        xd = x.rearrange("b (c p) d -> p (b c) d", p=P)
        od = out.rearrange("b (c p) d -> p (b c) d", p=P)

        BIASES, col = [], 0
        for at, n, b in ((B1, E * I, eb1.rearrange("e i -> (e i)")), (B1 + E * I, I, sh_b1),
                         (B2, E * D, eb2.rearrange("e d -> (e d)")), (B2 + E * D, D, sh_b2),
                         (BQKV, 3 * D, qkv_b), (BO, D, out_b), (BG, E, gate_b)):
            rows = min(P, n)
            BIASES.append((at, n, rows, col, b.rearrange("(p c) -> p c", p=rows)))
            col += n // rows
        NBIAS = col

        x_in = sem("x_in")
        wnat_in = sem("wnat_in")
        bias_in = sem("bias_in")
        bias_hi = sem("bias_hi")
        bias_lo = sem("bias_lo")
        bias_rows = sem("bias_rows")
        ewt_in = [sem(f"ewt_in{u}") for u in range(2)]
        ewt_used = sem("ewt_used")
        const_made = sem("const_made")
        pool_step = sem("pool_step")
        wT_turned = sem("wT_turned")
        wT_hi = sem("wT_hi")
        wT_lo = sem("wT_lo")
        gate_split = sem("gate_split")
        slots_made = sem("slots_made")
        rows_found = sem("rows_found")
        stored = sem("stored")

        class Ln:
            stats = sem("ln_stats")
            var = sem("ln_var")
            merge = sem("ln_merge")
            std = sem("ln_std")
            rstd = sem("ln_rstd")
            norm = sem("ln_norm")
            hi = sem("ln_hi")
            lo = sem("ln_lo")
            turned = sem("ln_turned")
            xT = sem("ln_xT")
            added = sem("ln_added")

        class Mix:
            qkv = sem("a_qkv")
            ssq = sem("a_ssq")
            std = sem("a_std")
            clamped = sem("a_clamped")
            rnorm = sem("a_rnorm")
            kn = sem("a_kn")
            kv = sem("a_kv")
            mean = sem("a_mean")
            gf = sem("a_gf")
            qg = sem("a_qg")
            done = sem("a_done")

        class Moe:
            def __init__(self, r):
                self.logits = sem(f"m{r}_logits")
                self.shifted = sem(f"m{r}_shifted")
                self.exp = sem(f"m{r}_exp")
                self.step = sem(f"m{r}_step")
                self.mask = sem(f"m{r}_mask")
                self.rank = sem(f"m{r}_rank")
                self.onehot = sem(f"m{r}_onehot")
                self.index = sem(f"m{r}_index")
                self.tok = sem(f"m{r}_tok")
                self.up = sem(f"m{r}_up")
                self.gelu = sem(f"m{r}_gelu")
                self.hi = sem(f"m{r}_hi")
                self.split = sem(f"m{r}_split")
                self.down = sem(f"m{r}_down")
                self.y = sem(f"m{r}_y")
                self.rows_out = sem(f"m{r}_rows_out")
                self.gidx = sem(f"m{r}_gidx")
                self.gath = [sem(f"m{r}_gath{u}") for u in range(8)]
                self.turn = sem(f"m{r}_turn")
                self.xg = sem(f"m{r}_xg")
                self.y_out = [sem(f"m{r}_y_out{u}") for u in range(4)]
                self.yidx = sem(f"m{r}_yidx")
                self.ygath = [sem(f"m{r}_ygath{u}") for u in range(4)]
                self.half = sem(f"m{r}_half")
                self.last = sem(f"m{r}_last")

        moe = [Moe(r) for r in range(2)]

        class Att:
            cleared = sem("t_cleared")
            full = sem("t_full")
            hi = sem("t_hi")
            stack = sem("t_stack")
            v = sem("t_v")
            score = sem("t_score")
            mx = sem("t_mx")
            neghi = sem("t_neghi")
            neg = sem("t_neg")
            q2 = sem("t_q2")
            scoreT = sem("t_scoreT")
            prob = sem("t_prob")
            pv = sem("t_pv")
            oT = sem("t_oT")
            rsum = sem("t_rsum")
            attn = sem("t_attn")
            ahi = sem("t_ahi")
            alo = sem("t_alo")
            done = sem("t_done")

        class Fill:
            def __init__(self, i, first, *readers):
                self.i, self.first, self.k, self.readers = i, first, 0, list(readers)

            def next(self):
                f = self.first + self.k
                self.k += 1
                return f % 2, self.i * 22 + f + 1

            def bank_free(self, semaphore, count):
                self.readers.append((semaphore, count))
                return self.readers.pop(0)

        LAST = NBATCH - 1

        def attention(eng, start, body, end):
            def projected(b):
                return (Att.stack, 4 * b + 8), (Att.v, b + 2)

            start(Fill(0, 0, None, None))
            body(0, 0, Fill(0, 12, *projected(0)), False, True, True)
            with eng.Fori(0, (NBATCH - 4) // 2) as i:
                body(2 * i + 1, 1, Fill(i, 19, *projected(2 * i + 1)), True, True, True)
                body(2 * i + 2, 0, Fill(i, 30, *projected(2 * i + 2)), True, True, True)
            at = 19 + 11 * (NBATCH - 4)
            body(LAST - 2, 1, Fill(0, at, *projected(LAST - 2)), True, True, True)
            body(LAST - 1, 0, Fill(0, at + 11, *projected(LAST - 1)), True, True, False)
            body(LAST, 1, Fill(0, at + 17, (Att.q2, 2 * LAST + 1), (Att.q2, 2 * LAST + 2)), True, False, False)
            end(Fill(0, at + 21, (Att.alo, LAST), (Att.done, LAST)), LAST)

        block = ctx.enter_context(nc.Block())

        HB = [ps[:, u, :] for u in range(4)]
        YB = [ps[:, 4 + u, 0:D] for u in range(2)]
        TB = [ps[:, 6 + u, :].bitcast(F16) for u in range(2)]
        IDX = ps[:, 7, 0:NBLK]
        GATE = ps[:, 4, 0:T * E]
        RANK = ps[:, 5, 0:E * T]
        TOT = ps[:, 5, E * T:2 * E * T]

        def two(ap, t):
            return ap[:, ds(2 * t, 2), :]

        @block.sync
        def _(sp):
            for g in range(4):
                n = T // 4
                sp.dma_start(xres[:, g * n:(g + 1) * n, :], xd[:, g * n:(g + 1) * n, :]).then_inc(x_in, 16)
            for i, w in enumerate((W_q, W_k, W_v)):
                sp.dma_start(wnat[:, i, :], w).then_inc(wnat_in, 16)
            sp.dma_start(wnat[:, 3:6, :], qkv_w.rearrange("(m p) d -> p m d", p=P)).then_inc(wnat_in, 16)
            sp.dma_start(wnat[:, 6, :], out_w).then_inc(wnat_in, 16)
            sp.dma_start(gstage, gate_w).then_inc(wnat_in, 16)
            for at, n, rows, c, b in BIASES:
                sp.dma_start(bnat[0:rows, c:c + n // rows], b).then_inc(bias_in, 16)

            def expert(e, u, w1, w2):
                sp.dma_start(wstage[:, u, 0, :], w1).then_inc(ewt_in[u], 16)
                sp.dma_start(wstage[:, u, 1, :].rearrange("p (c d) -> p c d", c=CH), w2).then_inc(ewt_in[u], 16)

            def one(w, e):
                return w[ds(e, 1), :, :].rearrange("a p n -> (a p) n")

            def two_of(e):
                return one(ew1, e), one(ew2, e).rearrange("(c p) d -> p c d", p=P)

            for u in range(2):
                expert(u, u, *two_of(u))
            sp.wait_ge(bias_lo, 1)
            for at, n, rows, c, b in BIASES:
                for r, half in ((0, bhi), (1, blo)):
                    sp.dma_start(bt[r:r + 1, at:at + n], half[0:rows, c:c + n // rows]).then_inc(bias_rows, 16)
            with sp.Fori(0, (E - 2) // 2) as i:
                for u in range(2):
                    sp.wait_ge(ewt_used, 2 * i + u + 1)
                    expert(0, u, *two_of(2 * i + 2 + u))
            sp.wait_ge(ewt_used, E - 1)
            expert(E, 0, sh_w1, sh_w2.rearrange("(c p) d -> p c d", p=P))

            def moe_stores(r):
                m, l, first = moe[r], Ln, (2 * r + 1) * NBATCH
                rows = rows_dram[r].rearrange("(t p) n -> p t n", p=P)
                with sp.Fori(0, NBATCH) as b:
                    sp.wait_ge(l.lo, first + b + 1)
                    sp.dma_start(two(rows, b), two(hl, b)).then_inc(m.rows_out, 16)
                ys = y_dram[r].rearrange("(n p) d -> p n d", p=P)
                with sp.Fori(0, NBLK // 4) as i:
                    for u in range(4):
                        sp.wait_ge(m.y, 2 + T + 4 * i + u + 1)
                        sp.dma_start(ys[:, ds(4 * i + u, 1), :], yst[:, u:u + 1, :]).then_inc(m.y_out[u], 16)

            moe_stores(0)
            moe_stores(1)
            sp.wait_ge(moe[1].last, T)
            sp.dma_start(od, xres[:, :, :]).then_inc(stored, 16)
            sp.wait_ge(stored, 16)

        @block.gpsimd
        def _(pool):
            steps = [0]

            def link(ins):
                steps[0] += 1
                ins.then_inc(pool_step, 1)
                pool.wait_ge(pool_step, steps[0])

            pool.iota(part_i[:, 0:1], pattern=[[0, 1]], base=0, channel_multiplier=1)
            pool.iota(iota_i[:, :], pattern=[[1, P]], base=0, channel_multiplier=0)
            pool.iota(ids_i[:, :], pattern=[[P, T]], base=0, channel_multiplier=1)
            pool.memset(ident16[:, :], 0.0)
            pool.memset(ident32[:, :], 0.0)
            pool.memset(upper16[:, :], 1.0)
            pool.memset(reset[:, :, :], 1.0)
            pool.memset(onesC[:, :], 1.0 / (SEQ * PS))
            pool.memset(ones16[:, :], 1.0)
            pool.memset(cXS[:, :], XS)
            pool.memset(zero16[:, :], 0.0)
            pool.memset(cWS[:, :], WS)
            link(pool.memset(eps[:, :], 1e-5))
            for m in (ident16, ident32):
                pool.affine_select(out=m[:, :], in_=m[:, :], compare_op=ALU.not_equal, fill=1.0,
                                   base=0, pattern=[[-1, P]], channel_multiplier=1)
            pool.affine_select(out=upper16[:, :], in_=upper16[:, :], compare_op=ALU.is_gt, fill=0.0,
                               base=0, pattern=[[1, P]], channel_multiplier=-1)
            pool.tensor_copy(iota_f[:, :], iota_i[:, :])
            pool.tensor_copy(ids_f[:, :], ids_i[:, :])
            pool.memset(reset[:, :, 0:1], 0.0)
            pool.memset(bt[:, :], 0.0).then_inc(const_made, 1)

            def half(w, e, h):
                return w[:, ds(e, 1), h, :]

            def split_expert(e, u, loads):
                before = steps[0] + 4 * e
                pool.wait_ge(ewt_in[u], loads)
                for n, w in ((1, 0), (2, 1)):
                    pool.tensor_tensor(wstage[:, u, w, :], wstage[:, u, w, :], cWS[:, 0:1].to_broadcast([P, I]), ALU.mult)\
                        .then_inc(pool_step, 1)
                for n, w, dst in ((1, 0, w1s), (2, 1, w2s)):
                    pool.wait_ge(pool_step, before + n)
                    pool.tensor_copy(half(dst, e, 0), wstage[:, u, w:w + 1, :]).then_inc(pool_step, 1)
                pool.wait_ge(pool_step, before + 4)
                pool.tensor_tensor(half(w1s, e, 1), wstage[:, u, 0:1, :], half(w1s, e, 0), ALU.subtract)
                pool.tensor_tensor(half(w2s, e, 1), wstage[:, u, 1:2, :], half(w2s, e, 0), ALU.subtract)\
                    .then_inc(ewt_used, 1)

            with pool.Fori(0, E // 2) as i:
                for u in range(2):
                    split_expert(2 * i + u, u, 32 * (i + 1))
            split_expert(E, 0, 32 * (E // 2 + 1))
            steps[0] += 4 * NE
            pool.memset(wqk[:, :, :, :], 0.0)
            pool.memset(vx[:, :, :, :, :], 0.0)
            pool.wait_ge(wT_lo, 1)
            link(pool.memset(bt[0:1, BKS:BKS + 4 * P].rearrange("p (h s) -> p h s", s=32)[:, :, 24:26], KX / XS))
            pool.wait_ge(bias_rows, 2 * 16 * len(BIASES))
            pool.memset(vx[:, :, :, :, HD:HD + 1], 1.0)
            for j, at in ((0, BQS), (1, BKS)):
                for rep in range(3):
                    f = slice(rep * HD, (rep + 1) * HD)
                    for h in range(2):
                        pool.tensor_copy(wqk[:, h, j, :].rearrange("p (h s) -> p h s", s=32)[:, :, f],
                                         wbT[:, h, j * D:(j + 1) * D].rearrange("p (h d) -> p h d", d=HD))
                    last = pool.tensor_copy(bt[0:2, at:at + 4 * P].rearrange("p (h s) -> p h s", s=32)[:, :, f],
                                            bt[0:2, BQKV + j * D:BQKV + (j + 1) * D].rearrange("p (h d) -> p h d", d=HD))
            last.then_inc(slots_made, 1)

            def moe_rows(r):
                m, l, first = moe[r], Ln, (2 * r + 1) * NBATCH
                with pool.Fori(0, NBATCH) as b:
                    pool.wait_ge(l.norm, first + b + 1)
                    pool.tensor_tensor(two(xres, b), two(xres, b), two(xn, b), ALU.add).then_inc(l.added, 1)
                for u in range(4):
                    pool.sem_inc(m.y_out[u], 16)
                pool.wait_ge(m.tok, 1)

                def fetches(groups, numbers, copied, free, fetch):
                    def step(f, v):
                        free(f)
                        pool.wait_ge(copied, f + 1)
                        if not (isinstance(f, int) and f + 1 == groups):
                            numbers(f + 1, (v + 1) % 4)
                        fetch(v)

                    numbers(0, 0)
                    pool.wait_ge(copied, 1)
                    numbers(1, 1)
                    fetch(0)
                    pool.wait_ge(copied, 2)
                    numbers(2, 2)
                    fetch(1)
                    passes = (groups - 3) // 4
                    with pool.Fori(0, passes) as i:
                        for v in range(4):
                            step(4 * i + v + 2, (v + 2) % 4)
                    for f in range(4 * passes + 2, groups):
                        step(f, f % 4)

                def row_numbers(f, v):
                    pool.tensor_copy(gidx[:, v, :], tok_i[:, ds(4 * f, 4)]).then_inc(m.gidx, 1)

                def rows_free(f):
                    pool.wait_ge(m.turn, 4 * f - 4)

                def fetch_rows(v):
                    for u in range(4):
                        g = 4 * (v % 2) + u
                        pool.indirect_dma_start(grow[:, g, :], None, rows_dram[r],
                                                bass.IndirectOffsetOnAxis(ap=gidx[:, v, u:u + 1], axis=0))\
                            .then_inc(m.gath[g], 16)

                pool.wait_ge(m.rows_out, 16 * NBATCH)
                fetches(NBLK // 4, row_numbers, m.gidx, rows_free, fetch_rows)

                def y_numbers(f, v):
                    pool.tensor_copy(yidx[:, v, :].rearrange("p (c k) -> p k c", k=TOPK),
                                     slot_i[:, :, ds(2 * f, 2)]).then_inc(m.yidx, 1)

                def y_free(f):
                    pool.wait_ge(m.last, 2 * f - 2)

                def fetch_y(v):
                    h = v % 2
                    for u in range(4):
                        pool.indirect_dma_start(gy[:, h, u, :], None, y_dram[r],
                                                bass.IndirectOffsetOnAxis(ap=yidx[:, v, u:u + 1], axis=0))\
                            .then_inc(m.ygath[2 * h + u % 2], 16)

                for u in range(4):
                    pool.wait_ge(m.y_out[u], 16 * (NBLK // 4 + 1))
                fetches(T // 2, y_numbers, m.yidx, y_free, fetch_y)

            moe_rows(0)
            pool.wait_ge(moe[0].last, T)
            pool.memset(negmax, 0.0).then_inc(Att.cleared, 1)
            moe_rows(1)

        @block.tensor
        def _(pe):
            def mm(o, a, b, start, stop):
                return pe.matmul(o, a, b, start=start, stop=stop)

            pe.wait_ge(const_made, 1)
            pe.wait_ge(wnat_in, 6 * 16)
            for i in range(7):
                turned = pe.transpose(ps[:, i // 4, P * (i % 4):P * (i % 4 + 1)], wnat[:, i, :], ident32[:, :])
            turned.then_inc(wT_turned, 1)

            def norm_turns(r, gate):
                l, first = Ln, r * NBATCH

                def turn(b, u):
                    pe.wait_ge(l.lo, first + b + 1)
                    for c in range(CB):
                        for h in range(2):
                            o = c * 2 * P + h * P
                            last = pe.transpose(TB[u][:, o:o + P],
                                                hl[:, ds(2 * b + c, 1), h * D:(h + 1) * D], ident16[:, :])
                    last.then_inc(l.turned, 1)

                def logits(b):
                    if not gate:
                        return
                    for c in range(CB):
                        t = 2 * b + c
                        o = GATE[:, ds(E * t, E)]
                        hi, lo = xT[:, ds(t, 1), 0:P], xT[:, ds(t, 1), P:2 * P]
                        mm(o, hi, gws[:, 0, :], True, False)
                        mm(o, hi, gws[:, 1, :], False, False)
                        mm(o, lo, gws[:, 0, :], False, False)
                        last = mm(o, cXS[:, 0:P], bt[:, BG:BG + E], False, True)
                    return last

                turn(0, 0)
                turn(1, 1)
                with pe.Fori(0, NBATCH // 2 - 1) as i:
                    for u in range(2):
                        b = 2 * i + u
                        pe.wait_ge(l.xT, first + b + 1)
                        turn(b + 2, u)
                        logits(b)
                if gate:
                    pe.wait_ge(l.xT, first + NBATCH)
                    logits(NBATCH - 2)
                    logits(NBATCH - 1).then_inc(moe[r // 2].logits, 1)

            def mix():
                pe.wait_ge(wT_lo, 1)
                pe.wait_ge(Ln.xT, NBATCH)

                def project(b, u):
                    for c in range(CB):
                        t = 2 * b + c
                        o = ps[:, 2 * u + c, 0:3 * D]
                        hi, lo = xT[:, ds(t, 1), 0:P], xT[:, ds(t, 1), P:2 * P]
                        mm(o, hi, waT[:, 0, :], True, False)
                        mm(o, hi, waT[:, 1, :], False, False)
                        last = mm(o, lo, waT[:, 0, :], False, True)
                    last.then_inc(Mix.qkv, 1)

                def mean(b, u):
                    pe.wait_ge(Mix.kv, b + 1)
                    mm(ps[:, 4 + u, 0:D], onesC[:, :], kv[:, u, 0, :], True, False)
                    mm(ps[:, 4 + u, 0:D], onesC[:, :], kv[:, u, 1, :], False, True).then_inc(Mix.mean, 1)

                project(0, 0)
                project(1, 1)
                with pe.Fori(0, NBATCH // 2 - 1) as i:
                    for u in range(2):
                        b = 2 * i + u
                        mean(b, u)
                        pe.wait_ge(Mix.done, b + 1)
                        project(b + 2, u)
                mean(NBATCH - 2, 0)
                mean(NBATCH - 1, 1)

            def moe_blocks(r):
                m = moe[r]
                pe.wait_ge(m.mask, 1)
                flat = mask16[:, :, :].rearrange("p e t -> p (e t)")
                mm(RANK, upper16[:, :], flat, True, True)
                mm(TOT, ones16[:, :], flat, True, True).then_inc(m.rank, 1)

                def up(n, u, e, hi, lo):
                    for c in range(CH):
                        o = HB[u][:, c * P:(c + 1) * P]
                        f = slice(c * P, (c + 1) * P)
                        w = w1s[:, ds(e, 1), 0, f]
                        mm(o, w, hi, True, False)
                        mm(o, w, lo, False, False)
                        mm(o, w1s[:, ds(e, 1), 1, f], hi, False, False)
                        last = mm(o, bt[:, ds(B1 + e * I + c * P, P)], cXS[:, 0:P], False, True)
                    last.then_inc(m.up, 1)

                def down(n, u, e):
                    pe.wait_ge(m.split, n + 1)
                    pe.wait_ge(m.y, n + 1)
                    o = YB[u % 2]
                    for c in range(CH):
                        f = slice(c * P, (c + 1) * P)
                        w = w2s[:, ds(e, 1), 0, f]
                        mm(o, hhi[:, u, f], w, c == 0, False)
                        mm(o, hhi[:, u, f], w2s[:, ds(e, 1), 1, f], False, False)
                        mm(o, hlo[:, u, f], w, False, False)
                    mm(o, cXS[:, 0:P], bt[:, ds(B2 + e * D, D)], False, True).then_inc(m.down, 1)

                def up_shared(t, u):
                    up(t, u, E, xT[:, ds(t, 1), 0:P], xT[:, ds(t, 1), P:2 * P])

                def number(t, u, stop):
                    pe.wait_ge(m.onehot, t + 1)
                    for k in range(TOPK):
                        last = mm(IDX, onerow[:, u % 2, k, :], oneblk[:, u % 2, k, :], False, stop and k == TOPK - 1)
                    last.then_inc(m.index, 1)

                pe.wait_ge(ewt_used, NE)
                mm(IDX, zero16[:, :], zero16[:, 0:NBLK], True, False)
                up_shared(0, 0)
                up_shared(1, 1)
                with pe.Fori(0, T // 4 - 1) as i:
                    for u in range(4):
                        up_shared(4 * i + u + 2, (u + 2) % 4)
                        down(4 * i + u, u, E)
                        number(4 * i + u, u, False)
                for u in range(4):
                    t = T - 4 + u
                    if u < 2:
                        up_shared(t + 2, u + 2)
                    down(t, u, E)
                    number(t, u, u == 3)

                def expert(n):
                    return pe.value_load(bexp_i[0:1, ds(n, 1)], min_val=0, max_val=E - 1)

                def turn(n, u, i):
                    pe.wait_ge(m.gath[u], 16 * (i + 1))
                    for h in range(2):
                        last = pe.transpose(TB[u % 2][:, h * P:(h + 1) * P],
                                            grow[:, u, h * D:(h + 1) * D], ident16[:, :])
                    last.then_inc(m.turn, 1)

                def up_routed(n, u):
                    pe.wait_ge(m.xg, n + 1)
                    up(T + n, u, expert(n), xg[:, u, 0:P], xg[:, u, P:2 * P])

                def down_routed(n, u):
                    down(T + n, u, expert(n))

                turn(0, 0, 0)
                turn(1, 1, 0)
                up_routed(0, 0)
                turn(2, 2, 0)
                up_routed(1, 1)
                with pe.Fori(0, NBLK // 8 - 1) as i:
                    for u in range(8):
                        n = 8 * i + u
                        turn(n + 3, (u + 3) % 8, i + (u + 3) // 8)
                        up_routed(n + 2, (u + 2) % 4)
                        down_routed(n, u % 4)
                for u in range(8):
                    n = NBLK - 8 + u
                    if u < 5:
                        turn(n + 3, u + 3, NBLK // 8 - 1)
                    if u < 6:
                        up_routed(n + 2, (u + 2) % 4)
                    down_routed(n, u % 4)

            def heads(hh):
                return slice(32 * hh, 32 * hh + 3 * HD), slice(32 * hh, 32 * hh + 32)

            def attn_fill(fill, semaphore, count):
                bank, _ = fill.next()
                before = fill.bank_free(semaphore, count)
                if before is not None:
                    pe.wait_ge(*before)
                return ps[:, 6 + bank, :]

            def project(fill, b, g):
                o = attn_fill(fill, Att.stack, 4 * b + g + 1)
                hi, lo = two(xT, b)[:, :, 0:P], two(xT, b)[:, :, P:2 * P]
                for n in range(2):
                    f = slice((2 * (g % 2) + n) * P, (2 * (g % 2) + n + 1) * P)
                    at = (BQS, BKS)[g // 2]
                    on = o[:, n * SEQ:(n + 1) * SEQ]
                    w = wqk[:, :, g // 2, f]
                    mm(on, w[:, 0, :], hi, True, False)
                    mm(on, w[:, 0, :], lo, False, False)
                    mm(on, w[:, 1, :], hi, False, False)
                    last = mm(on, bt[:, at + f.start:at + f.stop], cXS[:, :], False, True)
                last.then_inc(Att.full, 1)

            def values(fill, b):
                o = attn_fill(fill, Att.v, b + 1)
                for c in range(CB):
                    t = 2 * b + c
                    hi, lo = xT[:, ds(t, 1), 0:P], xT[:, ds(t, 1), P:2 * P]
                    on = o[:, c * D:(c + 1) * D]
                    mm(on, hi, wbT[:, 0, 2 * D:3 * D], True, False)
                    mm(on, hi, wbT[:, 1, 2 * D:3 * D], False, False)
                    mm(on, lo, wbT[:, 0, 2 * D:3 * D], False, False)
                    last = mm(on, cXS[:, 0:P], bt[:, BQKV + 2 * D:BQKV + 3 * D], False, True)
                last.then_inc(Att.full, 1)

            def score(b, u, s):
                c, jp, hh = s // 8, s // 4 % 2, s % 4
                if s == 0:
                    pe.wait_ge(Att.stack, 4 * b + 4)
                if not (isinstance(b, int) and 16 * b + s < 2):
                    pe.wait_ge(Att.mx, 16 * b + s - 1)
                for n in range(2):
                    j = 2 * jp + n
                    rows = heads(hh)[0]
                    last = mm(ps[:, 2 + s % 2, n * SEQ:(n + 1) * SEQ], qst[rows, u, j, c * P:(c + 1) * P],
                              kst[rows, u, j, :], True, True)
                last.then_inc(Att.score, 1)

            def maxima(fill, b, u, jp):
                o = attn_fill(fill, Att.q2, 2 * b + jp + 1)
                pe.wait_ge(Att.neg, b + 1)
                for n in range(2):
                    j = 2 * jp + n
                    on = o[:, n * SEQ:(n + 1) * SEQ]
                    mm(on, ident16[:, :], qst[:, u, j, :], True, False)
                    for c in range(CB):
                        last = mm(on[:, c * P:(c + 1) * P], negmax[:, c, j * P:(j + 1) * P], ident16[:, :],
                                  False, c == CB - 1)
                last.then_inc(Att.full, 1)

            def scoreT(b, u, s):
                jp, kc, hh = s // 8, s // 4 % 2, s % 4
                if s == 0:
                    pe.wait_ge(Att.q2, 2 * b + 2)
                if not (isinstance(b, int) and 16 * b + s < 2):
                    pe.wait_ge(Att.prob, 16 * b + s - 1)
                for n in range(2):
                    j = 2 * jp + n
                    rows = heads(hh)[1]
                    last = mm(ps[:, s % 2, n * SEQ:(n + 1) * SEQ], kst[rows, u, j, kc * P:(kc + 1) * P],
                              qst2[rows, j, :], True, True)
                last.then_inc(Att.scoreT, 1)

            def weigh(b, u, g):
                jp, kc = g // 2, g % 2
                pe.wait_ge(Att.prob, 16 * b + 4 * g + 4)
                if g == 0:
                    pe.wait_ge(Att.v, b + 1)
                    if not (isinstance(b, int) and b == 0):
                        pe.wait_ge(Att.oT, 2 * b)
                for n in range(2):
                    for hh in range(4):
                        last = pe.matmul(ps[32 * hh:32 * hh + 32, 4 + jp, n * SEQ:(n + 1) * SEQ],
                                         vx[:, u, kc, 4 * (2 * jp + n) + hh, :],
                                         prb[:, (4 * g + hh) % 8, n * SEQ:(n + 1) * SEQ],
                                         start=kc == 0 and n == 0, stop=kc == 1 and n == 1,
                                         skip_group_check=True)
                last.then_inc(Att.pv, 1)

            def turn_back(fill, b, c):
                o = attn_fill(fill, Att.attn, 2 * b + c + 1)
                pe.wait_ge(Att.oT, 2 * b + 2)
                for j in range(HG):
                    last = pe.transpose(o[:, j * P:(j + 1) * P],
                                        oT[:, j // 2, (j % 2) * SEQ + c * P:(j % 2) * SEQ + (c + 1) * P], ident32[:, :])
                last.then_inc(Att.full, 1)

            def turn_attn(fill, b):
                o = attn_fill(fill, Att.alo, b + 1)
                pe.wait_ge(Att.attn, 2 * b + 2)
                for c in range(CB):
                    last = pe.transpose(o[:, c * P:(c + 1) * P], attn[:, c, :], ident32[:, :])
                last.then_inc(Att.full, 1)

            def out_project(fill, b):
                o = attn_fill(fill, Att.done, b + 1)
                pe.wait_ge(Att.alo, b + 1)
                for c in range(CB):
                    f = slice(c * P, (c + 1) * P)
                    on = o[:, c * D:(c + 1) * D]
                    mm(on, ahi[:, f], wbT[:, 0, 3 * D:4 * D], True, False)
                    mm(on, ahi[:, f], wbT[:, 1, 3 * D:4 * D], False, False)
                    mm(on, alo[:, f], wbT[:, 0, 3 * D:4 * D], False, False)
                    last = mm(on, cXS[:, 0:P], bt[:, BO:BO + D], False, True)
                last.then_inc(Att.full, 1)

            def attn_body(b, u, fill, output, ahead, project2):
                for s in range(16):
                    if ahead:
                        score(b + 1, 1 - u, s)
                    scoreT(b, u, s)
                    if s in (6, 10, 14):
                        weigh(b, u, (s - 6) // 4)
                    if output and s == 3:
                        turn_back(fill, b - 1, 0)
                        turn_back(fill, b - 1, 1)
                    if output and s == 8:
                        turn_attn(fill, b - 1)
                    if output and s == 13:
                        out_project(fill, b - 1)
                weigh(b, u, 3)
                if project2:
                    project(fill, b + 2, 0)
                    project(fill, b + 2, 1)
                if ahead:
                    maxima(fill, b + 1, 1 - u, 0)
                    maxima(fill, b + 1, 1 - u, 1)
                if project2:
                    project(fill, b + 2, 2)
                    project(fill, b + 2, 3)
                    values(fill, b + 2)

            def attn_start(fill):
                for g in range(4):
                    project(fill, 0, g)
                values(fill, 0)
                for s in range(16):
                    score(0, 0, s)
                maxima(fill, 0, 0, 0)
                maxima(fill, 0, 0, 1)
                for g in range(4):
                    project(fill, 1, g)
                values(fill, 1)

            def attn_end(fill, b):
                turn_back(fill, b, 0)
                turn_back(fill, b, 1)
                turn_attn(fill, b)
                out_project(fill, b)

            norm_turns(0, False)
            mix()
            pe.wait_ge(bias_rows, 2 * 16 * len(BIASES))
            norm_turns(1, True)
            moe_blocks(0)
            norm_turns(2, False)
            pe.wait_ge(slots_made, 1)
            pe.wait_ge(Ln.xT, 3 * NBATCH)
            attention(pe, attn_start, attn_body, attn_end)
            norm_turns(3, True)
            moe_blocks(1)

        @block.scalar
        def _(act):
            act.wait_ge(wT_turned, 1)
            act.activation(waT[:, 0, :], ps[:, 0, 0:3 * D], ACT.Copy, scale=WS)
            act.activation(wbT[:, 0, 0:D], ps[:, 0, 3 * D:4 * D], ACT.Copy, scale=WS)
            act.activation(wbT[:, 0, D:4 * D], ps[:, 1, 0:3 * D], ACT.Copy, scale=WS)
            act.activation(gws[:, 0, :], gstage, ACT.Copy, scale=WS).then_inc(wT_hi, 1)

            def std(r):
                l, first = Ln, r * NBATCH
                act.wait_ge(l.var, r + 1)
                act.activation(rstd[:, :], var[:, :], ACT.Sqrt, bias=eps[:, 0:1], scale=1.0 / D).then_inc(l.std, 1)

            def norm(r):
                l, first = Ln, r * NBATCH

                def hi(b):
                    act.wait_ge(l.norm, first + b + 1)
                    act.activation(two(hl, b)[:, :, 0:D], two(xn, b), ACT.Copy, scale=XS).then_inc(l.hi, 1)

                def copy_out(b, u):
                    act.wait_ge(l.turned, first + b + 1)
                    act.activation(two(xT, b), TB[u][:, 0:4 * P].rearrange("p (c f) -> p c f", c=CB),
                                   ACT.Copy).then_inc(l.xT, 1)

                hi(0)
                hi(1)
                with act.Fori(0, NBATCH // 2 - 1) as i:
                    for u in range(2):
                        hi(2 * i + u + 2)
                        copy_out(2 * i + u, u)
                copy_out(NBATCH - 2, 0)
                copy_out(NBATCH - 1, 1)

            def mix():
                def front(b, u):
                    act.wait_ge(Mix.qkv, b + 1)
                    for c in range(CB):
                        for j in range(2):
                            last = act.activation(junk[:, 2 * c + j, :], ps[:, 2 * u + c, j * D:(j + 1) * D], ACT.Square,
                                                  accum_out=ssq[:, u, c, j:j + 1])
                    last.then_inc(Mix.ssq, 1)
                    act.wait_ge(Mix.ssq, b + 1)
                    act.activation(rnorm[:, u, :, :], ssq[:, u, :, :], ACT.Sqrt).then_inc(Mix.std, 1)
                    act.wait_ge(Mix.rnorm, b + 1)
                    for c in range(CB):
                        last = act.activation(kn[:, u, c, :], ps[:, 2 * u + c, D:2 * D], ACT.Copy,
                                              scale=rnorm[:, u, c, 1:2])
                    last.then_inc(Mix.kn, 1)

                def back(b, u):
                    act.wait_ge(Mix.mean, b + 1)
                    act.activation(gf[:, u, :], ps[:, 4 + u, 0:D], ACT.Copy).then_inc(Mix.gf, 1)

                front(0, 0)
                with act.Fori(0, NBATCH // 2 - 1) as i:
                    for u in range(2):
                        front(2 * i + u + 1, 1 - u)
                        back(2 * i + u, u)
                front(NBATCH - 1, 1)
                back(NBATCH - 2, 0)
                back(NBATCH - 1, 1)

            def moe_blocks(r):
                m = moe[r]
                act.wait_ge(m.shifted, 1)
                act.activation(prob[:, :, :], prob[:, :, :], ACT.Exp, scale=1.0 / PS).then_inc(m.exp, 1)

                def gelu(n, u):
                    act.wait_ge(m.up, n + 1)
                    act.activation(h32[:, u, :], HB[u], ACT.Gelu_apprx_tanh, scale=1.0 / PS).then_inc(m.gelu, 1)

                def copy_out(n, u):
                    act.wait_ge(m.turn, n + 1)
                    act.activation(xg[:, u, :], TB[u % 2][:, 0:2 * P], ACT.Copy).then_inc(m.xg, 1)

                with act.Fori(0, T // 4) as i:
                    for u in range(4):
                        gelu(4 * i + u, u)
                copy_out(0, 0)
                copy_out(1, 1)
                gelu(T, 0)
                copy_out(2, 2)
                gelu(T + 1, 1)
                with act.Fori(0, NBLK // 4 - 1) as i:
                    for u in range(4):
                        n = 4 * i + u
                        copy_out(n + 3, (u + 3) % 4)
                        gelu(T + n + 2, (u + 2) % 4)
                for u in range(2):
                    if u < 1:
                        copy_out(NBLK - 1, 3)
                    gelu(T + NBLK - 2 + u, u + 2)

            def attn_full(fill):
                bank, count = fill.next()
                act.wait_ge(Att.full, count)
                return bank, ps[:, 6 + bank, :]

            def stack_hi(fill):
                bank, o = attn_full(fill)
                act.activation(qkhi[:, bank, :], o, ACT.Copy).then_inc(Att.hi, 1)

            def values(fill, u):
                bank, o = attn_full(fill)
                for c in range(CB):
                    last = act.activation(vx[:, u, c, :, 0:HD],
                                          o[:, c * D:(c + 1) * D].rearrange("p (h d) -> p h d", d=HD),
                                          ACT.Copy, scale=1.0 / PS)
                last.then_inc(Att.v, 1)

            def maxima(fill, jp):
                bank, o = attn_full(fill)
                act.activation(qst2[:, 2 * jp:2 * jp + 2, :], o.rearrange("p (j n) -> p j n", j=2), ACT.Copy)\
                    .then_inc(Att.q2, 1)

            def exp(b, s):
                act.wait_ge(Att.scoreT, 16 * b + s + 1)
                if s >= 8 and s % 4 == 0:
                    act.wait_ge(Att.pv, 4 * b + (s - 8) // 4 + 1)
                act.activation(prb[:, s % 8, :], ps[:, s % 2, :], ACT.Exp, scale=HD ** -0.5 / (PS * PS))\
                    .then_inc(Att.prob, 1)

            def sums_out(b):
                for jp in range(2):
                    act.wait_ge(Att.pv, 4 * b + 2 * jp + 2)
                    act.activation(oT[:, jp, :], ps[:, 4 + jp, :], ACT.Copy).then_inc(Att.oT, 1)

            def attn_hi(fill):
                bank, o = attn_full(fill)
                act.activation(ahi, o[:, 0:SEQ], ACT.Copy, scale=XS).then_inc(Att.ahi, 1)

            def attn_body(b, u, fill, output, ahead, project2):
                if output:
                    sums_out(b - 1)
                    fill.k += 2
                for s in range(16):
                    exp(b, s)
                    if output and s == 9:
                        attn_hi(fill)
                        fill.k += 1
                if project2:
                    stack_hi(fill)
                    stack_hi(fill)
                if ahead:
                    maxima(fill, 0)
                    maxima(fill, 1)
                if project2:
                    stack_hi(fill)
                    stack_hi(fill)
                    values(fill, u)

            def attn_start(fill):
                for g in range(4):
                    stack_hi(fill)
                values(fill, 0)
                maxima(fill, 0)
                maxima(fill, 1)
                for g in range(4):
                    stack_hi(fill)
                values(fill, 1)

            def attn_end(fill, b):
                sums_out(b)
                fill.k += 2
                attn_hi(fill)

            std(0)
            norm(0)
            mix()
            std(1)
            norm(1)
            moe_blocks(0)
            std(2)
            norm(2)
            attention(act, attn_start, attn_body, attn_end)
            std(3)
            norm(3)
            moe_blocks(1)

        @block.vector
        def _(dve):
            dve.wait_ge(bias_in, 16 * len(BIASES))
            dve.wait_ge(const_made, 1)
            dve.tensor_scalar(bhi[:, 0:NBIAS - 1], bnat[:, 0:NBIAS - 1], WS, None, ALU.mult)
            dve.tensor_scalar(bhi[0:E, NBIAS - 1:NBIAS], bnat[0:E, NBIAS - 1:NBIAS], WS, None, ALU.mult)\
                .then_inc(bias_hi, 1)
            dve.wait_ge(bias_hi, 1)
            dve.scalar_tensor_tensor(blo[:, 0:NBIAS - 1], bnat[:, 0:NBIAS - 1], WS, bhi[:, 0:NBIAS - 1],
                                     ALU.mult, ALU.subtract)
            dve.scalar_tensor_tensor(blo[0:E, NBIAS - 1:NBIAS], bnat[0:E, NBIAS - 1:NBIAS], WS,
                                     bhi[0:E, NBIAS - 1:NBIAS], ALU.mult, ALU.subtract).then_inc(bias_lo, 1)
            dve.tensor_scalar(part_i[:, 1:2], part_i[:, 0:1], 31, 3, ALU.bitwise_and, ALU.arith_shift_right)\
                .then_inc(rows_found, 1)
            dve.wait_ge(rows_found, 1)
            dve.tensor_scalar(nsel[:, 0:1], part_i[:, 1:2], 2.0, -1.0, ALU.is_equal, ALU.mult)
            dve.tensor_scalar(nsel[:, 1:2], part_i[:, 1:2], 1.0, -1.0, ALU.is_equal, ALU.mult)
            dve.wait_ge(wT_hi, 1)
            dve.scalar_tensor_tensor(waT[:, 1, :], ps[:, 0, 0:3 * D], WS, waT[:, 0, :], ALU.mult, ALU.subtract)
            dve.scalar_tensor_tensor(wbT[:, 1, 0:D], ps[:, 0, 3 * D:4 * D], WS, wbT[:, 0, 0:D],
                                     ALU.mult, ALU.subtract)
            dve.scalar_tensor_tensor(wbT[:, 1, D:4 * D], ps[:, 1, 0:3 * D], WS, wbT[:, 0, D:4 * D],
                                     ALU.mult, ALU.subtract)
            dve.scalar_tensor_tensor(gws[:, 1, :], gstage, WS, gws[:, 0, :], ALU.mult, ALU.subtract)\
                .then_inc(wT_lo, 1)
            dve.wait_ge(x_in, 4 * 16)

            def norm(r):
                l, first = Ln, r * NBATCH
                with dve.Fori(0, T // 4) as i:
                    for u in range(4):
                        last = dve.bn_stats(stats[:, ds(4 * i + u, 1), :], xres[:, ds(4 * i + u, 1), :])
                    last.then_inc(l.stats, 1)
                dve.wait_ge(l.stats, (r + 1) * (T // 4))
                dve.tensor_tensor(mean[:, :], stats[:, :, 1], stats[:, :, 4], ALU.add)
                dve.tensor_tensor(var[:, :], stats[:, :, 2], stats[:, :, 5], ALU.add)
                dve.tensor_tensor(gap[:, :], stats[:, :, 1], stats[:, :, 4], ALU.subtract).then_inc(l.merge, 1)
                dve.wait_ge(l.merge, 2 * r + 1)
                dve.tensor_scalar(mean[:, :], mean[:, :], 0.5, None, ALU.mult)
                dve.tensor_tensor(gap[:, :], gap[:, :], gap[:, :], ALU.mult).then_inc(l.merge, 1)
                dve.wait_ge(l.merge, 2 * r + 2)
                dve.scalar_tensor_tensor(var[:, :], gap[:, :], D / 4.0, var[:, :], ALU.mult, ALU.add).then_inc(l.var, 1)
                dve.wait_ge(l.std, r + 1)
                dve.reciprocal(rstd[:, :], rstd[:, :]).then_inc(l.rstd, 1)
                dve.wait_ge(l.rstd, r + 1)

                def whole(b):
                    for c in range(CB):
                        t = 2 * b + c
                        last = dve.tensor_scalar(xn[:, ds(t, 1), :], xres[:, ds(t, 1), :],
                                                 mean[:, ds(t, 1)], rstd[:, ds(t, 1)],
                                                 ALU.subtract, ALU.mult)
                    last.then_inc(l.norm, 1)

                def lo(b):
                    dve.wait_ge(l.hi, first + b + 1)
                    h = two(hl, b)
                    dve.scalar_tensor_tensor(h[:, :, D:2 * D], two(xn, b), XS, h[:, :, 0:D],
                                             ALU.mult, ALU.subtract).then_inc(l.lo, 1)

                whole(0)
                with dve.Fori(0, NBATCH - 1) as b:
                    whole(b + 1)
                    lo(b)
                lo(NBATCH - 1)

            def mix():
                def front(b, u):
                    dve.wait_ge(Mix.std, b + 1)
                    dve.tensor_scalar(rnorm[:, u, :, :], rnorm[:, u, :, :], PS * 1e-12, None, ALU.max)\
                        .then_inc(Mix.clamped, 1)
                    dve.wait_ge(Mix.clamped, b + 1)
                    dve.reciprocal(rnorm[:, u, :, :], rnorm[:, u, :, :]).then_inc(Mix.rnorm, 1)
                    dve.wait_ge(Mix.kn, b + 1)
                    for c in range(CB):
                        last = dve.tensor_tensor(kv[:, u, c, :], kn[:, u, c, :],
                                                 ps[:, 2 * u + c, 2 * D:3 * D], ALU.mult)
                    last.then_inc(Mix.kv, 1)

                def back(b, u):
                    dve.wait_ge(Mix.gf, b + 1)
                    for c in range(CB):
                        last = dve.scalar_tensor_tensor(qg[:, u, c, :], ps[:, 2 * u + c, 0:D],
                                                        rnorm[:, u, c, 0:1], gf[:, u, :],
                                                        ALU.mult, ALU.mult)
                    last.then_inc(Mix.qg, 1)
                    dve.wait_ge(Mix.qg, b + 1)
                    dve.tensor_tensor(two(xres, b), two(xres, b), qg[:, u, :, :], ALU.add).then_inc(Mix.done, 1)

                front(0, 0)
                with dve.Fori(0, NBATCH // 2 - 1) as i:
                    for u in range(2):
                        front(2 * i + u + 1, 1 - u)
                        back(2 * i + u, u)
                front(NBATCH - 1, 1)
                back(NBATCH - 2, 0)
                back(NBATCH - 1, 1)
                dve.wait_ge(Mix.done, NBATCH)

            def over(ap, axis, n):
                shape = list(ap.shape)
                shape.insert(axis, n)
                return ap.unsqueeze(axis).to_broadcast(shape)

            def moe_blocks(r):
                m = moe[r]
                steps = [0]

                def link(ins):
                    steps[0] += 1
                    ins.then_inc(m.step, 1)
                    dve.wait_ge(m.step, steps[0])

                dve.sem_inc(m.y, 2)
                logit = GATE.rearrange("p (t e) -> p t e", e=E)
                iota_e = over(iota_f[:, 0:E], 1, T)
                dve.wait_ge(m.logits, 1)
                link(dve.tensor_reduce(rs[0][:, :], logit, AX_X, ALU.max))
                dve.tensor_tensor(prob[:, :, :], logit, over(rs[0][:, :], 2, E), ALU.subtract).then_inc(m.shifted, 1)
                dve.wait_ge(m.exp, 1)
                link(dve.tensor_reduce(rs[0][:, :], prob[:, :, :], AX_X, ALU.add))
                link(dve.reciprocal(rs[1][:, :], rs[0][:, :]))
                link(dve.tensor_tensor(prob[:, :, :], prob[:, :, :], over(rs[1][:, :], 2, E), ALU.mult))
                left = prob
                for k in range(TOPK):
                    link(dve.tensor_reduce(topp[:, k, :], left[:, :, :], AX_X, ALU.max))
                    link(dve.tensor_tensor(rt[0][:, :, :], left[:, :, :], over(topp[:, k, :], 2, E), ALU.is_equal))
                    link(dve.scalar_tensor_tensor(rt[1][:, :, :], rt[0][:, :, :], -float(E), iota_e, ALU.mult, ALU.add))
                    link(dve.tensor_reduce(rs[0][:, :], rt[1][:, :, :], AX_X, ALU.min))
                    link(dve.tensor_tensor(mask[k][:, :, :], rt[1][:, :, :], over(rs[0][:, :], 2, E), ALU.is_equal))
                    if k == 0:
                        link(dve.scalar_tensor_tensor(rt[2][:, :, :], mask[0][:, :, :], -2.0, prob[:, :, :],
                                                      ALU.mult, ALU.add))
                        left = rt[2]
                dve.tensor_tensor(mask16[:, :, :].rearrange("p e t -> p t e"), mask[0][:, :, :], mask[1][:, :, :],
                                  ALU.add).then_inc(m.mask, 1)
                link(dve.tensor_tensor(rs[0][:, :], topp[:, 0, :], topp[:, 1, :], ALU.add))
                link(dve.tensor_scalar(rs[1][:, :], rs[0][:, :], 1e-9, None, ALU.add))
                link(dve.reciprocal(rs[2][:, :], rs[1][:, :]))
                link(dve.tensor_tensor(wtop[:, :, :], topp[:, :, :], over(rs[2][:, :], 1, TOPK), ALU.mult))
                link(dve.memset(e8[3][:, :], 1.0))
                dve.wait_ge(m.rank, 1)
                flat = "p e t -> p (e t)"
                link(dve.tensor_tensor_scan(cum[:, :, :].rearrange(flat), reset[:, :, :].rearrange(flat), TOT,
                                            0.0, ALU.mult, ALU.add))
                link(dve.tensor_scalar(e8[0][:, :], cum[:, :, T - 1], 1.0 / P, (P - 1.0) / P - HALF, ALU.mult, ALU.add))
                link(dve.tensor_scalar(e8[0][:, :], e8[0][:, :], RND, RND, ALU.add, ALU.subtract))
                link(dve.tensor_tensor_scan(e8[1][:, :], e8[3][:, :], e8[0][:, :], 0.0, ALU.mult, ALU.add))
                link(dve.tensor_tensor(e8[2][:, :], e8[1][:, :], e8[0][:, :], ALU.subtract))
                link(dve.tensor_tensor(slotb[:, :, :].rearrange(flat), cum[:, :, :].rearrange(flat), TOT, ALU.subtract))
                link(dve.scalar_tensor_tensor(slotb[:, :, :], over(e8[2][:, :], 2, T), float(P), slotb[:, :, :],
                                              ALU.mult, ALU.add))
                link(dve.tensor_tensor(slotb[:, :, :].rearrange(flat), slotb[:, :, :].rearrange(flat), RANK, ALU.add))
                for k in range(TOPK):
                    link(dve.tensor_tensor(rt[0][:, :, :], mask[k][:, :, :], slotb[:, :, :].rearrange("p e t -> p t e"),
                                           ALU.mult))
                    link(dve.tensor_reduce(slot[:, k, :], rt[0][:, :, :], AX_X, ALU.add))
                link(dve.tensor_scalar(blk[:, :, :], slot[:, :, :], 1.0 / P, -HALF, ALU.mult, ALU.add))
                link(dve.tensor_scalar(blk[:, :, :], blk[:, :, :], RND, RND, ALU.add, ALU.subtract))
                dve.scalar_tensor_tensor(row[:, :, :], blk[:, :, :], -float(P), slot[:, :, :], ALU.mult, ALU.add)
                dve.tensor_copy(slot_i[:, :, :], slot[:, :, :])
                link(dve.tensor_tensor(bexp[:, :, :], over(e8[1][:, :], 1, NBLK), over(iota_f[:, 0:NBLK], 2, E),
                                       ALU.is_le))
                link(dve.tensor_reduce(bexpf[:, :], bexp[:, :, :], AX_X, ALU.add))
                link(dve.tensor_scalar(bexp_i[:, :], bexpf[:, :], float(E - 1), None, ALU.min))

                def split(n, u):
                    dve.wait_ge(m.gelu, n + 1)
                    dve.tensor_scalar(hhi[:, u, :], h32[:, u, :], XS, None, ALU.mult).then_inc(m.hi, 1)
                    dve.wait_ge(m.hi, n + 1)
                    dve.scalar_tensor_tensor(hlo[:, u, :], h32[:, u, :], XS, hhi[:, u, :], ALU.mult, ALU.subtract)\
                        .then_inc(m.split, 1)

                def onehot(t, u):
                    for k in range(TOPK):
                        dve.tensor_scalar(onerow[:, u % 2, k, :], iota_f[:, :], row[:, k, ds(t, 1)], None, ALU.is_equal)
                        last = dve.tensor_scalar(oneblk[:, u % 2, k, :], iota_f[:, 0:NBLK], blk[:, k, ds(t, 1)],
                                                 ids_f[:, ds(t, 1)], ALU.is_equal, ALU.mult)
                    last.then_inc(m.onehot, 1)

                def result_shared(t, u):
                    dve.wait_ge(m.down, t + 1)
                    o = xres[:, ds(t, 1), :]
                    dve.scalar_tensor_tensor(o, YB[u % 2].unsqueeze(1), 1.0 / PS, o, ALU.mult, ALU.add).then_inc(m.y, 1)

                dve.wait_ge(Ln.added, (r + 1) * NBATCH)
                split(0, 0)
                split(1, 1)
                onehot(0, 0)
                onehot(1, 1)
                with dve.Fori(0, T // 4 - 1) as i:
                    for u in range(4):
                        n = 4 * i + u
                        split(n + 2, (u + 2) % 4)
                        result_shared(n, u)
                        dve.wait_ge(m.index, n + 1)
                        onehot(n + 2, u)
                for u in range(4):
                    n = T - 4 + u
                    if u < 2:
                        split(n + 2, u + 2)
                    result_shared(n, u)
                    if u < 2:
                        dve.wait_ge(m.index, n + 1)
                        onehot(n + 2, u)
                dve.wait_ge(m.index, T)
                dve.tensor_copy(tok_i[:, :], IDX).then_inc(m.tok, 1)

                def result_routed(n, u, i):
                    dve.wait_ge(m.down, T + n + 1)
                    dve.wait_ge(m.y_out[u], 16 * (i + 1))
                    dve.tensor_scalar(yst[:, u, :], YB[u % 2], 1.0 / PS, None, ALU.mult).then_inc(m.y, 1)

                split(T, 0)
                split(T + 1, 1)
                with dve.Fori(0, NBLK // 4 - 1) as i:
                    for u in range(4):
                        n = 4 * i + u
                        split(T + n + 2, (u + 2) % 4)
                        result_routed(n, u, i)
                for u in range(4):
                    n = NBLK - 4 + u
                    if u < 2:
                        split(T + n + 2, u + 2)
                    result_routed(n, u, NBLK // 4 - 1)

                def combine(i, h, k):
                    dve.wait_ge(m.ygath[2 * h + k], 32 * (i + 1))
                    for c in range(2):
                        t = 4 * i + 2 * h + c
                        o = xres[:, ds(t, 1), :]
                        dve.scalar_tensor_tensor(o, gy[:, h, 2 * c + k, :].unsqueeze(1), wtop[:, k, ds(t, 1)], o,
                                                 ALU.mult, ALU.add).then_inc((m.half, m.last)[k], 1)

                with dve.Fori(0, T // 4) as i:
                    for h in range(2):
                        combine(i, h, 0)
                        dve.wait_ge(m.half, 4 * i + 2 * h + 2)
                        combine(i, h, 1)

            def attn_full(fill):
                bank, count = fill.next()
                dve.wait_ge(Att.full, count)
                return bank, ps[:, 6 + bank, :]

            def stack(fill, b, u, g):
                bank, o = attn_full(fill)
                dve.wait_ge(Att.hi, 4 * b + g + 1)
                dst = (qst, kst)[g // 2]
                dve.scalar_tensor_tensor(dst[:, u, 2 * (g % 2):2 * (g % 2) + 2, :].rearrange("p j n -> p (j n)"),
                                         qkhi[:, bank, :], nsel[:, g // 2:g // 2 + 1], o, ALU.mult, ALU.add)\
                    .then_inc(Att.stack, 1)

            def maximum(b, s):
                c, jp, hh = s // 8, s // 4 % 2, s % 4
                dve.wait_ge(Att.score, 16 * b + s + 1)
                j = 8 * jp + hh
                dve.tensor_reduce(mx[:, c, j:j + 5:4], ps[:, 2 + s % 2, :].rearrange("p (n k) -> p n k", n=2),
                                  AX_X, ALU.max).then_inc(Att.mx, 1)

            def negate(b):
                slots = negmax.rearrange("p c (h s) -> p c h s", s=32)
                dve.wait_ge(Att.mx, 16 * b + 16)
                dve.tensor_scalar(slots[:, :, :, 24], mx[:, :, :], -1.0 / KX, None, ALU.mult).then_inc(Att.neghi, 1)
                dve.wait_ge(Att.neghi, b + 1)
                dve.scalar_tensor_tensor(slots[:, :, :, 25], mx[:, :, :], -1.0 / KX, slots[:, :, :, 24],
                                         ALU.mult, ALU.subtract).then_inc(Att.neg, 1)

            def normalise(fill, b, c):
                bank, o = attn_full(fill)
                heads = o.rearrange("p (h s) -> p h s", s=32)
                dve.reciprocal(rsum[:, c, :], heads[:, :, HD]).then_inc(Att.rsum, 1)
                dve.wait_ge(Att.rsum, 2 * b + c + 1)
                dve.tensor_tensor(attn[:, c, :].rearrange("p (h d) -> p h d", d=HD), heads[:, :, 0:HD],
                                  over(rsum[:, c, :], 2, HD), ALU.mult)\
                    .then_inc(Att.attn, 1)

            def attn_lo(fill, b):
                bank, o = attn_full(fill)
                dve.wait_ge(Att.ahi, b + 1)
                dve.scalar_tensor_tensor(alo, o[:, 0:SEQ], XS, ahi, ALU.mult, ALU.subtract)\
                    .then_inc(Att.alo, 1)

            def add_result(fill, b):
                bank, o = attn_full(fill)
                dve.scalar_tensor_tensor(two(xres, b), o[:, 0:CB * D].rearrange("p (c d) -> p c d", c=CB),
                                         1.0 / PS, two(xres, b), ALU.mult, ALU.add)\
                    .then_inc(Att.done, 1)

            def attn_body(b, u, fill, output, ahead, project2):
                for s in range(16):
                    if ahead:
                        maximum(b + 1, s)
                    if output and s in (4, 5):
                        normalise(fill, b - 1, s - 4)
                    if output and s == 10:
                        attn_lo(fill, b - 1)
                    if output and s == 15:
                        add_result(fill, b - 1)
                if ahead:
                    negate(b + 1)
                if project2:
                    stack(fill, b + 2, u, 0)
                    stack(fill, b + 2, u, 1)
                if ahead:
                    fill.k += 2
                if project2:
                    stack(fill, b + 2, u, 2)
                    stack(fill, b + 2, u, 3)
                    fill.k += 1

            def attn_start(fill):
                for g in range(4):
                    stack(fill, 0, 0, g)
                fill.k += 1
                for s in range(16):
                    maximum(0, s)
                dve.wait_ge(Att.cleared, 1)
                negate(0)
                fill.k += 2
                for g in range(4):
                    stack(fill, 1, 1, g)
                fill.k += 1

            def attn_end(fill, b):
                normalise(fill, b, 0)
                normalise(fill, b, 1)
                attn_lo(fill, b)
                add_result(fill, b)
                dve.wait_ge(Att.done, b + 1)

            norm(0)
            mix()
            norm(1)
            moe_blocks(0)
            dve.wait_ge(moe[0].last, T)
            norm(2)
            attention(dve, attn_start, attn_body, attn_end)
            norm(3)
            moe_blocks(1)


_INS = ['L0_attn_a_x', 'L0_attn_a_W_q', 'L0_attn_a_W_k', 'L0_attn_a_W_v', 'L0_attn_b_qkv_w', 'L0_attn_b_qkv_b',
        'L0_attn_b_out_w', 'L0_attn_b_out_b', 'L0_ffn_gate_w', 'L0_ffn_gate_b', 'L0_ffn_sh_w1', 'L0_ffn_sh_b1',
        'L0_ffn_sh_w2', 'L0_ffn_sh_b2', 'L0_ffn_ew1', 'L0_ffn_eb1', 'L0_ffn_ew2', 'L0_ffn_eb2']


def kernel(**inputs):
    import numpy as np
    import concourse.bacc as bacc
    from concourse.bass_utils import run_bass_kernel_spmd

    nc = bacc.Bacc("TRN2", target_bir_lowering=False, num_devices=1)
    arrays, args = {}, []
    for name in _INS:
        a = np.ascontiguousarray(inputs[name])
        arrays[f"in_{name}"] = a
        args.append(nc.dram_tensor(f"in_{name}", a.shape, mybir.dt.from_np(a.dtype), kind="ExternalInput").ap())
    shape = inputs['L0_attn_a_x'].shape
    args.append(nc.dram_tensor("out_x", shape, F32, kind="ExternalOutput").ap())
    build(nc, *args)
    r = run_bass_kernel_spmd(nc, [arrays], core_ids=[0])
    return r.results[0]["out_x"]
```

```python
from contextlib import ExitStack

import concourse.bass as bass
from concourse import mybir

F32 = mybir.dt.float32
F16 = mybir.dt.float16
I32 = mybir.dt.int32
ALU = mybir.AluOpType
ACT = mybir.ActivationFunctionType
AX_X = mybir.AxisListType.X
ds = bass.ds


def build(nc, x, W_q, W_k, W_v, qkv_w, qkv_b, out_w, out_b, gate_w, gate_b, sh_w1, sh_b1, sh_w2,
          sh_b2, ew1, eb1, ew2, eb2, out):
    NBATCH, SEQ, D = x.shape
    P = 128
    T = NBATCH * SEQ // P
    CB = SEQ // P
    E, _, I = ew1.shape
    NE = E + 1
    CH = I // P
    TOPK = 2
    BT = 2
    BR = BT * P
    NBLK = -(-(TOPK * T * P + E * (BR - 1)) // BR // 4) * 4
    NT = NBLK * BT
    NS = T // BT
    NHEAD, HD = 16, D // 16
    HG = NHEAD // 4
    assert (D, CB, HD) == (128, 2, 8) and NBLK % 4 == 0 and NS % 4 == 0

    XS = 8.0
    WS = 64.0
    PS = XS * WS
    KX = 16384.0
    RND = 12582912.0

    def mid(n):
        return (n - 1) / (2.0 * n)

    MIDDLE = T * P // 2
    assert MIDDLE <= 2048

    B1, B2 = 0, NE * I
    BG = B2 + NE * D
    BQKV = BG + E
    BO = BQKV + 3 * D
    BQS = BO + D
    BKS = BQS + 4 * P
    BN = BKS + 4 * P

    ctx = ExitStack()
    with ctx:
        def sb(name, shape, dt):
            return ctx.enter_context(nc.sbuf_tensor(name, shape, dt))

        def sem(name):
            return ctx.enter_context(nc.semaphore(name))

        xres = sb("xres", [P, T, D], F32)
        xn = sb("xn", [P, T, D], F32)
        hl = sb("hl", [P, T, 2 * D], F16)
        xT = sb("xT", [P, T, 2 * P], F16)
        w1s = sb("w1s", [P, NE, 2, I], F16)
        w2s = sb("w2s", [P, NE, 2, CH * D], F16)
        bt = sb("bt", [P, BN], F16)
        gws = sb("gws", [P, 2, E], F16)
        waT = sb("waT", [P, 2, 3 * D], F16)
        wbT = sb("wbT", [P, 2, 4 * D], F16)
        wqk = sb("wqk", [P, 2, 2, 4 * P], F16)
        scratch = sb("scratch", [P, 4096], F32)
        ident16 = sb("ident16", [P, P], F16)
        ident32 = sb("ident32", [P, P], F32)
        upper16 = sb("upper16", [P, P], F16)
        ones16 = sb("ones16", [P, P], F16)
        cXS = sb("cXS", [P, SEQ], F16)
        zero16 = sb("zero16", [P, P], F16)
        onesC = sb("onesC", [P, P], F32)
        iota_i = sb("iota_i", [P, P], I32)
        iota_f = sb("iota_f", [P, P], F32)
        iota16 = sb("iota16", [P, P], F16)
        ids_i = sb("ids_i", [P, T], I32)
        ids_f = sb("ids_f", [P, T], F32)
        part_i = sb("part_i", [P, 4], I32)
        nsel = sb("nsel", [P, 2], F32)
        eps = sb("eps", [P, 1], F32)
        cWS = sb("cWS", [P, 1], F32)
        reset = sb("reset", [P, E, T], F32)
        stats = sb("stats", [P, T, 6], F32)
        mean = sb("mean", [P, T], F32)
        var = sb("var", [P, T], F32)
        gap = sb("gap", [P, T], F32)
        rstd = sb("rstd", [P, T], F32)
        rstdXS = sb("rstdXS", [P, T], F32)
        bnat = sb("bnat", [P, 56], F32)
        bhi = sb("bhi", [P, 56], F16)
        blo = sb("blo", [P, 56], F16)
        ssq = sb("ssq", [P, 2, CB, 2], F32)
        rnorm = sb("rnorm", [P, 2, CB, 2], F32)
        h32 = sb("h32", [P, 2, CH * BR], F32)
        hhi = sb("hhi", [P, 2, CH * BR], F16)
        hlo = sb("hlo", [P, 2, CH * BR], F16)
        xg = sb("xg", [P, 4, 2 * BR], F16)
        yst = sb("yst", [P, 4, BT, D], F32)
        gidx = sb("gidx", [P, 4, BT], I32)
        yidx = sb("yidx", [P, 4, 4], I32)
        prob = sb("prob", [P, T, E], F32)
        rt = [sb(f"rt{i}", [P, T, E], F32) for i in range(3)]
        mask = [sb(f"mask{k}", [P, T, E], F32) for k in range(TOPK)]
        mask16 = sb("mask16", [P, E, T], F16)
        rs = [sb(f"rs{i}", [P, T], F32) for i in range(3)]
        topp = sb("topp", [P, TOPK, T], F32)
        wtop = sb("wtop", [P, TOPK, T], F32)
        cum = sb("cum", [P, E, T], F32)
        slotb = sb("slotb", [P, E, T], F32)
        e8 = [sb(f"e8_{i}", [P, E], F32) for i in range(4)]
        slot = sb("slot", [P, TOPK, T], F32)
        blk = sb("blk", [P, TOPK, T], F32)
        row = sb("row", [P, TOPK, T], F32)
        slot_i = sb("slot_i", [P, TOPK, T], I32)
        bexp = sb("bexp", [P, NBLK, E], F32)
        bexpf = sb("bexpf", [P, NBLK], F32)
        bexp_i = sb("bexp_i", [P, NBLK], I32)
        tok_i = sb("tok_i", [P, NT], I32)
        onerow = sb("onerow", [P, 2, 4, TOPK, P], F16)
        oneblk = sb("oneblk", [P, 2, 4, TOPK, NT], F16)

        ps = ctx.enter_context(nc.psum_tensor("ps", [P, 8, 512], F32))

        rows_dram = [nc.dram_tensor(f"rows{r}", [T * P, 2 * D], F16, kind="Internal").ap()
                     for r in range(2)]
        y_dram = [nc.dram_tensor(f"ysorted{r}", [NT * P, D], F32, kind="Internal").ap()
                  for r in range(2)]

        qst = sb("qst", [P, 2, HG, SEQ], F16)
        kst = sb("kst", [P, 2, HG, SEQ], F16)
        vx = sb("vx", [P, 2, CB, NHEAD, 32], F32)
        mx = sb("mx", [P, CB, NHEAD], F32)
        rsum = sb("rsum", [P, CB, NHEAD], F32)
        prb = scratch[:, :].rearrange("p (n k) -> p n k", n=8)
        qkhi = hhi[:, 0, :].rearrange("p (f n) -> p f n", f=2)
        negmax = hlo[:, 0, :].rearrange("p (c n) -> p c n", c=CB)
        qst2 = hlo[:, 1, :].rearrange("p (j n) -> p j n", j=HG)
        oT = h32[:, 0, :].rearrange("p (a n) -> p a n", a=2)
        attn = h32[:, 1, 0:CB * D].rearrange("p (c d) -> p c d", c=CB)
        ahi, alo = xg[:, 0, 0:SEQ], xg[:, 1, 0:SEQ]

        def part(at, n, dt=F32):
            return scratch[:, at:at + n].bitcast(dt) if dt != F32 else scratch[:, at:at + n]

        junk = part(0, 4 * D).rearrange("p (n d) -> p n d", n=4)
        vs = part(4 * D, 4 * D).rearrange("p (u c d) -> p u c d", u=2, c=CB)
        gf = part(16 * D, 2 * D).rearrange("p (u d) -> p u d", u=2)
        kv = part(8 * D, 4 * D).rearrange("p (u c d) -> p u c d", u=2, c=CB)
        qg = part(12 * D, 4 * D).rearrange("p (u c d) -> p u c d", u=2, c=CB)
        grow = part(0, 8 * D, F16).rearrange("p (u n) -> p u n", u=8)
        gy = part(8 * D, 16 * D).rearrange("p (v u d) -> p v u d", v=4, u=4)

        wstage = h32[:, :, :].rearrange("p u (w n) -> p u w n", w=2)
        wnat = xn[:, 0:7, :]
        gstage = xn[:, 7, 0:E]

        xd = x.rearrange("b (c p) d -> p (b c) d", p=P)
        od = out.rearrange("b (c p) d -> p (b c) d", p=P)

        BIASES, col = [], 0
        for at, n, b in ((B1, E * I, eb1.rearrange("e i -> (e i)")), (B1 + E * I, I, sh_b1),
                         (B2, E * D, eb2.rearrange("e d -> (e d)")), (B2 + E * D, D, sh_b2),
                         (BQKV, 3 * D, qkv_b), (BO, D, out_b), (BG, E, gate_b)):
            rows = min(P, n)
            BIASES.append((at, n, rows, col, b.rearrange("(p c) -> p c", p=rows)))
            col += n // rows
        NBIAS = col

        x_in = sem("x_in")
        wnat_in = sem("wnat_in")
        bias_in = sem("bias_in")
        bias_hi = sem("bias_hi")
        bias_lo = sem("bias_lo")
        bias_rows = sem("bias_rows")
        ewt_in = [sem(f"ewt_in{u}") for u in range(2)]
        ewt_used = sem("ewt_used")
        const_made = sem("const_made")
        pool_step = sem("pool_step")
        wT_turned = sem("wT_turned")
        wT_hi = sem("wT_hi")
        wT_lo = sem("wT_lo")
        gate_split = sem("gate_split")
        slots_made = sem("slots_made")
        rows_found = sem("rows_found")
        stored = sem("stored")

        class Ln:
            stats = sem("ln_stats")
            var = sem("ln_var")
            merge = sem("ln_merge")
            std = sem("ln_std")
            rstd = sem("ln_rstd")
            norm = sem("ln_norm")
            lo = sem("ln_lo")
            turned = sem("ln_turned")
            xT = sem("ln_xT")
            added = sem("ln_added")

        class Mix:
            qkv = sem("a_qkv")
            v = sem("a_v")
            ssq = sem("a_ssq")
            std = sem("a_std")
            clamped = sem("a_clamped")
            rnorm = sem("a_rnorm")
            kv = sem("a_kv")
            mean = sem("a_mean")
            gf = sem("a_gf")
            qg = sem("a_qg")
            done = sem("a_done")

        class Moe:
            def __init__(self, r):
                self.logits = sem(f"m{r}_logits")
                self.shifted = sem(f"m{r}_shifted")
                self.exp = sem(f"m{r}_exp")
                self.step = sem(f"m{r}_step")
                self.mask = sem(f"m{r}_mask")
                self.rank = sem(f"m{r}_rank")
                self.onehot = sem(f"m{r}_onehot")
                self.index = sem(f"m{r}_index")
                self.tok = sem(f"m{r}_tok")
                self.up = sem(f"m{r}_up")
                self.gelu = sem(f"m{r}_gelu")
                self.hi = sem(f"m{r}_hi")
                self.split = sem(f"m{r}_split")
                self.down = sem(f"m{r}_down")
                self.y = sem(f"m{r}_y")
                self.rows_out = sem(f"m{r}_rows_out")
                self.gidx = sem(f"m{r}_gidx")
                self.gath = [sem(f"m{r}_gath{u}") for u in range(4)]
                self.turn = sem(f"m{r}_turn")
                self.xg = sem(f"m{r}_xg")
                self.y_out = [sem(f"m{r}_y_out{u}") for u in range(4)]
                self.yidx = sem(f"m{r}_yidx")
                self.ygath = [sem(f"m{r}_ygath{u}") for u in range(4)]
                self.half = sem(f"m{r}_half")
                self.last = sem(f"m{r}_last")

        moe = [Moe(r) for r in range(2)]

        class Att:
            cleared = sem("t_cleared")
            full = sem("t_full")
            hi = sem("t_hi")
            stack = sem("t_stack")
            v = sem("t_v")
            score = sem("t_score")
            mx = sem("t_mx")
            neghi = sem("t_neghi")
            neg = sem("t_neg")
            q2 = sem("t_q2")
            scoreT = sem("t_scoreT")
            prob = sem("t_prob")
            pv = sem("t_pv")
            oT = sem("t_oT")
            rsum = sem("t_rsum")
            attn = sem("t_attn")
            ahi = sem("t_ahi")
            alo = sem("t_alo")
            done = sem("t_done")

        class Fill:
            def __init__(self, i, first, *readers):
                self.i, self.first, self.k, self.readers = i, first, 0, list(readers)

            def next(self):
                f = self.first + self.k
                self.k += 1
                return f % 2, self.i * 22 + f + 1

            def bank_free(self, semaphore, count):
                self.readers.append((semaphore, count))
                return self.readers.pop(0)

        LAST = NBATCH - 1

        def attention(eng, start, body, end):
            def projected(b):
                return (Att.stack, 4 * b + 8), (Att.v, b + 2)

            start(Fill(0, 0, None, None))
            body(0, 0, Fill(0, 12, *projected(0)), False, True, True)
            with eng.Fori(0, (NBATCH - 4) // 2) as i:
                body(2 * i + 1, 1, Fill(i, 19, *projected(2 * i + 1)), True, True, True)
                body(2 * i + 2, 0, Fill(i, 30, *projected(2 * i + 2)), True, True, True)
            at = 19 + 11 * (NBATCH - 4)
            body(LAST - 2, 1, Fill(0, at, *projected(LAST - 2)), True, True, True)
            body(LAST - 1, 0, Fill(0, at + 11, *projected(LAST - 1)), True, True, False)
            body(LAST, 1, Fill(0, at + 17, (Att.q2, 2 * LAST + 1), (Att.q2, 2 * LAST + 2)), True, False, False)
            end(Fill(0, at + 21, (Att.alo, LAST), (Att.done, LAST)), LAST)

        block = ctx.enter_context(nc.Block())

        HB = [ps[:, 2 * u:2 * u + 2, :].rearrange("p b n -> p (b n)") for u in range(2)]
        YB = [ps[:, 4 + u, 0:BT * D].rearrange("p (k d) -> p k d", k=BT) for u in range(2)]
        TB = [ps[:, 6 + u, :].bitcast(F16) for u in range(2)]
        IDX = ps[:, 7, 0:NT]
        GATE = ps[:, 4, 0:T * E]
        RANK = ps[:, 5, 0:E * T]
        TOT = ps[:, 5, E * T:2 * E * T]

        def two(ap, t):
            return ap[:, ds(2 * t, 2), :]

        @block.sync
        def _(sp):
            for g in range(4):
                n = T // 4
                sp.dma_start(xres[:, g * n:(g + 1) * n, :], xd[:, g * n:(g + 1) * n, :]).then_inc(x_in, 16)
            for i, w in enumerate((W_q, W_k, W_v)):
                sp.dma_start(wnat[:, i, :], w).then_inc(wnat_in, 16)
            sp.dma_start(wnat[:, 3:6, :], qkv_w.rearrange("(m p) d -> p m d", p=P)).then_inc(wnat_in, 16)
            sp.dma_start(wnat[:, 6, :], out_w).then_inc(wnat_in, 16)
            sp.dma_start(gstage, gate_w).then_inc(wnat_in, 16)
            for at, n, rows, c, b in BIASES:
                sp.dma_start(bnat[0:rows, c:c + n // rows], b).then_inc(bias_in, 16)

            def expert(e, u, w1, w2):
                sp.dma_start(wstage[:, u, 0, :], w1).then_inc(ewt_in[u], 16)
                sp.dma_start(wstage[:, u, 1, :].rearrange("p (c d) -> p c d", c=CH), w2).then_inc(ewt_in[u], 16)

            def one(w, e):
                return w[ds(e, 1), :, :].rearrange("a p n -> (a p) n")

            def two_of(e):
                return one(ew1, e), one(ew2, e).rearrange("(c p) d -> p c d", p=P)

            for u in range(2):
                expert(u, u, *two_of(u))
            sp.wait_ge(bias_lo, 1)
            for at, n, rows, c, b in BIASES:
                for r, half in ((0, bhi), (1, blo)):
                    sp.dma_start(bt[r:r + 1, at:at + n], half[0:rows, c:c + n // rows]).then_inc(bias_rows, 16)
            with sp.Fori(0, (E - 2) // 2) as i:
                for u in range(2):
                    sp.wait_ge(ewt_used, 2 * i + u + 1)
                    expert(0, u, *two_of(2 * i + 2 + u))
            sp.wait_ge(ewt_used, E - 1)
            expert(E, 0, sh_w1, sh_w2.rearrange("(c p) d -> p c d", p=P))

            def moe_stores(r):
                m, l, first = moe[r], Ln, (2 * r + 1) * NBATCH
                rows = rows_dram[r].rearrange("(t p) n -> p t n", p=P)
                with sp.Fori(0, NBATCH) as b:
                    sp.wait_ge(l.lo, first + b + 1)
                    sp.dma_start(two(rows, b), two(hl, b)).then_inc(m.rows_out, 16)
                ys = y_dram[r].rearrange("(n k p) d -> p n k d", p=P, k=BT)
                with sp.Fori(0, NBLK // 4) as i:
                    for u in range(4):
                        sp.wait_ge(m.y, 2 + 4 * i + u + 1)
                        sp.dma_start(ys[:, ds(4 * i + u, 1), :, :], yst[:, u:u + 1, :, :]).then_inc(m.y_out[u], 16)

            moe_stores(0)
            moe_stores(1)
            sp.wait_ge(moe[1].last, T)
            sp.dma_start(od, xres[:, :, :]).then_inc(stored, 16)
            sp.wait_ge(stored, 16)

        @block.gpsimd
        def _(pool):
            steps = [0]

            def link(ins):
                steps[0] += 1
                ins.then_inc(pool_step, 1)
                pool.wait_ge(pool_step, steps[0])

            pool.iota(part_i[:, 0:1], pattern=[[0, 1]], base=0, channel_multiplier=1)
            pool.iota(iota_i[:, :], pattern=[[1, P]], base=0, channel_multiplier=0)
            pool.iota(ids_i[:, :], pattern=[[P, T]], base=-MIDDLE, channel_multiplier=1)
            pool.memset(ident16[:, :], 0.0)
            pool.memset(ident32[:, :], 0.0)
            pool.memset(upper16[:, :], 1.0)
            pool.memset(reset[:, :, :], 1.0)
            pool.memset(onesC[:, :], 1.0 / (SEQ * PS))
            pool.memset(ones16[:, :], 1.0)
            pool.memset(cXS[:, :], XS)
            pool.memset(zero16[:, :], 0.0)
            pool.memset(cWS[:, :], WS)
            link(pool.memset(eps[:, :], 1e-5))
            for m in (ident16, ident32):
                pool.affine_select(out=m[:, :], in_=m[:, :], compare_op=ALU.not_equal, fill=1.0,
                                   base=0, pattern=[[-1, P]], channel_multiplier=1)
            pool.affine_select(out=upper16[:, :], in_=upper16[:, :], compare_op=ALU.is_gt, fill=0.0,
                               base=0, pattern=[[1, P]], channel_multiplier=-1)
            pool.tensor_copy(iota_f[:, :], iota_i[:, :])
            pool.tensor_copy(iota16[:, :], iota_i[:, :])
            pool.tensor_copy(ids_f[:, :], ids_i[:, :])
            pool.memset(reset[:, :, 0:1], 0.0)
            pool.memset(bt[:, :], 0.0).then_inc(const_made, 1)

            def half(w, e, h):
                return w[:, ds(e, 1), h, :]

            def split_expert(e, u, loads):
                before = steps[0] + 4 * e
                pool.wait_ge(ewt_in[u], loads)
                for n, w in ((1, 0), (2, 1)):
                    pool.tensor_tensor(wstage[:, u, w, :], wstage[:, u, w, :], cWS[:, 0:1].to_broadcast([P, I]), ALU.mult)\
                        .then_inc(pool_step, 1)
                for n, w, dst in ((1, 0, w1s), (2, 1, w2s)):
                    pool.wait_ge(pool_step, before + n)
                    pool.tensor_copy(half(dst, e, 0), wstage[:, u, w:w + 1, :]).then_inc(pool_step, 1)
                pool.wait_ge(pool_step, before + 4)
                pool.tensor_tensor(half(w1s, e, 1), wstage[:, u, 0:1, :], half(w1s, e, 0), ALU.subtract)
                pool.tensor_tensor(half(w2s, e, 1), wstage[:, u, 1:2, :], half(w2s, e, 0), ALU.subtract)\
                    .then_inc(ewt_used, 1)

            with pool.Fori(0, E // 2) as i:
                for u in range(2):
                    split_expert(2 * i + u, u, 32 * (i + 1))
            split_expert(E, 0, 32 * (E // 2 + 1))
            steps[0] += 4 * NE
            pool.memset(wqk[:, :, :, :], 0.0)
            pool.memset(vx[:, :, :, :, :], 0.0)
            pool.wait_ge(wT_lo, 1)
            link(pool.memset(bt[0:1, BKS:BKS + 4 * P].rearrange("p (h s) -> p h s", s=32)[:, :, 24:26], KX / XS))
            pool.wait_ge(bias_rows, 2 * 16 * len(BIASES))
            pool.memset(vx[:, :, :, :, HD:HD + 1], 1.0)
            for j, at in ((0, BQS), (1, BKS)):
                for rep in range(3):
                    f = slice(rep * HD, (rep + 1) * HD)
                    for h in range(2):
                        pool.tensor_copy(wqk[:, h, j, :].rearrange("p (h s) -> p h s", s=32)[:, :, f],
                                         wbT[:, h, j * D:(j + 1) * D].rearrange("p (h d) -> p h d", d=HD))
                    last = pool.tensor_copy(bt[0:2, at:at + 4 * P].rearrange("p (h s) -> p h s", s=32)[:, :, f],
                                            bt[0:2, BQKV + j * D:BQKV + (j + 1) * D].rearrange("p (h d) -> p h d", d=HD))
            last.then_inc(slots_made, 1)

            def moe_rows(r):
                m, l, first = moe[r], Ln, (2 * r + 1) * NBATCH
                with pool.Fori(0, NBATCH) as b:
                    pool.wait_ge(l.norm, first + b + 1)
                    pool.tensor_tensor(two(xres, b), two(xres, b), two(xn, b), ALU.add).then_inc(l.added, 1)
                for u in range(4):
                    pool.sem_inc(m.y_out[u], 16)
                pool.wait_ge(m.tok, 1)

                def fetches(groups, numbers, copied, used, fetch):
                    def step(f, v):
                        if not (isinstance(f, int) and f < 3):
                            used(f - 3)
                        pool.wait_ge(copied, f + 1)
                        if not (isinstance(f, int) and f + 1 == groups):
                            numbers(f + 1, (v + 1) % 4)
                        fetch(v)

                    numbers(0, 0)
                    for f in range(3):
                        step(f, f)
                    passes = (groups - 4) // 4
                    with pool.Fori(0, passes) as i:
                        for v in range(4):
                            step(4 * i + v + 3, (v + 3) % 4)
                    for f in range(4 * passes + 3, groups):
                        step(f, f % 4)

                def row_numbers(f, v):
                    pool.tensor_copy(gidx[:, v, :], tok_i[:, ds(BT * f, BT)]).then_inc(m.gidx, 1)

                def rows_used(f):
                    pool.wait_ge(m.turn, f + 1)

                def fetch_rows(v):
                    for t in range(BT):
                        pool.indirect_dma_start(grow[:, BT * v + t, :], None, rows_dram[r],
                                                bass.IndirectOffsetOnAxis(ap=gidx[:, v, t:t + 1], axis=0))\
                            .then_inc(m.gath[v], 16)

                pool.wait_ge(m.rows_out, 16 * NBATCH)
                fetches(NBLK, row_numbers, m.gidx, rows_used, fetch_rows)

                def y_numbers(f, v):
                    pool.tensor_copy(yidx[:, v, :].rearrange("p (c k) -> p k c", k=TOPK),
                                     slot_i[:, :, ds(2 * f, 2)]).then_inc(m.yidx, 1)

                def y_used(f):
                    pool.wait_ge(m.last, 2 * f + 2)

                def fetch_y(v):
                    for u in range(4):
                        pool.indirect_dma_start(gy[:, v, u, :], None, y_dram[r],
                                                bass.IndirectOffsetOnAxis(ap=yidx[:, v, u:u + 1], axis=0))\
                            .then_inc(m.ygath[v], 16)

                for u in range(4):
                    pool.wait_ge(m.y_out[u], 16 * (NBLK // 4 + 1))
                fetches(T // 2, y_numbers, m.yidx, y_used, fetch_y)

            moe_rows(0)
            pool.wait_ge(moe[0].last, T)
            pool.memset(negmax, 0.0).then_inc(Att.cleared, 1)
            moe_rows(1)

        @block.tensor
        def _(pe):
            def mm(o, a, b, start, stop):
                return pe.matmul(o, a, b, start=start, stop=stop)

            pe.wait_ge(const_made, 1)
            pe.wait_ge(wnat_in, 6 * 16)
            for i in range(7):
                turned = pe.transpose(ps[:, i // 4, P * (i % 4):P * (i % 4 + 1)], wnat[:, i, :], ident32[:, :])
            turned.then_inc(wT_turned, 1)

            def norm_turns(r, gate):
                l, first = Ln, r * NBATCH

                def turn(b, u):
                    pe.wait_ge(l.lo, first + b + 1)
                    for c in range(CB):
                        for h in range(2):
                            o = c * 2 * P + h * P
                            last = pe.transpose(TB[u][:, o:o + P],
                                                hl[:, ds(2 * b + c, 1), h * D:(h + 1) * D], ident16[:, :])
                    last.then_inc(l.turned, 1)

                def logits(b):
                    if not gate:
                        return
                    for c in range(CB):
                        t = 2 * b + c
                        o = GATE[:, ds(E * t, E)]
                        hi, lo = xT[:, ds(t, 1), 0:P], xT[:, ds(t, 1), P:2 * P]
                        mm(o, hi, gws[:, 0, :], True, False)
                        mm(o, hi, gws[:, 1, :], False, False)
                        mm(o, lo, gws[:, 0, :], False, False)
                        last = mm(o, cXS[:, 0:P], bt[:, BG:BG + E], False, True)
                    return last

                turn(0, 0)
                turn(1, 1)
                with pe.Fori(0, NBATCH // 2 - 1) as i:
                    for u in range(2):
                        b = 2 * i + u
                        pe.wait_ge(l.xT, first + b + 1)
                        turn(b + 2, u)
                        logits(b)
                if gate:
                    pe.wait_ge(l.xT, first + NBATCH)
                    logits(NBATCH - 2)
                    logits(NBATCH - 1).then_inc(moe[r // 2].logits, 1)

            def mix():
                pe.wait_ge(wT_lo, 1)
                pe.wait_ge(Ln.xT, NBATCH)

                def project(b, u):
                    for c in range(CB):
                        t = 2 * b + c
                        o = ps[:, 2 * u + c, 0:3 * D]
                        hi, lo = xT[:, ds(t, 1), 0:P], xT[:, ds(t, 1), P:2 * P]
                        mm(o, hi, waT[:, 0, :], True, False)
                        mm(o, hi, waT[:, 1, :], False, False)
                        last = mm(o, lo, waT[:, 0, :], False, True)
                    last.then_inc(Mix.qkv, 1)

                def mean(b, u):
                    pe.wait_ge(Mix.kv, b + 1)
                    mm(ps[:, 4 + u, 0:D], onesC[:, :], kv[:, u, 0, :], True, False)
                    mm(ps[:, 4 + u, 0:D], onesC[:, :], kv[:, u, 1, :], False, True).then_inc(Mix.mean, 1)

                project(0, 0)
                project(1, 1)
                with pe.Fori(0, NBATCH // 2 - 1) as i:
                    for u in range(2):
                        b = 2 * i + u
                        mean(b, u)
                        pe.wait_ge(Mix.qg, b + 1)
                        project(b + 2, u)
                mean(NBATCH - 2, 0)
                mean(NBATCH - 1, 1)

            def moe_blocks(r):
                m = moe[r]
                pe.wait_ge(m.mask, 1)
                flat = mask16[:, :, :].rearrange("p e t -> p (e t)")
                mm(RANK, upper16[:, :], flat, True, True)
                mm(TOT, ones16[:, :], flat, True, True).then_inc(m.rank, 1)

                def up(n, u, e, hi, lo):
                    if not (isinstance(n, int) and n < 2):
                        pe.wait_ge(m.gelu, n - 1)
                    for c in range(CH):
                        o = HB[u % 2][:, c * BR:(c + 1) * BR]
                        f = slice(c * P, (c + 1) * P)
                        w = w1s[:, ds(e, 1), 0, f]
                        mm(o, w, hi, True, False)
                        mm(o, w, lo, False, False)
                        mm(o, w1s[:, ds(e, 1), 1, f], hi, False, False)
                        last = mm(o, bt[:, ds(B1 + e * I + c * P, P)], cXS[:, 0:BR], False, True)
                    last.then_inc(m.up, 1)

                def down(n, u, e):
                    pe.wait_ge(m.split, n + 1)
                    pe.wait_ge(m.y, n + 1)
                    for c in range(CH):
                        f = slice(c * D, (c + 1) * D)
                        whi, wlo = w2s[:, ds(e, 1), 0, f], w2s[:, ds(e, 1), 1, f]
                        for k, (h, w) in enumerate(((hhi, whi), (hlo, whi), (hhi, wlo))):
                            for t in range(BT):
                                at = c * BR + t * P
                                pe.matmul(YB[u % 2][:, t, :], h[:, u % 2, at:at + P], w,
                                          start=(c, k, t) == (0, 0, 0), stop=False, skip_group_check=True)
                    for t in range(BT):
                        last = pe.matmul(YB[u % 2][:, t, :], cXS[:, 0:P], bt[:, ds(B2 + e * D, D)],
                                         start=False, stop=t == BT - 1, skip_group_check=True)
                    last.then_inc(m.down, 1)

                def number(g, u):
                    pe.wait_ge(m.onehot, g + 1)
                    for c in range(4):
                        for k in range(TOPK):
                            last = mm(IDX, onerow[:, u, c, k, :], oneblk[:, u, c, k, :], False, False)
                    last.then_inc(m.index, 1)

                mm(IDX, zero16[:, :], zero16[:, 0:NT], True, False)
                with pe.Fori(0, T // 8) as i:
                    for u in range(2):
                        number(2 * i + u, u)
                mm(IDX, zero16[:, :], zero16[:, 0:NT], False, True).then_inc(m.index, 1)

                def up_shared(n, u):
                    up(NBLK + n, u, E, two(xT, n)[:, :, 0:P], two(xT, n)[:, :, P:2 * P])

                def experts(n, k):
                    return nc.values_load_multi_w_load_instructions(
                        bexp_i[0:1, ds(n, k)], engines=[mybir.EngineType.PE], min_val=0, max_val=E - 1,
                        skip_runtime_bounds_check_because="VectorE kept it within 0 and E - 1")[1]

                def turn(n, u, i):
                    pe.wait_ge(m.gath[u], 16 * BT * (i + 1))
                    for h in range(2):
                        for t in range(BT):
                            o = h * BR + t * P
                            last = pe.transpose(TB[u % 2][:, o:o + P],
                                                grow[:, BT * u + t, h * D:(h + 1) * D], ident16[:, :])
                    last.then_inc(m.turn, 1)

                def up_routed(n, u, e):
                    pe.wait_ge(m.xg, n + 1)
                    up(n, u, e, xg[:, u, 0:BR], xg[:, u, BR:2 * BR])

                pe.wait_ge(ewt_used, NE)
                turn(0, 0, 0)
                turn(1, 1, 0)
                es = experts(0, 2)
                up_routed(0, 0, es[0])
                turn(2, 2, 0)
                up_routed(1, 1, es[1])
                with pe.Fori(0, NBLK // 4 - 1) as i:
                    es = experts(4 * i, 6)
                    for u in range(4):
                        n = 4 * i + u
                        up_routed(n + 2, (u + 2) % 4, es[u + 2])
                        turn(n + 3, (u + 3) % 4, i + (u + 3) // 4)
                        down(n, u, es[u])
                es = experts(NBLK - 4, 4)
                for u in range(4):
                    n = NBLK - 4 + u
                    if u < 2:
                        up_routed(n + 2, u + 2, es[u + 2])
                    else:
                        up_shared(u - 2, u)
                    if u < 1:
                        turn(n + 3, u + 3, NBLK // 4 - 1)
                    down(n, u, es[u])
                with pe.Fori(0, NS // 2 - 1) as i:
                    for u in range(2):
                        up_shared(2 * i + u + 2, u)
                        down(NBLK + 2 * i + u, u, E)
                for u in range(2):
                    down(NBLK + NS - 2 + u, u, E)

            def heads(hh):
                return slice(32 * hh, 32 * hh + 3 * HD), slice(32 * hh, 32 * hh + 32)

            def attn_fill(fill, semaphore, count):
                bank, _ = fill.next()
                before = fill.bank_free(semaphore, count)
                if before is not None:
                    pe.wait_ge(*before)
                return ps[:, 6 + bank, :]

            def project(fill, b, g):
                o = attn_fill(fill, Att.stack, 4 * b + g + 1)
                hi, lo = two(xT, b)[:, :, 0:P], two(xT, b)[:, :, P:2 * P]
                for n in range(2):
                    f = slice((2 * (g % 2) + n) * P, (2 * (g % 2) + n + 1) * P)
                    at = (BQS, BKS)[g // 2]
                    on = o[:, n * SEQ:(n + 1) * SEQ]
                    w = wqk[:, :, g // 2, f]
                    mm(on, w[:, 0, :], hi, True, False)
                    mm(on, w[:, 0, :], lo, False, False)
                    mm(on, w[:, 1, :], hi, False, False)
                    last = mm(on, bt[:, at + f.start:at + f.stop], cXS[:, :], False, True)
                last.then_inc(Att.full, 1)

            def values(fill, b):
                o = attn_fill(fill, Att.v, b + 1)
                for c in range(CB):
                    t = 2 * b + c
                    hi, lo = xT[:, ds(t, 1), 0:P], xT[:, ds(t, 1), P:2 * P]
                    on = o[:, c * D:(c + 1) * D]
                    mm(on, hi, wbT[:, 0, 2 * D:3 * D], True, False)
                    mm(on, hi, wbT[:, 1, 2 * D:3 * D], False, False)
                    mm(on, lo, wbT[:, 0, 2 * D:3 * D], False, False)
                    last = mm(on, cXS[:, 0:P], bt[:, BQKV + 2 * D:BQKV + 3 * D], False, True)
                last.then_inc(Att.full, 1)

            def score(b, u, s):
                c, jp, hh = s // 8, s // 4 % 2, s % 4
                if s == 0:
                    pe.wait_ge(Att.stack, 4 * b + 4)
                if not (isinstance(b, int) and 16 * b + s < 2):
                    pe.wait_ge(Att.mx, 16 * b + s - 1)
                for n in range(2):
                    j = 2 * jp + n
                    rows = heads(hh)[0]
                    last = mm(ps[:, 2 + s % 2, n * SEQ:(n + 1) * SEQ], qst[rows, u, j, c * P:(c + 1) * P],
                              kst[rows, u, j, :], True, True)
                last.then_inc(Att.score, 1)

            def maxima(fill, b, u, jp):
                o = attn_fill(fill, Att.q2, 2 * b + jp + 1)
                pe.wait_ge(Att.neg, b + 1)
                for n in range(2):
                    j = 2 * jp + n
                    on = o[:, n * SEQ:(n + 1) * SEQ]
                    mm(on, ident16[:, :], qst[:, u, j, :], True, False)
                    for c in range(CB):
                        last = mm(on[:, c * P:(c + 1) * P], negmax[:, c, j * P:(j + 1) * P], ident16[:, :],
                                  False, c == CB - 1)
                last.then_inc(Att.full, 1)

            def scoreT(b, u, s):
                jp, kc, hh = s // 8, s // 4 % 2, s % 4
                if s == 0:
                    pe.wait_ge(Att.q2, 2 * b + 2)
                if not (isinstance(b, int) and 16 * b + s < 2):
                    pe.wait_ge(Att.prob, 16 * b + s - 1)
                for n in range(2):
                    j = 2 * jp + n
                    rows = heads(hh)[1]
                    last = mm(ps[:, s % 2, n * SEQ:(n + 1) * SEQ], kst[rows, u, j, kc * P:(kc + 1) * P],
                              qst2[rows, j, :], True, True)
                last.then_inc(Att.scoreT, 1)

            def weigh(b, u, g):
                jp, kc = g // 2, g % 2
                pe.wait_ge(Att.prob, 16 * b + 4 * g + 4)
                if g == 0:
                    pe.wait_ge(Att.v, b + 1)
                    if not (isinstance(b, int) and b == 0):
                        pe.wait_ge(Att.oT, 2 * b)
                for n in range(2):
                    for hh in range(4):
                        last = pe.matmul(ps[32 * hh:32 * hh + 32, 4 + jp, n * SEQ:(n + 1) * SEQ],
                                         vx[:, u, kc, 4 * (2 * jp + n) + hh, :],
                                         prb[:, (4 * g + hh) % 8, n * SEQ:(n + 1) * SEQ],
                                         start=kc == 0 and n == 0, stop=kc == 1 and n == 1,
                                         skip_group_check=True)
                last.then_inc(Att.pv, 1)

            def turn_back(fill, b, c):
                o = attn_fill(fill, Att.attn, 2 * b + c + 1)
                pe.wait_ge(Att.oT, 2 * b + 2)
                for j in range(HG):
                    last = pe.transpose(o[:, j * P:(j + 1) * P],
                                        oT[:, j // 2, (j % 2) * SEQ + c * P:(j % 2) * SEQ + (c + 1) * P], ident32[:, :])
                last.then_inc(Att.full, 1)

            def turn_attn(fill, b):
                o = attn_fill(fill, Att.alo, b + 1)
                pe.wait_ge(Att.attn, 2 * b + 2)
                for c in range(CB):
                    last = pe.transpose(o[:, c * P:(c + 1) * P], attn[:, c, :], ident32[:, :])
                last.then_inc(Att.full, 1)

            def out_project(fill, b):
                o = attn_fill(fill, Att.done, b + 1)
                pe.wait_ge(Att.alo, b + 1)
                for c in range(CB):
                    f = slice(c * P, (c + 1) * P)
                    on = o[:, c * D:(c + 1) * D]
                    mm(on, ahi[:, f], wbT[:, 0, 3 * D:4 * D], True, False)
                    mm(on, ahi[:, f], wbT[:, 1, 3 * D:4 * D], False, False)
                    mm(on, alo[:, f], wbT[:, 0, 3 * D:4 * D], False, False)
                    last = mm(on, cXS[:, 0:P], bt[:, BO:BO + D], False, True)
                last.then_inc(Att.full, 1)

            def attn_body(b, u, fill, output, ahead, project2):
                for s in range(16):
                    if ahead:
                        score(b + 1, 1 - u, s)
                    scoreT(b, u, s)
                    if s in (6, 10, 14):
                        weigh(b, u, (s - 6) // 4)
                    if output and s == 3:
                        turn_back(fill, b - 1, 0)
                        turn_back(fill, b - 1, 1)
                    if output and s == 8:
                        turn_attn(fill, b - 1)
                    if output and s == 13:
                        out_project(fill, b - 1)
                weigh(b, u, 3)
                if project2:
                    project(fill, b + 2, 0)
                    project(fill, b + 2, 1)
                if ahead:
                    maxima(fill, b + 1, 1 - u, 0)
                    maxima(fill, b + 1, 1 - u, 1)
                if project2:
                    project(fill, b + 2, 2)
                    project(fill, b + 2, 3)
                    values(fill, b + 2)

            def attn_start(fill):
                for g in range(4):
                    project(fill, 0, g)
                values(fill, 0)
                for s in range(16):
                    score(0, 0, s)
                maxima(fill, 0, 0, 0)
                maxima(fill, 0, 0, 1)
                for g in range(4):
                    project(fill, 1, g)
                values(fill, 1)

            def attn_end(fill, b):
                turn_back(fill, b, 0)
                turn_back(fill, b, 1)
                turn_attn(fill, b)
                out_project(fill, b)

            norm_turns(0, False)
            mix()
            pe.wait_ge(bias_rows, 2 * 16 * len(BIASES))
            norm_turns(1, True)
            moe_blocks(0)
            norm_turns(2, False)
            pe.wait_ge(slots_made, 1)
            pe.wait_ge(Ln.xT, 3 * NBATCH)
            attention(pe, attn_start, attn_body, attn_end)
            norm_turns(3, True)
            moe_blocks(1)

        @block.scalar
        def _(act):
            act.wait_ge(wT_turned, 1)
            act.activation(waT[:, 0, :], ps[:, 0, 0:3 * D], ACT.Copy, scale=WS)
            act.activation(wbT[:, 0, 0:D], ps[:, 0, 3 * D:4 * D], ACT.Copy, scale=WS)
            act.activation(wbT[:, 0, D:4 * D], ps[:, 1, 0:3 * D], ACT.Copy, scale=WS)
            act.activation(gws[:, 0, :], gstage, ACT.Copy, scale=WS).then_inc(wT_hi, 1)

            def std(r):
                l, first = Ln, r * NBATCH
                act.wait_ge(l.var, r + 1)
                act.activation(rstd[:, :], var[:, :], ACT.Sqrt, bias=eps[:, 0:1], scale=1.0 / D).then_inc(l.std, 1)

            def norm(r):
                l, first = Ln, r * NBATCH

                def copy_out(b, u):
                    act.wait_ge(l.turned, first + b + 1)
                    act.activation(two(xT, b), TB[u][:, 0:4 * P].rearrange("p (c f) -> p c f", c=CB),
                                   ACT.Copy).then_inc(l.xT, 1)

                with act.Fori(0, NBATCH // 2) as i:
                    for u in range(2):
                        copy_out(2 * i + u, u)

            def mix():
                def norms(b, u):
                    act.wait_ge(Mix.qkv, b + 1)
                    for c in range(CB):
                        for j in range(2):
                            last = act.activation(junk[:, 2 * c + j, :], ps[:, 2 * u + c, j * D:(j + 1) * D], ACT.Square,
                                                  accum_out=ssq[:, u, c, j:j + 1])
                    last.then_inc(Mix.ssq, 1)
                    act.wait_ge(Mix.ssq, b + 1)
                    act.activation(rnorm[:, u, :, :], ssq[:, u, :, :], ACT.Sqrt).then_inc(Mix.std, 1)

                def value(b, u):
                    act.activation(vs[:, u, :, :], ps[:, 2 * u:2 * u + 2, 2 * D:3 * D], ACT.Copy).then_inc(Mix.v, 1)

                def mean(b, u):
                    act.wait_ge(Mix.mean, b + 1)
                    act.activation(gf[:, u, :], ps[:, 4 + u, 0:D], ACT.Copy).then_inc(Mix.gf, 1)

                norms(0, 0)
                value(0, 0)
                with act.Fori(0, NBATCH // 2 - 1) as i:
                    for u in range(2):
                        norms(2 * i + u + 1, 1 - u)
                        mean(2 * i + u, u)
                        value(2 * i + u + 1, 1 - u)
                norms(NBATCH - 1, 1)
                mean(NBATCH - 2, 0)
                value(NBATCH - 1, 1)
                mean(NBATCH - 1, 1)

            def moe_blocks(r):
                m = moe[r]
                act.wait_ge(m.shifted, 1)
                act.activation(prob[:, :, :], prob[:, :, :], ACT.Exp, scale=1.0 / PS).then_inc(m.exp, 1)

                def gelu(n, u):
                    act.wait_ge(m.up, n + 1)
                    if not (isinstance(n, int) and n < 2):
                        act.wait_ge(m.split, n - 1)
                    act.activation(h32[:, u % 2, :], HB[u % 2], ACT.Gelu_apprx_tanh, scale=1.0 / PS).then_inc(m.gelu, 1)

                def copy_out(n, u):
                    act.wait_ge(m.turn, n + 1)
                    act.activation(xg[:, u, :], TB[u % 2][:, 0:2 * BR], ACT.Copy).then_inc(m.xg, 1)

                copy_out(0, 0)
                copy_out(1, 1)
                gelu(0, 0)
                copy_out(2, 2)
                gelu(1, 1)
                with act.Fori(0, NBLK // 4 - 1) as i:
                    for u in range(4):
                        n = 4 * i + u
                        copy_out(n + 3, (u + 3) % 4)
                        gelu(n + 2, u)
                copy_out(NBLK - 1, 3)
                gelu(NBLK - 2, 0)
                gelu(NBLK - 1, 1)
                with act.Fori(0, NS // 2) as i:
                    for u in range(2):
                        gelu(NBLK + 2 * i + u, u)

            def attn_full(fill):
                bank, count = fill.next()
                act.wait_ge(Att.full, count)
                return bank, ps[:, 6 + bank, :]

            def stack_hi(fill):
                bank, o = attn_full(fill)
                act.activation(qkhi[:, bank, :], o, ACT.Copy).then_inc(Att.hi, 1)

            def values(fill, u):
                bank, o = attn_full(fill)
                for c in range(CB):
                    last = act.activation(vx[:, u, c, :, 0:HD],
                                          o[:, c * D:(c + 1) * D].rearrange("p (h d) -> p h d", d=HD),
                                          ACT.Copy, scale=1.0 / PS)
                last.then_inc(Att.v, 1)

            def maxima(fill, jp):
                bank, o = attn_full(fill)
                act.activation(qst2[:, 2 * jp:2 * jp + 2, :], o.rearrange("p (j n) -> p j n", j=2), ACT.Copy)\
                    .then_inc(Att.q2, 1)

            def exp(b, s):
                act.wait_ge(Att.scoreT, 16 * b + s + 1)
                if s >= 8 and s % 4 == 0:
                    act.wait_ge(Att.pv, 4 * b + (s - 8) // 4 + 1)
                act.activation(prb[:, s % 8, :], ps[:, s % 2, :], ACT.Exp, scale=HD ** -0.5 / (PS * PS))\
                    .then_inc(Att.prob, 1)

            def sums_out(b):
                for jp in range(2):
                    act.wait_ge(Att.pv, 4 * b + 2 * jp + 2)
                    act.activation(oT[:, jp, :], ps[:, 4 + jp, :], ACT.Copy).then_inc(Att.oT, 1)

            def attn_hi(fill):
                bank, o = attn_full(fill)
                act.activation(ahi, o[:, 0:SEQ], ACT.Copy, scale=XS).then_inc(Att.ahi, 1)

            def attn_body(b, u, fill, output, ahead, project2):
                if output:
                    sums_out(b - 1)
                    fill.k += 2
                for s in range(16):
                    exp(b, s)
                    if output and s == 9:
                        attn_hi(fill)
                        fill.k += 1
                if project2:
                    stack_hi(fill)
                    stack_hi(fill)
                if ahead:
                    maxima(fill, 0)
                    maxima(fill, 1)
                if project2:
                    stack_hi(fill)
                    stack_hi(fill)
                    values(fill, u)

            def attn_start(fill):
                for g in range(4):
                    stack_hi(fill)
                values(fill, 0)
                maxima(fill, 0)
                maxima(fill, 1)
                for g in range(4):
                    stack_hi(fill)
                values(fill, 1)

            def attn_end(fill, b):
                sums_out(b)
                fill.k += 2
                attn_hi(fill)

            std(0)
            norm(0)
            mix()
            std(1)
            norm(1)
            moe_blocks(0)
            std(2)
            norm(2)
            attention(act, attn_start, attn_body, attn_end)
            std(3)
            norm(3)
            moe_blocks(1)

        @block.vector
        def _(dve):
            dve.wait_ge(bias_in, 16 * len(BIASES))
            dve.wait_ge(const_made, 1)
            dve.tensor_scalar(bhi[:, 0:NBIAS - 1], bnat[:, 0:NBIAS - 1], WS, None, ALU.mult)
            dve.tensor_scalar(bhi[0:E, NBIAS - 1:NBIAS], bnat[0:E, NBIAS - 1:NBIAS], WS, None, ALU.mult)\
                .then_inc(bias_hi, 1)
            dve.wait_ge(bias_hi, 1)
            dve.scalar_tensor_tensor(blo[:, 0:NBIAS - 1], bnat[:, 0:NBIAS - 1], WS, bhi[:, 0:NBIAS - 1],
                                     ALU.mult, ALU.subtract)
            dve.scalar_tensor_tensor(blo[0:E, NBIAS - 1:NBIAS], bnat[0:E, NBIAS - 1:NBIAS], WS,
                                     bhi[0:E, NBIAS - 1:NBIAS], ALU.mult, ALU.subtract).then_inc(bias_lo, 1)
            dve.tensor_scalar(part_i[:, 1:2], part_i[:, 0:1], 31, 3, ALU.bitwise_and, ALU.arith_shift_right)\
                .then_inc(rows_found, 1)
            dve.wait_ge(rows_found, 1)
            dve.tensor_scalar(nsel[:, 0:1], part_i[:, 1:2], 2.0, -1.0, ALU.is_equal, ALU.mult)
            dve.tensor_scalar(nsel[:, 1:2], part_i[:, 1:2], 1.0, -1.0, ALU.is_equal, ALU.mult)
            dve.wait_ge(wT_hi, 1)
            dve.scalar_tensor_tensor(waT[:, 1, :], ps[:, 0, 0:3 * D], WS, waT[:, 0, :], ALU.mult, ALU.subtract)
            dve.scalar_tensor_tensor(wbT[:, 1, 0:D], ps[:, 0, 3 * D:4 * D], WS, wbT[:, 0, 0:D],
                                     ALU.mult, ALU.subtract)
            dve.scalar_tensor_tensor(wbT[:, 1, D:4 * D], ps[:, 1, 0:3 * D], WS, wbT[:, 0, D:4 * D],
                                     ALU.mult, ALU.subtract)
            dve.scalar_tensor_tensor(gws[:, 1, :], gstage, WS, gws[:, 0, :], ALU.mult, ALU.subtract)\
                .then_inc(wT_lo, 1)
            dve.wait_ge(x_in, 4 * 16)

            def norm(r):
                l, first = Ln, r * NBATCH
                with dve.Fori(0, T // 4) as i:
                    for u in range(4):
                        last = dve.bn_stats(stats[:, ds(4 * i + u, 1), :], xres[:, ds(4 * i + u, 1), :])
                    last.then_inc(l.stats, 1)
                dve.wait_ge(l.stats, (r + 1) * (T // 4))
                dve.tensor_tensor(mean[:, :], stats[:, :, 1], stats[:, :, 4], ALU.add)
                dve.tensor_tensor(var[:, :], stats[:, :, 2], stats[:, :, 5], ALU.add)
                dve.tensor_tensor(gap[:, :], stats[:, :, 1], stats[:, :, 4], ALU.subtract).then_inc(l.merge, 1)
                dve.wait_ge(l.merge, 2 * r + 1)
                dve.tensor_scalar(mean[:, :], mean[:, :], 0.5, None, ALU.mult)
                dve.tensor_tensor(gap[:, :], gap[:, :], gap[:, :], ALU.mult).then_inc(l.merge, 1)
                dve.wait_ge(l.merge, 2 * r + 2)
                dve.scalar_tensor_tensor(var[:, :], gap[:, :], D / 4.0, var[:, :], ALU.mult, ALU.add).then_inc(l.var, 1)
                dve.wait_ge(l.std, r + 1)
                dve.reciprocal(rstd[:, :], rstd[:, :]).then_inc(l.rstd, 1)
                dve.wait_ge(l.rstd, 2 * r + 1)
                dve.tensor_scalar(rstdXS[:, :], rstd[:, :], XS, None, ALU.mult).then_inc(l.rstd, 1)
                dve.wait_ge(l.rstd, 2 * r + 2)

                def whole(b):
                    for c in range(CB):
                        t = 2 * b + c
                        for o, scale in ((xn[:, ds(t, 1), :], rstd), (hl[:, ds(t, 1), 0:D], rstdXS)):
                            last = dve.tensor_scalar(o, xres[:, ds(t, 1), :], mean[:, ds(t, 1)], scale[:, ds(t, 1)],
                                                     ALU.subtract, ALU.mult)
                    last.then_inc(l.norm, 1)

                def lo(b):
                    dve.wait_ge(l.norm, first + b + 1)
                    h = two(hl, b)
                    dve.scalar_tensor_tensor(h[:, :, D:2 * D], two(xn, b), XS, h[:, :, 0:D],
                                             ALU.mult, ALU.subtract).then_inc(l.lo, 1)

                whole(0)
                with dve.Fori(0, NBATCH - 1) as b:
                    whole(b + 1)
                    lo(b)
                lo(NBATCH - 1)

            def mix():
                def front(b, u):
                    dve.wait_ge(Mix.std, b + 1)
                    dve.tensor_scalar(rnorm[:, u, :, :], rnorm[:, u, :, :], PS * 1e-12, None, ALU.max)\
                        .then_inc(Mix.clamped, 1)
                    dve.wait_ge(Mix.clamped, b + 1)
                    dve.reciprocal(rnorm[:, u, :, :], rnorm[:, u, :, :]).then_inc(Mix.rnorm, 1)
                    dve.wait_ge(Mix.rnorm, b + 1)
                    dve.wait_ge(Mix.v, b + 1)
                    for c in range(CB):
                        last = dve.scalar_tensor_tensor(kv[:, u, c, :], ps[:, 2 * u + c, D:2 * D], rnorm[:, u, c, 1:2],
                                                        vs[:, u, c, :], ALU.mult, ALU.mult)
                    last.then_inc(Mix.kv, 1)

                def back(b, u):
                    dve.wait_ge(Mix.gf, b + 1)
                    for c in range(CB):
                        last = dve.scalar_tensor_tensor(qg[:, u, c, :], ps[:, 2 * u + c, 0:D],
                                                        rnorm[:, u, c, 0:1], gf[:, u, :],
                                                        ALU.mult, ALU.mult)
                    last.then_inc(Mix.qg, 1)

                def add(b, u):
                    dve.wait_ge(Mix.qg, b + 1)
                    dve.tensor_tensor(two(xres, b), two(xres, b), qg[:, u, :, :], ALU.add).then_inc(Mix.done, 1)

                front(0, 0)
                with dve.Fori(0, NBATCH // 2 - 1) as i:
                    for u in range(2):
                        back(2 * i + u, u)
                        front(2 * i + u + 1, 1 - u)
                        add(2 * i + u, u)
                back(NBATCH - 2, 0)
                front(NBATCH - 1, 1)
                add(NBATCH - 2, 0)
                back(NBATCH - 1, 1)
                add(NBATCH - 1, 1)
                dve.wait_ge(Mix.done, NBATCH)

            def over(ap, axis, n):
                shape = list(ap.shape)
                shape.insert(axis, n)
                return ap.unsqueeze(axis).to_broadcast(shape)

            def moe_blocks(r):
                m = moe[r]
                steps = [0]

                def link(ins):
                    steps[0] += 1
                    ins.then_inc(m.step, 1)
                    dve.wait_ge(m.step, steps[0])

                dve.sem_inc(m.y, 2)
                logit = GATE.rearrange("p (t e) -> p t e", e=E)
                iota_e = over(iota_f[:, 0:E], 1, T)
                dve.wait_ge(m.logits, 1)
                link(dve.tensor_reduce(rs[0][:, :], logit, AX_X, ALU.max))
                dve.tensor_tensor(prob[:, :, :], logit, over(rs[0][:, :], 2, E), ALU.subtract).then_inc(m.shifted, 1)
                dve.wait_ge(m.exp, 1)
                link(dve.tensor_reduce(rs[0][:, :], prob[:, :, :], AX_X, ALU.add))
                link(dve.reciprocal(rs[1][:, :], rs[0][:, :]))
                link(dve.tensor_tensor(prob[:, :, :], prob[:, :, :], over(rs[1][:, :], 2, E), ALU.mult))
                left = prob
                for k in range(TOPK):
                    link(dve.tensor_reduce(topp[:, k, :], left[:, :, :], AX_X, ALU.max))
                    link(dve.tensor_tensor(rt[0][:, :, :], left[:, :, :], over(topp[:, k, :], 2, E), ALU.is_equal))
                    link(dve.scalar_tensor_tensor(rt[1][:, :, :], rt[0][:, :, :], -float(E), iota_e, ALU.mult, ALU.add))
                    link(dve.tensor_reduce(rs[0][:, :], rt[1][:, :, :], AX_X, ALU.min))
                    link(dve.tensor_tensor(mask[k][:, :, :], rt[1][:, :, :], over(rs[0][:, :], 2, E), ALU.is_equal))
                    if k == 0:
                        link(dve.scalar_tensor_tensor(rt[2][:, :, :], mask[0][:, :, :], -2.0, prob[:, :, :],
                                                      ALU.mult, ALU.add))
                        left = rt[2]
                dve.tensor_tensor(mask16[:, :, :].rearrange("p e t -> p t e"), mask[0][:, :, :], mask[1][:, :, :],
                                  ALU.add).then_inc(m.mask, 1)
                link(dve.tensor_tensor(rs[0][:, :], topp[:, 0, :], topp[:, 1, :], ALU.add))
                link(dve.tensor_scalar(rs[1][:, :], rs[0][:, :], 1e-9, None, ALU.add))
                link(dve.reciprocal(rs[2][:, :], rs[1][:, :]))
                link(dve.tensor_tensor(wtop[:, :, :], topp[:, :, :], over(rs[2][:, :], 1, TOPK), ALU.mult))
                link(dve.memset(e8[3][:, :], 1.0))
                dve.wait_ge(m.rank, 1)
                flat = "p e t -> p (e t)"
                link(dve.tensor_tensor_scan(cum[:, :, :].rearrange(flat), reset[:, :, :].rearrange(flat), TOT,
                                            0.0, ALU.mult, ALU.add))
                link(dve.tensor_scalar(e8[0][:, :], cum[:, :, T - 1], 1.0 / BR, (BR - 1.0) / BR - mid(BR), ALU.mult, ALU.add))
                link(dve.tensor_scalar(e8[0][:, :], e8[0][:, :], RND, RND, ALU.add, ALU.subtract))
                link(dve.tensor_tensor_scan(e8[1][:, :], e8[3][:, :], e8[0][:, :], 0.0, ALU.mult, ALU.add))
                link(dve.tensor_tensor(e8[2][:, :], e8[1][:, :], e8[0][:, :], ALU.subtract))
                link(dve.tensor_tensor(slotb[:, :, :].rearrange(flat), cum[:, :, :].rearrange(flat), TOT, ALU.subtract))
                link(dve.scalar_tensor_tensor(slotb[:, :, :], over(e8[2][:, :], 2, T), float(BR), slotb[:, :, :],
                                              ALU.mult, ALU.add))
                link(dve.tensor_tensor(slotb[:, :, :].rearrange(flat), slotb[:, :, :].rearrange(flat), RANK, ALU.add))
                for k in range(TOPK):
                    link(dve.tensor_tensor(rt[0][:, :, :], mask[k][:, :, :], slotb[:, :, :].rearrange("p e t -> p t e"),
                                           ALU.mult))
                    link(dve.tensor_reduce(slot[:, k, :], rt[0][:, :, :], AX_X, ALU.add))
                link(dve.tensor_scalar(blk[:, :, :], slot[:, :, :], 1.0 / P, -mid(P), ALU.mult, ALU.add))
                link(dve.tensor_scalar(blk[:, :, :], blk[:, :, :], RND, RND, ALU.add, ALU.subtract))
                dve.scalar_tensor_tensor(row[:, :, :], blk[:, :, :], -float(P), slot[:, :, :], ALU.mult, ALU.add)
                dve.tensor_copy(slot_i[:, :, :], slot[:, :, :])
                link(dve.tensor_tensor(bexp[:, :, :], over(e8[1][:, :], 1, NBLK), over(iota_f[:, 0:NBLK], 2, E),
                                       ALU.is_le))
                link(dve.tensor_reduce(bexpf[:, :], bexp[:, :, :], AX_X, ALU.add))
                link(dve.tensor_scalar(bexp_i[:, :], bexpf[:, :], float(E - 1), None, ALU.min))

                def split(n, u):
                    dve.wait_ge(m.gelu, n + 1)
                    dve.tensor_scalar(hhi[:, u, :], h32[:, u, :], XS, None, ALU.mult).then_inc(m.hi, 1)
                    dve.wait_ge(m.hi, n + 1)
                    dve.scalar_tensor_tensor(hlo[:, u, :], h32[:, u, :], XS, hhi[:, u, :], ALU.mult, ALU.subtract)\
                        .then_inc(m.split, 1)

                def onehot(g, u):
                    if not (isinstance(g, int) and g < 2):
                        dve.wait_ge(m.index, g - 1)
                    for c in range(4):
                        t = 4 * g + c
                        for k in range(TOPK):
                            dve.tensor_scalar(onerow[:, u, c, k, :], iota16[:, :], row[:, k, ds(t, 1)], None, ALU.is_equal)
                            last = dve.tensor_scalar(oneblk[:, u, c, k, :], iota16[:, 0:NT], blk[:, k, ds(t, 1)],
                                                     ids_f[:, ds(t, 1)], ALU.is_equal, ALU.mult)
                    last.then_inc(m.onehot, 1)

                onehot(0, 0)
                onehot(1, 1)
                with dve.Fori(1, T // 8) as i:
                    for u in range(2):
                        onehot(2 * i + u, u)
                dve.wait_ge(m.index, T // 4 + 1)
                dve.tensor_scalar(tok_i[:, :], IDX, float(MIDDLE), None, ALU.add).then_inc(m.tok, 1)

                def result_routed(n, u, i):
                    dve.wait_ge(m.down, n + 1)
                    dve.wait_ge(m.y_out[u], 16 * (i + 1))
                    dve.tensor_scalar(yst[:, u, :, :], YB[u % 2], 1.0 / PS, None, ALU.mult).then_inc(m.y, 1)

                split(0, 0)
                split(1, 1)
                with dve.Fori(0, NBLK // 4 - 1) as i:
                    for u in range(4):
                        n = 4 * i + u
                        result_routed(n, u, i)
                        split(n + 2, u % 2)
                for u in range(4):
                    n = NBLK - 4 + u
                    result_routed(n, u, NBLK // 4 - 1)
                    split(n + 2, u % 2)

                def result_shared(n, u):
                    dve.wait_ge(m.down, NBLK + n + 1)
                    o = two(xres, n)
                    dve.scalar_tensor_tensor(o, YB[u], 1.0 / PS, o, ALU.mult, ALU.add).then_inc(m.y, 1)

                def combine(f, v, i):
                    dve.wait_ge(m.y, 2 + NBLK + f + 1)
                    dve.wait_ge(m.ygath[v], 64 * (i + 1))
                    for k in range(TOPK):
                        if k:
                            dve.wait_ge(m.half, 2 * f + 2)
                        for c in range(2):
                            t = 2 * f + c
                            o = xres[:, ds(t, 1), :]
                            dve.scalar_tensor_tensor(o, gy[:, v, 2 * c + k, :].unsqueeze(1), wtop[:, k, ds(t, 1)], o,
                                                     ALU.mult, ALU.add).then_inc((m.half, m.last)[k], 1)

                dve.wait_ge(Ln.added, (r + 1) * NBATCH)
                for n in range(2):
                    result_shared(n, n)
                    split(NBLK + n + 2, n)
                with dve.Fori(0, NS // 4 - 1) as i:
                    for v in range(4):
                        n = 4 * i + v + 2
                        result_shared(n, v % 2)
                        split(NBLK + n + 2, v % 2)
                        combine(n - 2, v, i)
                for v in range(4):
                    if v < 2:
                        result_shared(NS - 2 + v, v)
                    combine(NS - 4 + v, v, NS // 4 - 1)

            def attn_full(fill):
                bank, count = fill.next()
                dve.wait_ge(Att.full, count)
                return bank, ps[:, 6 + bank, :]

            def stack(fill, b, u, g):
                bank, o = attn_full(fill)
                dve.wait_ge(Att.hi, 4 * b + g + 1)
                dst = (qst, kst)[g // 2]
                dve.scalar_tensor_tensor(dst[:, u, 2 * (g % 2):2 * (g % 2) + 2, :].rearrange("p j n -> p (j n)"),
                                         qkhi[:, bank, :], nsel[:, g // 2:g // 2 + 1], o, ALU.mult, ALU.add)\
                    .then_inc(Att.stack, 1)

            def maximum(b, s):
                c, jp, hh = s // 8, s // 4 % 2, s % 4
                dve.wait_ge(Att.score, 16 * b + s + 1)
                j = 8 * jp + hh
                dve.tensor_reduce(mx[:, c, j:j + 5:4], ps[:, 2 + s % 2, :].rearrange("p (n k) -> p n k", n=2),
                                  AX_X, ALU.max).then_inc(Att.mx, 1)

            def negate(b):
                slots = negmax.rearrange("p c (h s) -> p c h s", s=32)
                dve.wait_ge(Att.mx, 16 * b + 16)
                dve.tensor_scalar(slots[:, :, :, 24], mx[:, :, :], -1.0 / KX, None, ALU.mult).then_inc(Att.neghi, 1)
                dve.wait_ge(Att.neghi, b + 1)
                dve.scalar_tensor_tensor(slots[:, :, :, 25], mx[:, :, :], -1.0 / KX, slots[:, :, :, 24],
                                         ALU.mult, ALU.subtract).then_inc(Att.neg, 1)

            def normalise(fill, b, c):
                bank, o = attn_full(fill)
                heads = o.rearrange("p (h s) -> p h s", s=32)
                dve.reciprocal(rsum[:, c, :], heads[:, :, HD]).then_inc(Att.rsum, 1)
                dve.wait_ge(Att.rsum, 2 * b + c + 1)
                dve.tensor_tensor(attn[:, c, :].rearrange("p (h d) -> p h d", d=HD), heads[:, :, 0:HD],
                                  over(rsum[:, c, :], 2, HD), ALU.mult)\
                    .then_inc(Att.attn, 1)

            def attn_lo(fill, b):
                bank, o = attn_full(fill)
                dve.wait_ge(Att.ahi, b + 1)
                dve.scalar_tensor_tensor(alo, o[:, 0:SEQ], XS, ahi, ALU.mult, ALU.subtract)\
                    .then_inc(Att.alo, 1)

            def add_result(fill, b):
                bank, o = attn_full(fill)
                dve.scalar_tensor_tensor(two(xres, b), o[:, 0:CB * D].rearrange("p (c d) -> p c d", c=CB),
                                         1.0 / PS, two(xres, b), ALU.mult, ALU.add)\
                    .then_inc(Att.done, 1)

            def attn_body(b, u, fill, output, ahead, project2):
                for s in range(16):
                    if ahead:
                        maximum(b + 1, s)
                    if output and s in (4, 5):
                        normalise(fill, b - 1, s - 4)
                    if output and s == 10:
                        attn_lo(fill, b - 1)
                    if output and s == 15:
                        add_result(fill, b - 1)
                if ahead:
                    negate(b + 1)
                if project2:
                    stack(fill, b + 2, u, 0)
                    stack(fill, b + 2, u, 1)
                if ahead:
                    fill.k += 2
                if project2:
                    stack(fill, b + 2, u, 2)
                    stack(fill, b + 2, u, 3)
                    fill.k += 1

            def attn_start(fill):
                for g in range(4):
                    stack(fill, 0, 0, g)
                fill.k += 1
                for s in range(16):
                    maximum(0, s)
                dve.wait_ge(Att.cleared, 1)
                negate(0)
                fill.k += 2
                for g in range(4):
                    stack(fill, 1, 1, g)
                fill.k += 1

            def attn_end(fill, b):
                normalise(fill, b, 0)
                normalise(fill, b, 1)
                attn_lo(fill, b)
                add_result(fill, b)
                dve.wait_ge(Att.done, b + 1)

            norm(0)
            mix()
            norm(1)
            moe_blocks(0)
            dve.wait_ge(moe[0].last, T)
            norm(2)
            attention(dve, attn_start, attn_body, attn_end)
            norm(3)
            moe_blocks(1)


_INS = ['L0_attn_a_x', 'L0_attn_a_W_q', 'L0_attn_a_W_k', 'L0_attn_a_W_v', 'L0_attn_b_qkv_w', 'L0_attn_b_qkv_b',
        'L0_attn_b_out_w', 'L0_attn_b_out_b', 'L0_ffn_gate_w', 'L0_ffn_gate_b', 'L0_ffn_sh_w1', 'L0_ffn_sh_b1',
        'L0_ffn_sh_w2', 'L0_ffn_sh_b2', 'L0_ffn_ew1', 'L0_ffn_eb1', 'L0_ffn_ew2', 'L0_ffn_eb2']


def kernel(**inputs):
    import numpy as np
    import concourse.bacc as bacc
    from concourse.bass_utils import run_bass_kernel_spmd

    nc = bacc.Bacc("TRN2", target_bir_lowering=False, num_devices=1)
    arrays, args = {}, []
    for name in _INS:
        a = np.ascontiguousarray(inputs[name])
        arrays[f"in_{name}"] = a
        args.append(nc.dram_tensor(f"in_{name}", a.shape, mybir.dt.from_np(a.dtype), kind="ExternalInput").ap())
    shape = inputs['L0_attn_a_x'].shape
    args.append(nc.dram_tensor("out_x", shape, F32, kind="ExternalOutput").ap())
    build(nc, *args)
    r = run_bass_kernel_spmd(nc, [arrays], core_ids=[0])
    return r.results[0]["out_x"]
```

```python
from contextlib import ExitStack

import concourse.bass as bass
from concourse import mybir

F32 = mybir.dt.float32
F16 = mybir.dt.float16
I32 = mybir.dt.int32
ALU = mybir.AluOpType
ACT = mybir.ActivationFunctionType
AX_X = mybir.AxisListType.X
ds = bass.ds


def build(nc, x, W_q, W_k, W_v, qkv_w, qkv_b, out_w, out_b, gate_w, gate_b, sh_w1, sh_b1, sh_w2,
          sh_b2, ew1, eb1, ew2, eb2, out):
    NBATCH, SEQ, D = x.shape
    P = 128
    T = NBATCH * SEQ // P
    CB = SEQ // P
    E, _, I = ew1.shape
    NE = E + 1
    CH = I // P
    TOPK = 2
    BT = 2
    BR = BT * P
    NBLK = (TOPK * T * P + E * (BR - 1)) // BR
    LOOPED = (NBLK - 3) // 4
    REST = NBLK - 4 * LOOPED
    NT = NBLK * BT
    NS = T // BT
    NG = 4
    GT, GB = T // NG, NBATCH // NG
    NHEAD, HD = 16, D // 16
    HG = NHEAD // 4
    assert (D, CB, HD) == (128, 2, 8) and REST == 3 and NS % 4 == 0 and GB == 4

    XS = 8.0
    WS = 64.0
    PS = XS * WS
    KX = 16384.0
    RND = 12582912.0

    def mid(n):
        return (n - 1) / (2.0 * n)

    MIDDLE = T * P // 2
    assert MIDDLE <= 2048

    B2 = 0
    BG = B2 + D
    BV = BG + E
    BO = BV + D
    BN = BO + D

    ctx = ExitStack()
    with ctx:
        def sb(name, shape, dt):
            return ctx.enter_context(nc.sbuf_tensor(name, shape, dt))

        def sem(name):
            return ctx.enter_context(nc.semaphore(name))

        xres = sb("xres", [P, T, D], F32)
        xn = sb("xn", [P, T, D], F32)
        hl = sb("hl", [P, T, 2 * D], F16)
        xT = sb("xT", [P, T, 2 * P], F16)
        w1s = sb("w1s", [P, NE, 2, I], F16)
        w2s = sb("w2s", [P, NE, 2, CH * D], F16)
        bt = sb("bt", [P, BN], F16)
        b1T = sb("b1T", [P, NE * CH], F32)
        b2s = sb("b2s", [P, E, D], F32)
        gws = sb("gws", [P, 2, E], F16)
        waT = sb("waT", [P, 2, 3 * D], F16)
        wbT = sb("wbT", [P, 2, 4 * D], F16)
        place16 = sb("place16", [P, 2, 2, 4 * P], F16)
        qkb = sb("qkb", [P, 2], F32)
        kxrow = sb("kxrow", [P, 1], F32)
        scratch = sb("scratch", [P, 4096], F32)
        ident16 = sb("ident16", [P, P], F16)
        ident32 = sb("ident32", [P, P], F32)
        upper16 = sb("upper16", [P, P], F16)
        ones16 = sb("ones16", [P, P], F16)
        cXS = sb("cXS", [P, SEQ], F16)
        zero16 = sb("zero16", [P, P], F16)
        onesC = sb("onesC", [P, P], F32)
        iota_i = sb("iota_i", [P, P], I32)
        iota_f = sb("iota_f", [P, P], F32)
        iota16 = sb("iota16", [P, P], F16)
        ids16 = sb("ids16", [P, T], F16)
        ids_i = sb("ids_i", [P, T], I32)
        part_i = sb("part_i", [P, 4], I32)
        eps = sb("eps", [P, 1], F32)
        cWS = sb("cWS", [P, 1], F32)
        warm = sb("warm", [P, 1], F32)
        reset = sb("reset", [P, E, T], F32)
        stats = sb("stats", [P, T, 6], F32)
        mean = sb("mean", [P, T], F32)
        var = sb("var", [P, T], F32)
        gap = sb("gap", [P, T], F32)
        rstd = sb("rstd", [P, T], F32)
        bnat = sb("bnat", [P, 56], F32)
        bhi = sb("bhi", [P, 56], F16)
        blo = sb("blo", [P, 56], F16)
        ssq = sb("ssq", [P, 2, CB, 2], F32)
        rnorm = sb("rnorm", [P, 2, CB, 2], F32)
        h32 = sb("h32", [P, 2, CH * BR], F32)
        hhi = sb("hhi", [P, 2, CH * BR], F16)
        hlo = sb("hlo", [P, 2, CH * BR], F16)
        xg = sb("xg", [P, 4, 2 * BR], F16)
        yst = sb("yst", [P, 4, BT, D], F32)
        gidx = sb("gidx", [P, 4, BT], I32)
        yidx = sb("yidx", [P, 4, 4], I32)
        prob = sb("prob", [P, T, E], F32)
        rt = [sb(f"rt{i}", [P, T, E], F32) for i in range(3)]
        mask = [sb(f"mask{k}", [P, T, E], F32) for k in range(TOPK)]
        mask16 = sb("mask16", [P, E, T], F16)
        rs = [sb(f"rs{i}", [P, T], F32) for i in range(3)]
        topp = sb("topp", [P, TOPK, T], F32)
        wtop = sb("wtop", [P, TOPK, T], F32)
        cum = sb("cum", [P, E, T], F32)
        slotb = sb("slotb", [P, E, T], F32)
        e8 = [sb(f"e8_{i}", [P, E], F32) for i in range(4)]
        slot = sb("slot", [P, TOPK, T], F32)
        blk = sb("blk", [P, TOPK, T], F32)
        blk16 = sb("blk16", [P, T, TOPK], F16)
        row16 = sb("row16", [P, T, TOPK], F16)
        slot_i = sb("slot_i", [P, TOPK, T], I32)
        bexp = sb("bexp", [P, NBLK, E], F32)
        bexpf = sb("bexpf", [P, NBLK], F32)
        bexp_i = sb("bexp_i", [P, NBLK], I32)
        tok_i = sb("tok_i", [P, NT], I32)
        onerow = sb("onerow", [P, 2, 4, TOPK, P], F16)
        oneblk = sb("oneblk", [P, 2, 4, TOPK, NT], F16)

        ps = ctx.enter_context(nc.psum_tensor("ps", [P, 8, 512], F32))

        rows_dram = [nc.dram_tensor(f"rows{r}", [T * P, 2 * D], F16, kind="Internal").ap()
                     for r in range(2)]
        y_dram = [nc.dram_tensor(f"ysorted{r}", [NT * P, D], F32, kind="Internal").ap()
                  for r in range(2)]

        qst = sb("qst", [P, 2, HG, SEQ], F16)
        kst = sb("kst", [P, 2, HG, SEQ], F16)
        vx = sb("vx", [P, 2, CB, NHEAD, 32], F32)
        mx = sb("mx", [P, CB, NHEAD], F32)
        rsum = sb("rsum", [P, CB, NHEAD], F32)
        prb = scratch[:, :].rearrange("p (n k) -> p n k", n=8)
        qkhi = hhi[:, 0, 0:2 * SEQ].rearrange("p (j n) -> p j n", j=2)
        qklo = hhi[:, 1, 0:2 * SEQ].rearrange("p (j n) -> p j n", j=2)
        negmax = hlo[:, 0, :].rearrange("p (c n) -> p c n", c=CB)
        qst2 = hlo[:, 1, :].rearrange("p (j n) -> p j n", j=HG)
        oT = h32[:, 0, :].rearrange("p (a n) -> p a n", a=2)
        attn = h32[:, 1, 0:CB * D].rearrange("p (c d) -> p c d", c=CB)
        kmask = xn[:, :, :].rearrange("p t d -> p (t d)").bitcast(F16).rearrange(
            "p (u h j n) -> p u h j n", u=2, h=4, j=HG)
        ahi, alo = xg[:, 0, 0:SEQ], xg[:, 1, 0:SEQ]

        def part(at, n, dt=F32):
            return scratch[:, at:at + n].bitcast(dt) if dt != F32 else scratch[:, at:at + n]

        junk = part(0, 4 * D).rearrange("p (n d) -> p n d", n=4)
        qvs = part(4 * D, 8 * D).rearrange("p (u c j d) -> p u c j d", u=2, c=CB, j=2)
        kv = part(12 * D, 4 * D).rearrange("p (u c d) -> p u c d", u=2, c=CB)
        qg = part(16 * D, 4 * D).rearrange("p (u c d) -> p u c d", u=2, c=CB)
        grow = part(0, 8 * D, F16).rearrange("p (u n) -> p u n", u=8)
        gy = part(8 * D, 16 * D).rearrange("p (v u d) -> p v u d", v=4, u=4)

        wstage = h32[:, :, :].rearrange("p u (w n) -> p u w n", w=2)
        wnat = part(20 * D, 7 * D).rearrange("p (i d) -> p i d", d=D)
        b1nat = part(27 * D, D)[0:NE * CH, :]
        gstage = part(28 * D, E)

        xd = x.rearrange("b (c p) d -> p (b c) d", p=P)
        od = out.rearrange("b (c p) d -> p (b c) d", p=P)

        BIASES, col = [], 0
        for at, n, b in ((B2, D, sh_b2), (BV, D, qkv_b[2 * D:3 * D]), (BO, D, out_b), (BG, E, gate_b)):
            rows = min(P, n)
            BIASES.append((at, n, rows, col, b.rearrange("(p c) -> p c", p=rows)))
            col += n // rows
        NBIAS = col

        x_in = [sem(f"x_in{g}") for g in range(NG)]
        wnat_in = sem("wnat_in")
        bias_in = sem("bias_in")
        bias_hi = sem("bias_hi")
        bias_lo = sem("bias_lo")
        bias_rows = sem("bias_rows")
        ewt_in = [sem(f"ewt_in{u}") for u in range(2)]
        ewt_used = sem("ewt_used")
        const_made = sem("const_made")
        pool_step = sem("pool_step")
        wT_turned = sem("wT_turned")
        wT_hi = sem("wT_hi")
        wT_lo = sem("wT_lo")
        gate_split = sem("gate_split")
        slots_made = sem("slots_made")
        rows_found = sem("rows_found")
        qkb_in = sem("qkb_in")
        b2_in = sem("b2_in")
        stored = sem("stored")

        class Ln:
            stats = sem("ln_stats")
            var = sem("ln_var")
            merge = sem("ln_merge")
            std = sem("ln_std")
            rstd = sem("ln_rstd")
            norm = sem("ln_norm")
            hi = sem("ln_hi")
            lo = sem("ln_lo")
            turned = sem("ln_turned")
            xT = sem("ln_xT")
            xTv = sem("ln_xTv")
            added = sem("ln_added")

        class Mix:
            qkv = sem("a_qkv")
            qv = sem("a_qv")
            ssq = sem("a_ssq")
            std = sem("a_std")
            clamped = sem("a_clamped")
            rnorm = sem("a_rnorm")
            kv = sem("a_kv")
            mean = sem("a_mean")
            qg = sem("a_qg")
            done = sem("a_done")

        class Moe:
            def __init__(self, r):
                self.logits = sem(f"m{r}_logits")
                self.shifted = sem(f"m{r}_shifted")
                self.exp = sem(f"m{r}_exp")
                self.step = sem(f"m{r}_step")
                self.mask = sem(f"m{r}_mask")
                self.rank = sem(f"m{r}_rank")
                self.onehot = sem(f"m{r}_onehot")
                self.inblk = sem(f"m{r}_inblk")
                self.numbered = sem(f"m{r}_numbered")
                self.index = sem(f"m{r}_index")
                self.tok = sem(f"m{r}_tok")
                self.up = sem(f"m{r}_up")
                self.gelu = sem(f"m{r}_gelu")
                self.hi = sem(f"m{r}_hi")
                self.split = sem(f"m{r}_split")
                self.down = sem(f"m{r}_down")
                self.y = sem(f"m{r}_y")
                self.rows_out = sem(f"m{r}_rows_out")
                self.gidx = sem(f"m{r}_gidx")
                self.gath = [sem(f"m{r}_gath{u}") for u in range(4)]
                self.turn = sem(f"m{r}_turn")
                self.xg = sem(f"m{r}_xg")
                self.y_out = [sem(f"m{r}_y_out{u}") for u in range(4)]
                self.yidx = sem(f"m{r}_yidx")
                self.ygath = [sem(f"m{r}_ygath{u}") for u in range(4)]
                self.half = sem(f"m{r}_half")
                self.last = sem(f"m{r}_last")

        VBATCH = (NBATCH - 7, NBATCH - 5, NBATCH - 3, NBATCH - 1)
        SBATCH = [b for b in range(NBATCH) if b not in VBATCH]

        def copied(r, b):
            if b in VBATCH:
                return Ln.xTv, len(VBATCH) * r + VBATCH.index(b) + 1
            return Ln.xT, len(SBATCH) * r + SBATCH.index(b) + 1

        moe = [Moe(r) for r in range(2)]

        class Att:
            cleared = sem("t_cleared")
            full = sem("t_full")
            hi = sem("t_hi")
            qk = sem("t_qk")
            stack = sem("t_stack")
            kmask = [[sem(f"t_kmask{u}{h}") for h in range(2)] for u in range(2)]
            v = sem("t_v")
            score = sem("t_score")
            mx = sem("t_mx")
            neghi = sem("t_neghi")
            neg = sem("t_neg")
            q2 = sem("t_q2")
            scoreT = sem("t_scoreT")
            prob = sem("t_prob")
            pv = sem("t_pv")
            oT = sem("t_oT")
            rsum = sem("t_rsum")
            attn = sem("t_attn")
            ahi = sem("t_ahi")
            alo = sem("t_alo")
            done = sem("t_done")

        ORDER = ("back0", "maxima1", "QK", "values", "back1", "K0", "maxima0", "attn", "Q0", "out", "K1", "Q1")
        STACKS = {"K0": (1, 0), "Q0": (0, 0), "K1": (1, 1), "Q1": (0, 1)}

        def place(name):
            return [x for x in ORDER if x in STACKS].index(name)

        def reader(name, b):
            if name in STACKS:
                return Att.stack, 4 * (b + 2) + place(name) + 1
            return {"QK": (Att.qk, b + 3), "values": (Att.v, b + 2),
                    "maxima1": (Att.q2, 2 * b + 2), "maxima0": (Att.q2, 2 * b + 3),
                    "back0": (Att.attn, 2 * b - 1), "back1": (Att.attn, 2 * b), "attn": (Att.alo, b),
                    "out": (Att.done, b)}[name]

        class Body:

            def __init__(self, b, i, at, names, before):
                self.i, self.at, self.names = i, at, names
                self.readers = before + [reader(x, b) for x in names]

            def bank(self, name):
                return (self.at + self.names.index(name)) % 2

            def filled(self, name):
                return self.i * 2 * len(ORDER) + self.at + self.names.index(name) + 1

            def free(self, name):
                return self.readers[self.names.index(name)]

        LAST = NBATCH - 1

        def attention(eng, start, body, end):
            def names(output, ahead, project):
                skip = ((() if output else ("back0", "back1", "attn", "out")) + (() if ahead else ("values", "maxima0"))
                        + (() if project else ("QK", *STACKS)))
                return [x for x in ORDER if x not in skip]

            def last_two(b, names):
                return [reader(x, b) for x in names[-2:]]

            stacks = [x for x in ORDER if x == "QK" or x in STACKS]
            full, first = names(True, True, True), names(False, True, True)
            short, final = names(True, True, False), names(True, False, False)
            second = ["values"] + stacks[:-1] + ["maxima0", "Q1"]
            start(Body(-2, 0, 0, stacks, [None, None]),
                  Body(-1, 0, len(stacks), second, last_two(-2, stacks)))
            at = 2 * len(stacks) + 2
            body(0, 0, Body(0, 0, at, first, last_two(-1, second)), False, True, True)
            at += len(first)
            with eng.Fori(0, (NBATCH - 4) // 2) as i:
                for k in range(2):
                    b = 2 * i + 1 + k
                    body(b, 1 - k, Body(b, i, at + k * len(full), full, last_two(b - 1, full)), True, True, True)
            at += (NBATCH - 4) * len(full)
            for b, kinds, before in ((LAST - 2, full, full), (LAST - 1, short, full), (LAST, final, short)):
                body(b, b % 2, Body(b, 0, at, kinds, last_two(b - 1, before)), True, b < LAST, b < LAST - 1)
                at += len(kinds)
            end(Body(LAST + 1, 0, at, ["back0", "back1", "attn", "out"], last_two(LAST, final)), LAST)

        block = ctx.enter_context(nc.Block())

        HB = [ps[:, 2 * u:2 * u + 2, :].rearrange("p b n -> p (b n)") for u in range(2)]
        YB = [ps[:, 4 + u, 0:BT * D].rearrange("p (k d) -> p k d", k=BT) for u in range(2)]
        TB = [ps[:, 6 + u, :].bitcast(F16) for u in range(2)]
        LB = [ps[:, 4 + u, :].bitcast(F16) for u in range(4)]
        IDX = ps[:, 7, 0:NT]
        GATE = ps[:, 0, 0:T * E]
        RANK = ps[:, 1, 0:E * T]
        TOT = ps[:, 1, E * T:2 * E * T]

        def group(ap, g):
            return ap[:, ds(GT * g, GT), :]

        def two(ap, t):
            return ap[:, ds(2 * t, 2), :]

        @block.sync
        def _(sp):
            for g in range(NG):
                sp.dma_start(group(xres, g), group(xd, g)).then_inc(x_in[g], 16)
            for i, w in enumerate((W_q, W_k, W_v)):
                sp.dma_start(wnat[:, i, :], w).then_inc(wnat_in, 16)
            sp.dma_start(wnat[:, 3:6, :], qkv_w.rearrange("(m p) d -> p m d", p=P)).then_inc(wnat_in, 16)
            sp.dma_start(wnat[:, 6, :], out_w).then_inc(wnat_in, 16)
            sp.dma_start(gstage, gate_w).then_inc(wnat_in, 16)
            sp.dma_start(b1nat[0:E * CH, :], eb1.rearrange("e (c p) -> (e c) p", p=P)).then_inc(wnat_in, 16)
            sp.dma_start(b1nat[E * CH:NE * CH, :], sh_b1.rearrange("(c p) -> c p", p=P)).then_inc(wnat_in, 16)
            for at, n, rows, c, b in BIASES:
                sp.dma_start(bnat[0:rows, c:c + n // rows], b).then_inc(bias_in, 16)
            for j in range(2):
                sp.dma_start(qkb[:, j:j + 1], qkv_b[j * D:(j + 1) * D].rearrange("(p c) -> p c", p=P))\
                    .then_inc(qkb_in, 16)

            sp.dma_start(b2s[:, :, :], eb2.unsqueeze(0).to_broadcast([P, E, D])).then_inc(b2_in, 16)

            def expert(e, u, w1, w2):
                sp.dma_start(wstage[:, u, 0, :], w1).then_inc(ewt_in[u], 16)
                sp.dma_start(wstage[:, u, 1, :].rearrange("p (c d) -> p c d", c=CH), w2).then_inc(ewt_in[u], 16)

            def one(w, e):
                return w[ds(e, 1), :, :].rearrange("a p n -> (a p) n")

            def two_of(e):
                return one(ew1, e), one(ew2, e).rearrange("(c p) d -> p c d", p=P)

            for u in range(2):
                expert(u, u, *two_of(u))
            with sp.Fori(0, (E - 2) // 2) as i:
                for u in range(2):
                    sp.wait_ge(ewt_used, 2 * i + u + 1)
                    expert(0, u, *two_of(2 * i + 2 + u))
            sp.wait_ge(bias_lo, 1)
            for at, n, rows, c, b in BIASES:
                for r, half in ((0, bhi), (1, blo)):
                    sp.dma_start(bt[r:r + 1, at:at + n], half[0:rows, c:c + n // rows]).then_inc(bias_rows, 16)
            sp.wait_ge(ewt_used, E - 1)
            expert(E, 0, sh_w1, sh_w2.rearrange("(c p) d -> p c d", p=P))

            def moe_stores(r):
                m, l, first = moe[r], Ln, (2 * r + 1) * NG
                rows = rows_dram[r].rearrange("(t p) n -> p t n", p=P)
                for g in range(NG):
                    sp.wait_ge(l.lo, first + g + 1)
                    sp.dma_start(group(rows, g), group(hl, g)).then_inc(m.rows_out, 16)
                ys = y_dram[r].rearrange("(n k p) d -> p n k d", p=P, k=BT)

                def store(n, u):
                    sp.wait_ge(m.y, 2 + n + 1)
                    sp.dma_start(ys[:, ds(n, 1), :, :], yst[:, u:u + 1, :, :]).then_inc(m.y_out[u], 16)

                with sp.Fori(0, LOOPED) as i:
                    for u in range(4):
                        store(4 * i + u, u)
                for u in range(REST):
                    store(4 * LOOPED + u, u)

            def attn_mask(b, u):
                for jp in range(2):
                    sp.wait_ge(Att.stack, 4 * b + place(("K0", "Q1")[jp]) + 1)
                    for hh in range(4):
                        rows, j = slice(32 * hh, 32 * hh + 32), slice(2 * jp, 2 * jp + 2)
                        sp.dma_start(kmask[rows, u, hh, j, :], kst[rows, u, j, :]).then_inc(Att.kmask[u][jp], 16)

            moe_stores(0)
            sp.wait_ge(Att.cleared, NG)
            with sp.Fori(0, NBATCH // 2) as i:
                for u in range(2):
                    attn_mask(2 * i + u, u)
            moe_stores(1)
            for g in range(NG):
                sp.wait_ge(moe[1].last, GT * (g + 1))
                sp.dma_start(group(od, g), group(xres, g)).then_inc(stored, 16)
            sp.wait_ge(stored, 16 * NG)

        @block.gpsimd
        def _(pool):
            steps = [0]

            def link(ins):
                steps[0] += 1
                ins.then_inc(pool_step, 1)
                pool.wait_ge(pool_step, steps[0])

            pool.iota(part_i[:, 0:1], pattern=[[0, 1]], base=0, channel_multiplier=1)
            pool.iota(iota_i[:, :], pattern=[[1, P]], base=0, channel_multiplier=0)
            pool.iota(ids_i[:, :], pattern=[[P, T]], base=-MIDDLE, channel_multiplier=1)
            pool.memset(ident16[:, :], 0.0)
            pool.memset(ident32[:, :], 0.0)
            pool.memset(upper16[:, :], 1.0)
            pool.memset(reset[:, :, :], 1.0)
            pool.memset(onesC[:, :], 1.0 / (SEQ * PS))
            pool.memset(ones16[:, :], 1.0)
            pool.memset(cXS[:, :], XS)
            pool.memset(zero16[:, :], 0.0)
            pool.memset(cWS[:, :], WS)
            link(pool.memset(eps[:, :], 1e-5))
            for m in (ident16, ident32):
                pool.affine_select(out=m[:, :], in_=m[:, :], compare_op=ALU.not_equal, fill=1.0,
                                   base=0, pattern=[[-1, P]], channel_multiplier=1)
            pool.affine_select(out=upper16[:, :], in_=upper16[:, :], compare_op=ALU.is_gt, fill=0.0,
                               base=0, pattern=[[1, P]], channel_multiplier=-1)
            pool.tensor_copy(iota_f[:, :], iota_i[:, :])
            pool.tensor_copy(iota16[:, :], iota_i[:, :])
            pool.tensor_copy(ids16[:, :], ids_i[:, :])
            pool.memset(reset[:, :, 0:1], 0.0).then_inc(const_made, 1)
            pool.memset(bt[:, :], 0.0).then_inc(const_made, 1)

            def half(w, e, h):
                return w[:, ds(e, 1), h, :]

            def split_expert(e, u, loads):
                before = steps[0] + 4 * e
                pool.wait_ge(ewt_in[u], loads)
                for n, w in ((1, 0), (2, 1)):
                    pool.tensor_tensor(wstage[:, u, w, :], wstage[:, u, w, :], cWS[:, 0:1].to_broadcast([P, I]),
                                       ALU.mult).then_inc(pool_step, 1)
                for n, w, dst in ((1, 0, w1s), (2, 1, w2s)):
                    pool.wait_ge(pool_step, before + n)
                    pool.tensor_copy(half(dst, e, 0), wstage[:, u, w:w + 1, :]).then_inc(pool_step, 1)
                pool.wait_ge(pool_step, before + 4)
                pool.tensor_tensor(half(w1s, e, 1), wstage[:, u, 0:1, :], half(w1s, e, 0), ALU.subtract)
                pool.tensor_tensor(half(w2s, e, 1), wstage[:, u, 1:2, :], half(w2s, e, 0), ALU.subtract)\
                    .then_inc(ewt_used, 1)

            with pool.Fori(0, E // 2) as i:
                for u in range(2):
                    split_expert(2 * i + u, u, 32 * (i + 1))
            split_expert(E, 0, 32 * (E // 2 + 1))
            steps[0] += 4 * NE
            pool.memset(place16[:, :, :, :], 0.0)
            link(pool.memset(vx[:, :, :, :, :], 0.0))
            pool.memset(vx[:, :, :, :, HD:HD + 1], 1.0)
            for j, halves in ((0, (0, 0, 1)), (1, (0, 1, 0))):
                for rep, h in enumerate(halves):
                    last = pool.tensor_copy(
                        place16[:, j, h, :].rearrange("p (h s) -> p h s", s=32)[:, :, rep * HD:(rep + 1) * HD],
                        ident16[:, :].rearrange("p (h d) -> p h d", d=HD))
            last.then_inc(slots_made, 1)

            def moe_rows(r):
                m, l, first = moe[r], Ln, (2 * r + 1) * NG
                for g in range(NG):
                    pool.wait_ge(l.hi, first + g + 1)
                    pool.tensor_tensor(group(xres, g), group(xres, g), group(xn, g), ALU.add).then_inc(l.added, 1)
                for u in range(4):
                    pool.sem_inc(m.y_out[u], 16)

                with pool.Fori(0, T // 8) as i:
                    for u in range(2):
                        g = 2 * i + u
                        pool.wait_ge(m.inblk, g + 1)
                        ids = ids16[:, ds(4 * g, 4)].unsqueeze(2).unsqueeze(2).to_broadcast([P, 4, TOPK, NT])
                        pool.tensor_tensor(oneblk[:, u, :, :, :], oneblk[:, u, :, :, :], ids, ALU.mult)\
                            .then_inc(m.numbered, 1)
                pool.wait_ge(m.tok, 1)

                def fetches(groups, numbers, copied, used, fetch):
                    def step(f, v):
                        if not (isinstance(f, int) and f < 3):
                            used(f - 3)
                        pool.wait_ge(copied, f + 1)
                        if not (isinstance(f, int) and f + 1 == groups):
                            numbers(f + 1, (v + 1) % 4)
                        fetch(v)

                    numbers(0, 0)
                    for f in range(3):
                        step(f, f)
                    passes = (groups - 4) // 4
                    with pool.Fori(0, passes) as i:
                        for v in range(4):
                            step(4 * i + v + 3, (v + 3) % 4)
                    for f in range(4 * passes + 3, groups):
                        step(f, f % 4)

                def row_numbers(f, v):
                    pool.tensor_copy(gidx[:, v, :], tok_i[:, ds(BT * f, BT)]).then_inc(m.gidx, 1)

                def rows_used(f):
                    pool.wait_ge(m.turn, f + 1)

                def fetch_rows(v):
                    for t in range(BT):
                        pool.indirect_dma_start(grow[:, BT * v + t, :], None, rows_dram[r],
                                                bass.IndirectOffsetOnAxis(ap=gidx[:, v, t:t + 1], axis=0))\
                            .then_inc(m.gath[v], 16)

                pool.wait_ge(m.rows_out, 16 * NG)
                fetches(NBLK, row_numbers, m.gidx, rows_used, fetch_rows)

                def y_numbers(f, v):
                    pool.tensor_copy(yidx[:, v, :].rearrange("p (c k) -> p k c", k=TOPK),
                                     slot_i[:, :, ds(2 * f, 2)]).then_inc(m.yidx, 1)

                def y_used(f):
                    pool.wait_ge(m.last, 2 * f + 2)

                def fetch_y(v):
                    for u in range(4):
                        pool.indirect_dma_start(gy[:, v, u, :], None, y_dram[r],
                                                bass.IndirectOffsetOnAxis(ap=yidx[:, v, u:u + 1], axis=0))\
                            .then_inc(m.ygath[v], 16)

                for u in range(4):
                    pool.wait_ge(m.y_out[u], 16 * (len(range(u, NBLK, 4)) + 1))
                fetches(T // 2, y_numbers, m.yidx, y_used, fetch_y)

            moe_rows(0)
            pool.wait_ge(moe[0].last, T)
            pool.memset(negmax, 0.0)
            for g in range(NG):
                pool.wait_ge(Ln.lo, 2 * NG + g + 1)
                pool.memset(kmask[:, g // 2, g % 2 * 2:g % 2 * 2 + 2, :, :], 0.0).then_inc(Att.cleared, 1)
            moe_rows(1)

        @block.tensor
        def _(pe):
            def mm(o, a, b, start, stop):
                return pe.matmul(o, a, b, start=start, stop=stop)

            pe.wait_ge(const_made, 1)
            pe.wait_ge(wnat_in, 8 * 16)
            for i in range(7):
                pe.transpose(ps[:, i // 4, P * (i % 4):P * (i % 4 + 1)], wnat[:, i, :], ident32[:, :])
            pe.transpose(ps[:, 1, 3 * P:3 * P + NE * CH], b1nat, ident32[0:NE * CH, 0:NE * CH]).then_inc(wT_turned, 1)

            def norm_turns(r, gate):
                l, first = Ln, r * NBATCH

                def turn(b, u, g):
                    pe.wait_ge(l.lo, NG * r + g + 1)
                    for c in range(CB):
                        for h in range(2):
                            o = c * 2 * P + h * P
                            last = pe.transpose(LB[u][:, o:o + P],
                                                hl[:, 2 * b + c, h * D:(h + 1) * D], ident16[:, :])
                    last.then_inc(l.turned, 1)

                def logits(b):
                    if not gate:
                        return
                    for c in range(CB):
                        t = 2 * b + c
                        o = GATE[:, E * t:E * (t + 1)]
                        hi, lo = xT[:, t, 0:P], xT[:, t, P:2 * P]
                        mm(o, hi, gws[:, 0, :], True, False)
                        mm(o, hi, gws[:, 1, :], False, False)
                        mm(o, lo, gws[:, 0, :], False, False)
                        last = mm(o, cXS[:, 0:P], bt[:, BG:BG + E], False, True)
                    return last

                for b in range(GB):
                    turn(b, b, 0)
                for b in range(NBATCH):
                    if gate or b + GB < NBATCH:
                        pe.wait_ge(*copied(r, b))
                    if b + GB < NBATCH:
                        turn(b + GB, b % GB, b // GB + 1)
                    last = logits(b)
                if gate:
                    last.then_inc(moe[r // 2].logits, 1)

            def mix():
                pe.wait_ge(wT_lo, 1)
                for b in NBATCH - 2, NBATCH - 1:
                    pe.wait_ge(*copied(0, b))

                def project(b, u):
                    for c in range(CB):
                        t = 2 * b + c
                        o = ps[:, 2 * u + c, 0:3 * D]
                        hi, lo = xT[:, ds(t, 1), 0:P], xT[:, ds(t, 1), P:2 * P]
                        mm(o, hi, waT[:, 0, :], True, False)
                        mm(o, hi, waT[:, 1, :], False, False)
                        last = mm(o, lo, waT[:, 0, :], False, True)
                    last.then_inc(Mix.qkv, 1)

                def mean(b, u):
                    pe.wait_ge(Mix.kv, b + 1)
                    if not (isinstance(b, int) and b < 2):
                        pe.wait_ge(Mix.qg, b - 1)
                    mm(ps[:, 4 + u, 0:D], onesC[:, :], kv[:, u, 0, :], True, False)
                    mm(ps[:, 4 + u, 0:D], onesC[:, :], kv[:, u, 1, :], False, True).then_inc(Mix.mean, 1)

                project(0, 0)
                project(1, 1)
                for b in range(2):
                    mean(b, b)
                    project(b + 2, b)
                with pe.Fori(1, NBATCH // 2 - 1) as i:
                    for u in range(2):
                        mean(2 * i + u, u)
                        project(2 * i + u + 2, u)
                mean(NBATCH - 2, 0)
                mean(NBATCH - 1, 1)

            def moe_blocks(r):
                m = moe[r]
                pe.wait_ge(m.mask, 1)
                flat = mask16[:, :, :].rearrange("p e t -> p (e t)")
                mm(RANK, upper16[:, :], flat, True, True)
                mm(TOT, ones16[:, :], flat, True, True).then_inc(m.rank, 1)

                def up(n, u, e, hi, lo):
                    if not (isinstance(n, int) and n < 2):
                        pe.wait_ge(m.gelu, n - 1)
                    for c in range(CH):
                        o = HB[u % 2][:, c * BR:(c + 1) * BR]
                        f = slice(c * P, (c + 1) * P)
                        w = w1s[:, ds(e, 1), 0, f]
                        mm(o, w, hi, True, False)
                        mm(o, w, lo, False, False)
                        last = mm(o, w1s[:, ds(e, 1), 1, f], hi, False, True)
                    last.then_inc(m.up, 1)

                def down(n, u, e, shared=False):
                    pe.wait_ge(m.split, n + 1)
                    pe.wait_ge(m.y, n + 1)
                    for c in range(CH):
                        f = slice(c * D, (c + 1) * D)
                        whi, wlo = w2s[:, ds(e, 1), 0, f], w2s[:, ds(e, 1), 1, f]
                        for k, (h, w) in enumerate(((hhi, whi), (hlo, whi), (hhi, wlo))):
                            for t in range(BT):
                                at = c * BR + t * P
                                last = pe.matmul(YB[u % 2][:, t, :], h[:, u % 2, at:at + P], w,
                                                 start=(c, k, t) == (0, 0, 0),
                                                 stop=not shared and (c, k, t) == (CH - 1, 2, BT - 1),
                                                 skip_group_check=True)
                    if shared:
                        for t in range(BT):
                            last = pe.matmul(YB[u % 2][:, t, :], cXS[:, 0:P], bt[:, B2:B2 + D],
                                             start=False, stop=t == BT - 1, skip_group_check=True)
                    last.then_inc(m.down, 1)

                def number(g, u):
                    pe.wait_ge(m.onehot, g + 1)
                    pe.wait_ge(m.numbered, g + 1)
                    for c in range(4):
                        for k in range(TOPK):
                            last = mm(IDX, onerow[:, u, c, k, :], oneblk[:, u, c, k, :], False, False)
                    last.then_inc(m.index, 1)

                mm(IDX, zero16[:, :], zero16[:, 0:NT], True, False)
                with pe.Fori(0, T // 8) as i:
                    for u in range(2):
                        number(2 * i + u, u)
                mm(IDX, zero16[:, :], zero16[:, 0:NT], False, True).then_inc(m.index, 1)

                def up_shared(n, v):
                    up(NBLK + n, NBLK + v, E, two(xT, n)[:, :, 0:P], two(xT, n)[:, :, P:2 * P])

                def experts(n, k):
                    return nc.values_load_multi_w_load_instructions(
                        bexp_i[0:1, ds(n, k)], engines=[mybir.EngineType.PE], min_val=0, max_val=E - 1,
                        skip_runtime_bounds_check_because="VectorE kept it within 0 and E - 1")[1]

                def turn(n, u, i):
                    pe.wait_ge(m.gath[u], 16 * BT * (i + 1))
                    for h in range(2):
                        for t in range(BT):
                            o = h * BR + t * P
                            last = pe.transpose(TB[u % 2][:, o:o + P],
                                                grow[:, BT * u + t, h * D:(h + 1) * D], ident16[:, :])
                    last.then_inc(m.turn, 1)

                def up_routed(n, u, e):
                    pe.wait_ge(m.xg, n + 1)
                    up(n, u, e, xg[:, u, 0:BR], xg[:, u, BR:2 * BR])

                pe.wait_ge(ewt_used, NE)
                turn(0, 0, 0)
                turn(1, 1, 0)
                es = experts(0, 2)
                up_routed(0, 0, es[0])
                turn(2, 2, 0)
                up_routed(1, 1, es[1])
                with pe.Fori(0, LOOPED) as i:
                    es = experts(4 * i, 6)
                    for u in range(4):
                        n = 4 * i + u
                        up_routed(n + 2, (u + 2) % 4, es[u + 2])
                        turn(n + 3, (u + 3) % 4, i + (u + 3) // 4)
                        down(n, u, es[u])
                es = experts(NBLK - 3, 3)
                for u in range(3):
                    if u < 1:
                        up_routed(NBLK - 1, 2, es[2])
                    else:
                        up_shared(u - 1, u - 1)
                    down(NBLK - 3 + u, u, es[u])
                with pe.Fori(0, NS // 2 - 1) as i:
                    for u in range(2):
                        up_shared(2 * i + u + 2, u)
                        down(NBLK + 2 * i + u, NBLK + u, E, True)
                for u in range(2):
                    down(NBLK + NS - 2 + u, NBLK + u, E, True)

            def attn_fill(body, name):
                before = body.free(name)
                if before is not None:
                    pe.wait_ge(*before)
                return ps[:, 6 + body.bank(name), :]

            def project(body, b):
                o = attn_fill(body, "QK")
                hi, lo = two(xT, b)[:, :, 0:P], two(xT, b)[:, :, P:2 * P]
                for j in range(2):
                    on, f = o[:, j * SEQ:(j + 1) * SEQ], slice(j * D, (j + 1) * D)
                    mm(on, wbT[:, 0, f], hi, True, False)
                    mm(on, wbT[:, 0, f], lo, False, False)
                    last = mm(on, wbT[:, 1, f], hi, False, True)
                last.then_inc(Att.full, 1)

            def stack(body, name, b):
                o = attn_fill(body, name)
                if name == "K0":
                    pe.wait_ge(Att.qk, b + 1)
                j, half = STACKS[name]
                for n in range(2):
                    on, f = o[:, n * SEQ:(n + 1) * SEQ], slice((2 * half + n) * P, (2 * half + n + 1) * P)
                    mm(on, place16[:, j, 0, f], qkhi[:, j, :], True, False)
                    last = mm(on, place16[:, j, 1, f], qklo[:, j, :], False, True)
                last.then_inc(Att.full, 1)

            def values(body, b):
                o = attn_fill(body, "values")
                for c in range(CB):
                    t = 2 * b + c
                    hi, lo = xT[:, ds(t, 1), 0:P], xT[:, ds(t, 1), P:2 * P]
                    on = o[:, c * D:(c + 1) * D]
                    mm(on, hi, wbT[:, 0, 2 * D:3 * D], True, False)
                    mm(on, hi, wbT[:, 1, 2 * D:3 * D], False, False)
                    mm(on, lo, wbT[:, 0, 2 * D:3 * D], False, False)
                    last = mm(on, cXS[:, 0:P], bt[:, BV:BV + D], False, True)
                last.then_inc(Att.full, 1)

            def score(b, u, s):
                jp, c, hh = s // 8, s // 4 % 2, s % 4
                if s % 8 == 0:
                    pe.wait_ge(Att.kmask[u][jp], 32 * (b - u) + 64)
                    pe.wait_ge(Att.stack, 4 * b + place(f"Q{jp}") + 1)
                if not (isinstance(b, int) and 16 * b + s < 2):
                    pe.wait_ge(Att.mx, 16 * b + s - 1)
                for n in range(2):
                    j = 2 * jp + n
                    last = mm(ps[:, 2 + s % 2, n * SEQ:(n + 1) * SEQ], qst[:, u, j, c * P:(c + 1) * P],
                              kmask[:, u, hh, j, :], True, True)
                last.then_inc(Att.score, 1)

            def maxima(body, b, jp):
                o = attn_fill(body, f"maxima{jp}")
                pe.wait_ge(Att.neg, 2 * b + jp + 1)
                for n in range(2):
                    j = 2 * jp + n
                    on = o[:, n * SEQ:(n + 1) * SEQ]
                    for c in range(CB):
                        last = mm(on[:, c * P:(c + 1) * P], negmax[:, c, j * P:(j + 1) * P], ident16[:, :], True, True)
                last.then_inc(Att.full, 1)

            def scoreT(b, u, s):
                jp, kc, hh = s // 8, s // 4 % 2, s % 4
                if s % 8 == 0:
                    pe.wait_ge(Att.q2, 2 * b + jp + 1)
                if not (isinstance(b, int) and 16 * b + s < 2):
                    pe.wait_ge(Att.prob, 16 * b + s - 1)
                for n in range(2):
                    j = 2 * jp + n
                    last = mm(ps[:, s % 2, n * SEQ:(n + 1) * SEQ], kmask[:, u, hh, j, kc * P:(kc + 1) * P],
                              qst2[:, j, :], True, True)
                last.then_inc(Att.scoreT, 1)

            def weigh(b, u, g, n):
                jp, kc = g // 2, g % 2
                if n == 0:
                    pe.wait_ge(Att.prob, 16 * b + 4 * g + 4)
                if (g, n) == (0, 0):
                    pe.wait_ge(Att.v, b + 1)
                if kc == 0 and n == 0 and not (isinstance(b, int) and b == 0):
                    pe.wait_ge(Att.oT, 2 * b - 1 + jp)
                for hh in range(4):
                    last = pe.matmul(ps[32 * hh:32 * hh + 32, 4 + jp, n * SEQ:(n + 1) * SEQ],
                                     vx[:, u, kc, 4 * (2 * jp + n) + hh, :],
                                     prb[:, (4 * g + hh) % 8, n * SEQ:(n + 1) * SEQ],
                                     start=kc == 0 and n == 0, stop=kc == 1 and n == 1,
                                     skip_group_check=True)
                if n == 1:
                    last.then_inc(Att.pv, 1)

            def turn_back(body, b, jp):
                o = attn_fill(body, f"back{jp}")
                pe.wait_ge(Att.oT, 2 * b + jp + 1)
                for c in range(CB):
                    for n in range(2):
                        last = pe.transpose(o[:, c * SEQ + n * P:c * SEQ + (n + 1) * P],
                                            oT[:, jp, n * SEQ + c * P:n * SEQ + (c + 1) * P], ident32[:, :])
                last.then_inc(Att.full, 1)

            def turn_attn(body, b):
                o = attn_fill(body, "attn")
                pe.wait_ge(Att.attn, 2 * b + 2)
                for c in range(CB):
                    last = pe.transpose(o[:, c * P:(c + 1) * P], attn[:, c, :], ident32[:, :])
                last.then_inc(Att.full, 1)

            def out_project(body, b):
                o = attn_fill(body, "out")
                pe.wait_ge(Att.alo, b + 1)
                for c in range(CB):
                    f = slice(c * P, (c + 1) * P)
                    on = o[:, c * D:(c + 1) * D]
                    mm(on, ahi[:, f], wbT[:, 0, 3 * D:4 * D], True, False)
                    mm(on, ahi[:, f], wbT[:, 1, 3 * D:4 * D], False, False)
                    mm(on, alo[:, f], wbT[:, 0, 3 * D:4 * D], False, False)
                    last = mm(on, cXS[:, 0:P], bt[:, BO:BO + D], False, True)
                last.then_inc(Att.full, 1)

            def attn_body(b, u, body, output, ahead, project2):
                for s in range(16):
                    if ahead:
                        score(b + 1, 1 - u, s)
                    scoreT(b, u, s)
                    if output and s in (1, 2):
                        weigh(b - 1, 1 - u, 3, s - 1)
                    if s == 1 and output:
                        turn_back(body, b - 1, 0)
                    if s == 3:
                        maxima(body, b, 1)
                    if s == 4 and project2:
                        project(body, b + 2)
                    if s >= 5 and s % 2 == 1:
                        weigh(b, u, (s - 5) // 4, (s - 5) // 2 % 2)
                    if s == 5 and ahead:
                        values(body, b + 1)
                    if s == 7 and output:
                        turn_back(body, b - 1, 1)
                    if s == 8 and project2:
                        stack(body, "K0", b + 2)
                    if s == 9 and ahead:
                        maxima(body, b + 1, 0)
                    if s == 10 and output:
                        turn_attn(body, b - 1)
                    if s == 12 and project2:
                        stack(body, "Q0", b + 2)
                    if s == 13 and output:
                        out_project(body, b - 1)
                    if s == 14 and project2:
                        stack(body, "K1", b + 2)
                    if s == 15 and project2:
                        stack(body, "Q1", b + 2)

            def attn_start(body, body1):
                project(body, 0)
                for name in STACKS:
                    stack(body, name, 0)
                values(body1, 0)
                project(body1, 1)
                for s in range(16):
                    score(0, 0, s)
                    if s in (4, 6, 8):
                        stack(body1, ("K0", "Q0", "K1")[s // 2 - 2], 1)
                    if s == 12:
                        maxima(body1, 0, 0)
                    if s == 14:
                        stack(body1, "Q1", 1)

            def attn_end(body, b):
                weigh(b, b % 2, 3, 0)
                weigh(b, b % 2, 3, 1)
                turn_back(body, b, 0)
                turn_back(body, b, 1)
                turn_attn(body, b)
                out_project(body, b)

            norm_turns(0, False)
            mix()
            pe.wait_ge(bias_rows, 2 * 16 * len(BIASES))
            norm_turns(1, True)
            moe_blocks(0)
            norm_turns(2, False)
            pe.wait_ge(slots_made, 1)
            for b in NBATCH - 2, NBATCH - 1:
                pe.wait_ge(*copied(2, b))
            attention(pe, attn_start, attn_body, attn_end)
            norm_turns(3, True)
            moe_blocks(1)

        @block.scalar
        def _(act):
            def std(r):
                l, first = Ln, r * NBATCH
                act.wait_ge(l.var, r + 1)
                act.activation(rstd[:, :], var[:, :], ACT.Sqrt, bias=eps[:, 0:1], scale=1.0 / D).then_inc(l.std, 1)

            def norm(r):
                l, first = Ln, r * NBATCH

                def hi(g):
                    act.wait_ge(l.norm, NG * r + g + 1)
                    act.activation(group(hl, g)[:, :, 0:D], group(xn, g), ACT.Copy, scale=XS).then_inc(l.hi, 1)

                def copy_out(b):
                    act.wait_ge(l.turned, first + b + 1)
                    act.activation(two(xT, b), LB[b % GB][:, 0:4 * P].rearrange("p (c f) -> p c f", c=CB),
                                   ACT.Copy).then_inc(l.xT, 1)

                for g in range(NG):
                    hi(g)
                    if 0 < g < NG - 1:
                        for b in range(GB * (g - 1), GB * g):
                            copy_out(b)
                for b in SBATCH[2 * GB:]:
                    copy_out(b)

            def mix():
                def norms(b, u):
                    act.wait_ge(Mix.qkv, b + 1)
                    for c in range(CB):
                        for j in range(2):
                            last = act.activation(junk[:, 2 * c + j, :], ps[:, 2 * u + c, j * D:(j + 1) * D],
                                                  ACT.Square, accum_out=ssq[:, u, c, j:j + 1])
                    last.then_inc(Mix.ssq, 1)
                    act.wait_ge(Mix.ssq, b + 1)
                    if not (isinstance(b, int) and b < 2):
                        act.wait_ge(Mix.qg, b - 1)
                    act.activation(rnorm[:, u, :, :], ssq[:, u, :, :], ACT.Sqrt).then_inc(Mix.std, 1)

                    bank = ps[:, 2 * u:2 * u + 2, 0:4 * D].rearrange("p c (j d) -> p c j d", d=D)
                    act.activation(qvs[:, u, :, :, :], bank[:, :, 0:3:2, :], ACT.Copy).then_inc(Mix.qv, 1)

                norms(0, 0)
                norms(1, 1)
                with act.Fori(1, NBATCH // 2) as i:
                    for u in range(2):
                        norms(2 * i + u, u)

            def moe_blocks(r):
                m = moe[r]
                act.wait_ge(m.shifted, 1)
                act.activation(prob[:, :, :], prob[:, :, :], ACT.Exp, scale=1.0 / PS).then_inc(m.exp, 1)

                def gelu(n, u, e):
                    act.wait_ge(m.up, n + 1)
                    if not (isinstance(n, int) and n < 2):
                        act.wait_ge(m.split, n - 1)
                    for c in range(CH):
                        f = slice(c * BR, (c + 1) * BR)
                        last = act.activation(h32[:, u % 2, f], HB[u % 2][:, f], ACT.Gelu_apprx_tanh,
                                              bias=b1T[:, ds(e * CH + c, 1)], scale=1.0 / PS)
                    last.then_inc(m.gelu, 1)

                def experts(n, k):
                    return nc.values_load_multi_w_load_instructions(
                        bexp_i[0:1, ds(n, k)], engines=[mybir.EngineType.Activation], min_val=0, max_val=E - 1,
                        skip_runtime_bounds_check_because="VectorE kept it within 0 and E - 1")[1]

                def copy_out(n, u):
                    act.wait_ge(m.turn, n + 1)
                    act.activation(xg[:, u, :], TB[u % 2][:, 0:2 * BR], ACT.Copy).then_inc(m.xg, 1)

                act.activation(warm[:, :], eps[:, 0:1], ACT.Gelu_apprx_tanh)
                copy_out(0, 0)
                copy_out(1, 1)
                es = experts(0, 2)
                gelu(0, 0, es[0])
                copy_out(2, 2)
                gelu(1, 1, es[1])
                with act.Fori(0, LOOPED) as i:
                    es = experts(4 * i + 2, 4)
                    for u in range(4):
                        n = 4 * i + u
                        copy_out(n + 3, (u + 3) % 4)
                        gelu(n + 2, u, es[u])
                gelu(NBLK - 1, 2, experts(NBLK - 1, 1)[0])
                with act.Fori(0, NS // 2) as i:
                    for u in range(2):
                        gelu(NBLK + 2 * i + u, NBLK + u, E)

            def attn_full(body, name):
                act.wait_ge(Att.full, body.filled(name))
                return body.bank(name), ps[:, 6 + body.bank(name), :]

            def qk_hi(body):
                _, o = attn_full(body, "QK")
                for j in range(2):
                    last = act.activation(qkhi[:, j, :], o[:, j * SEQ:(j + 1) * SEQ], ACT.Identity,
                                          bias=qkb[:, j:j + 1])
                last.then_inc(Att.hi, 1)

            def stack(body, name, u):
                _, o = attn_full(body, name)
                j, half = STACKS[name]
                dst = (qst, kst)[j][:, u, 2 * half:2 * half + 2, :].rearrange("p j n -> p (j n)")
                if j:
                    act.activation(dst, o, ACT.Identity, bias=kxrow[:, 0:1]).then_inc(Att.stack, 1)
                else:
                    act.activation(dst, o, ACT.Copy).then_inc(Att.stack, 1)

            def values(body, u):
                _, o = attn_full(body, "values")
                for c in range(CB):
                    last = act.activation(vx[:, u, c, :, 0:HD],
                                          o[:, c * D:(c + 1) * D].rearrange("p (h d) -> p h d", d=HD),
                                          ACT.Copy, scale=1.0 / PS)
                last.then_inc(Att.v, 1)

            def exp(b, s):
                act.wait_ge(Att.scoreT, 16 * b + s + 1)
                if s % 4 == 0 and not (isinstance(b, int) and 4 * b + s // 4 < 2):
                    act.wait_ge(Att.pv, 4 * b + s // 4 - 1)
                act.activation(prb[:, s % 8, :], ps[:, s % 2, :], ACT.Exp, scale=HD ** -0.5 / (PS * PS))\
                    .then_inc(Att.prob, 1)

            def sums_out(b, jp):
                act.wait_ge(Att.pv, 4 * b + 2 * jp + 2)
                act.activation(oT[:, jp, :], ps[:, 4 + jp, :], ACT.Copy).then_inc(Att.oT, 1)

            def attn_hi(body):
                _, o = attn_full(body, "attn")
                act.activation(ahi, o[:, 0:SEQ], ACT.Copy, scale=XS).then_inc(Att.ahi, 1)

            def attn_body(b, u, body, output, ahead, project2):
                for s in range(16):
                    exp(b, s)
                    if s == 2 and output:
                        sums_out(b - 1, 1)
                    if s == 4 and project2:
                        qk_hi(body)
                    if s == 5 and ahead:
                        values(body, 1 - u)
                    if s == 8 and project2:
                        stack(body, "K0", u)
                    if s == 10 and output:
                        attn_hi(body)
                    if s == 12:
                        sums_out(b, 0)
                    if s == 12 and project2:
                        stack(body, "Q0", u)
                    if s == 14 and project2:
                        stack(body, "K1", u)
                    if s == 15 and project2:
                        stack(body, "Q1", u)

            def attn_start(body, body1):
                act.activation(warm[:, :], eps[:, 0:1], ACT.Exp)
                qk_hi(body)
                for name in STACKS:
                    stack(body, name, 0)
                values(body1, 0)
                qk_hi(body1)
                for name in STACKS:
                    stack(body1, name, 1)

            def attn_end(body, b):
                sums_out(b, 1)
                attn_hi(body)

            act.wait_ge(const_made, 1)
            act.activation(warm[:, :], eps[:, 0:1], ACT.Sqrt)
            std(0)
            act.wait_ge(wT_turned, 1)
            act.activation(b1T[:, :], ps[:, 1, 3 * P:3 * P + NE * CH], ACT.Copy)
            act.activation(waT[:, 0, :], ps[:, 0, 0:3 * D], ACT.Copy, scale=WS)
            act.activation(wbT[:, 0, 0:D], ps[:, 0, 3 * D:4 * D], ACT.Copy, scale=WS)
            act.activation(wbT[:, 0, D:4 * D], ps[:, 1, 0:3 * D], ACT.Copy, scale=WS)
            act.activation(gws[:, 0, :], gstage, ACT.Copy, scale=WS).then_inc(wT_hi, 1)
            norm(0)
            mix()
            std(1)
            norm(1)
            moe_blocks(0)
            std(2)
            norm(2)
            attention(act, attn_start, attn_body, attn_end)
            std(3)
            norm(3)
            moe_blocks(1)

        @block.vector
        def _(dve):
            def over(ap, axis, n):
                shape = list(ap.shape)
                shape.insert(axis, n)
                return ap.unsqueeze(axis).to_broadcast(shape)

            def tile_stats(b):
                for c in range(CB):
                    last = dve.bn_stats(stats[:, ds(2 * b + c, 1), :], xres[:, ds(2 * b + c, 1), :])
                last.then_inc(Ln.stats, 1)

            for g in range(NG):
                dve.wait_ge(x_in[g], 16)
                for b in range(GB * g, GB * (g + 1)):
                    tile_stats(b)
            def norm(r):
                l, first = Ln, r * NBATCH
                dve.wait_ge(l.stats, (r + 1) * NBATCH)
                dve.tensor_tensor(mean[:, :], stats[:, :, 1], stats[:, :, 4], ALU.add)
                dve.tensor_tensor(var[:, :], stats[:, :, 2], stats[:, :, 5], ALU.add)
                dve.tensor_tensor(gap[:, :], stats[:, :, 1], stats[:, :, 4], ALU.subtract).then_inc(l.merge, 1)
                dve.wait_ge(l.merge, 2 * r + 1)
                dve.tensor_scalar(mean[:, :], mean[:, :], 0.5, None, ALU.mult)
                dve.tensor_tensor(gap[:, :], gap[:, :], gap[:, :], ALU.mult).then_inc(l.merge, 1)
                dve.wait_ge(l.merge, 2 * r + 2)
                dve.scalar_tensor_tensor(var[:, :], gap[:, :], D / 4.0, var[:, :], ALU.mult, ALU.add).then_inc(l.var, 1)
                dve.wait_ge(l.std, r + 1)
                dve.reciprocal(rstd[:, :], rstd[:, :]).then_inc(l.rstd, 1)
                dve.wait_ge(l.rstd, r + 1)

                def norm_rows(g):
                    for t in range(GT * g, GT * (g + 1)):
                        last = dve.tensor_scalar(xn[:, t, :], xres[:, t, :], mean[:, t:t + 1], rstd[:, t:t + 1],
                                                 ALU.subtract, ALU.mult)
                    last.then_inc(l.norm, 1)

                def lo(g):
                    dve.wait_ge(l.hi, NG * r + g + 1)
                    h = group(hl, g)
                    dve.scalar_tensor_tensor(h[:, :, D:2 * D], group(xn, g), XS, h[:, :, 0:D],
                                             ALU.mult, ALU.subtract).then_inc(l.lo, 1)

                def copy_out(b):
                    dve.wait_ge(l.turned, first + b + 1)
                    dve.tensor_copy(two(xT, b), LB[b % GB][:, 0:4 * P].rearrange("p (c f) -> p c f", c=CB))\
                        .then_inc(l.xTv, 1)

                norm_rows(0)
                norm_rows(1)
                for g in range(2, NG):
                    lo(g - 2)
                    norm_rows(g)
                lo(NG - 2)
                lo(NG - 1)
                for b in VBATCH:
                    copy_out(b)

            def mix():
                def clamp(b, u):
                    dve.wait_ge(Mix.std, b + 1)
                    dve.tensor_scalar(rnorm[:, u, :, :], rnorm[:, u, :, :], PS * 1e-12, None, ALU.max)\
                        .then_inc(Mix.clamped, 1)

                def invert(b, u):
                    dve.wait_ge(Mix.clamped, b + 1)
                    dve.reciprocal(rnorm[:, u, :, :], rnorm[:, u, :, :]).then_inc(Mix.rnorm, 1)

                def front(b, u):
                    dve.wait_ge(Mix.rnorm, b + 1)
                    dve.wait_ge(Mix.qv, b + 1)
                    for c in range(CB):
                        last = dve.scalar_tensor_tensor(kv[:, u, c, :], ps[:, 2 * u + c, D:2 * D], rnorm[:, u, c, 1:2],
                                                        qvs[:, u, c, 1, :], ALU.mult, ALU.mult)
                    last.then_inc(Mix.kv, 1)

                def back(b, u, c):
                    if c == 0:
                        dve.wait_ge(Mix.mean, b + 1)
                    return dve.scalar_tensor_tensor(qg[:, u, c, :], qvs[:, u, c, 0, :], rnorm[:, u, c, 0:1],
                                                    ps[:, 4 + u, 0:D], ALU.mult, ALU.mult)

                def add(b, u):
                    dve.wait_ge(Mix.qg, b + 1)
                    dve.tensor_tensor(two(xres, b), two(xres, b), qg[:, u, :, :], ALU.add).then_inc(Mix.done, 1)

                def moments(b):
                    dve.wait_ge(Mix.done, b + 1)
                    tile_stats(b)

                def step(b, u):
                    ahead = not (isinstance(b, int) and b == LAST)
                    if ahead:
                        clamp(b + 1, 1 - u)
                    back(b, u, 0)
                    if ahead:
                        invert(b + 1, 1 - u)
                    back(b, u, 1).then_inc(Mix.qg, 1)
                    if ahead:
                        front(b + 1, 1 - u)
                    if not (isinstance(b, int) and b == 0):
                        moments(b - 1)
                    add(b, u)

                clamp(0, 0)
                invert(0, 0)
                front(0, 0)
                step(0, 0)
                step(1, 1)
                with dve.Fori(1, NBATCH // 2 - 1) as i:
                    for u in range(2):
                        step(2 * i + u, u)
                step(LAST - 1, 0)
                step(LAST, 1)
                moments(LAST)

            def moe_blocks(r):
                m = moe[r]
                steps = [0]

                def link(ins):
                    steps[0] += 1
                    ins.then_inc(m.step, 1)
                    dve.wait_ge(m.step, steps[0])

                dve.sem_inc(m.y, 2)
                logit = GATE.rearrange("p (t e) -> p t e", e=E)
                iota_e = over(iota_f[:, 0:E], 1, T)
                dve.wait_ge(m.logits, 1)
                link(dve.tensor_reduce(rs[0][:, :], logit, AX_X, ALU.max))
                dve.tensor_tensor(prob[:, :, :], logit, over(rs[0][:, :], 2, E), ALU.subtract).then_inc(m.shifted, 1)
                link(dve.tensor_tensor(rt[0][:, :, :], logit, over(rs[0][:, :], 2, E), ALU.is_equal))
                for k in range(TOPK):
                    if k == 1:
                        dve.wait_ge(m.exp, 1)
                        link(dve.scalar_tensor_tensor(rt[2][:, :, :], mask[0][:, :, :], -2.0, prob[:, :, :],
                                                      ALU.mult, ALU.add))
                        link(dve.tensor_reduce(topp[:, 1, :], rt[2][:, :, :], AX_X, ALU.max))
                        link(dve.tensor_tensor(rt[0][:, :, :], rt[2][:, :, :], over(topp[:, 1, :], 2, E), ALU.is_equal))
                    link(dve.scalar_tensor_tensor(rt[1][:, :, :], rt[0][:, :, :], -float(E), iota_e, ALU.mult, ALU.add))
                    link(dve.tensor_reduce(rs[k][:, :], rt[1][:, :, :], AX_X, ALU.min))
                    link(dve.tensor_tensor(mask[k][:, :, :], rt[1][:, :, :], over(rs[k][:, :], 2, E), ALU.is_equal))
                dve.tensor_tensor(mask16[:, :, :].rearrange("p e t -> p t e"), mask[0][:, :, :], mask[1][:, :, :],
                                  ALU.add).then_inc(m.mask, 1)
                dve.memset(e8[3][:, :], 1.0)
                dve.wait_ge(m.rank, 1)
                flat = "p e t -> p (e t)"
                link(dve.tensor_tensor_scan(cum[:, :, :].rearrange(flat), reset[:, :, :].rearrange(flat), TOT,
                                            0.0, ALU.mult, ALU.add))
                link(dve.tensor_scalar(e8[0][:, :], cum[:, :, T - 1], 1.0 / BR, (BR - 1.0) / BR - mid(BR),
                                       ALU.mult, ALU.add))
                link(dve.tensor_scalar(e8[0][:, :], e8[0][:, :], RND, RND, ALU.add, ALU.subtract))
                link(dve.tensor_tensor_scan(e8[1][:, :], e8[3][:, :], e8[0][:, :], 0.0, ALU.mult, ALU.add))
                link(dve.tensor_tensor(e8[2][:, :], e8[1][:, :], e8[0][:, :], ALU.subtract))
                link(dve.tensor_tensor(slotb[:, :, :].rearrange(flat), cum[:, :, :].rearrange(flat), TOT, ALU.subtract))
                link(dve.scalar_tensor_tensor(slotb[:, :, :], over(e8[2][:, :], 2, T), float(BR), slotb[:, :, :],
                                              ALU.mult, ALU.add))
                link(dve.tensor_tensor(slotb[:, :, :].rearrange(flat), slotb[:, :, :].rearrange(flat), RANK, ALU.add))
                for k in range(TOPK):
                    link(dve.tensor_tensor(rt[0][:, :, :], mask[k][:, :, :], slotb[:, :, :].rearrange("p e t -> p t e"),
                                           ALU.mult))
                    link(dve.tensor_reduce(slot[:, k, :], rt[0][:, :, :], AX_X, ALU.add))
                link(dve.tensor_scalar(blk[:, :, :], slot[:, :, :], 1.0 / P, -mid(P), ALU.mult, ALU.add))
                link(dve.tensor_scalar(blk[:, :, :], blk[:, :, :], RND, RND, ALU.add, ALU.subtract))
                dve.tensor_copy(blk16[:, :, :].rearrange("p t k -> p k t"), blk[:, :, :])
                link(dve.scalar_tensor_tensor(row16[:, :, :].rearrange("p t k -> p k t"), blk[:, :, :], -float(P),
                                              slot[:, :, :], ALU.mult, ALU.add))

                def split(n, u):
                    dve.wait_ge(m.gelu, n + 1)
                    dve.tensor_scalar(hhi[:, u, :], h32[:, u, :], XS, None, ALU.mult).then_inc(m.hi, 1)
                    dve.wait_ge(m.hi, n + 1)
                    dve.scalar_tensor_tensor(hlo[:, u, :], h32[:, u, :], XS, hhi[:, u, :], ALU.mult, ALU.subtract)\
                        .then_inc(m.split, 1)

                def wide(ap, g, n):
                    return ap[:, ds(4 * g, 4), :].unsqueeze(3).to_broadcast([P, 4, TOPK, n])

                def columns(n):
                    return iota16[:, 0:n].unsqueeze(1).unsqueeze(1).to_broadcast([P, 4, TOPK, n])

                def onehot(g, u):
                    if not (isinstance(g, int) and g < 2):
                        dve.wait_ge(m.index, g - 1)
                    dve.tensor_tensor(oneblk[:, u, :, :, :], columns(NT), wide(blk16, g, NT), ALU.is_equal)\
                        .then_inc(m.inblk, 1)
                    dve.tensor_tensor(onerow[:, u, :, :, :], columns(P), wide(row16, g, P), ALU.is_equal)\
                        .then_inc(m.onehot, 1)

                onehot(0, 0)
                onehot(1, 1)
                with dve.Fori(1, T // 8) as i:
                    for u in range(2):
                        onehot(2 * i + u, u)
                link(dve.tensor_tensor(bexp[:, :, :], over(e8[1][:, :], 1, NBLK), over(iota_f[:, 0:NBLK], 2, E),
                                       ALU.is_le))
                link(dve.tensor_reduce(bexpf[:, :], bexp[:, :, :], AX_X, ALU.add))
                link(dve.tensor_scalar(bexp_i[:, :], bexpf[:, :], float(E - 1), None, ALU.min))
                dve.tensor_copy(slot_i[:, :, :], slot[:, :, :])
                dve.wait_ge(m.index, T // 4 + 1)
                dve.tensor_scalar(tok_i[:, :], IDX, float(MIDDLE), None, ALU.add).then_inc(m.tok, 1)

                def experts(n, k):
                    return nc.values_load_multi_w_load_instructions(
                        bexp_i[0:1, ds(n, k)], engines=[mybir.EngineType.DVE], min_val=0, max_val=E - 1,
                        skip_runtime_bounds_check_because="VectorE kept it within 0 and E - 1")[1]

                def result_routed(n, u, i, e):
                    dve.wait_ge(m.down, n + 1)
                    dve.wait_ge(m.y_out[u], 16 * (i + 1))
                    dve.scalar_tensor_tensor(yst[:, u, :, :], YB[u % 2], 1.0 / PS,
                                             b2s[:, ds(e, 1), :].to_broadcast([P, BT, D]), ALU.mult, ALU.add)\
                        .then_inc(m.y, 1)

                link(dve.tensor_reduce(topp[:, 0, :], prob[:, :, :], AX_X, ALU.max))
                link(dve.tensor_reduce(rs[0][:, :], prob[:, :, :], AX_X, ALU.add))
                link(dve.reciprocal(rs[1][:, :], rs[0][:, :]))
                link(dve.tensor_tensor(topp[:, :, :], topp[:, :, :], over(rs[1][:, :], 1, TOPK), ALU.mult))
                link(dve.tensor_tensor(rs[0][:, :], topp[:, 0, :], topp[:, 1, :], ALU.add))
                link(dve.tensor_scalar(rs[1][:, :], rs[0][:, :], 1e-9, None, ALU.add))
                link(dve.reciprocal(rs[2][:, :], rs[1][:, :]))
                link(dve.tensor_tensor(wtop[:, :, :], topp[:, :, :], over(rs[2][:, :], 1, TOPK), ALU.mult))

                split(0, 0)
                split(1, 1)
                dve.wait_ge(b2_in, 16)
                with dve.Fori(0, LOOPED) as i:
                    es = experts(4 * i, 4)
                    for u in range(4):
                        n = 4 * i + u
                        result_routed(n, u, i, es[u])
                        split(n + 2, u % 2)
                es = experts(4 * LOOPED, REST)
                for u in range(REST):
                    n = 4 * LOOPED + u
                    result_routed(n, u, LOOPED, es[u])
                    split(n + 2, u % 2)

                def result_shared(n, v):
                    dve.wait_ge(m.down, NBLK + n + 1)
                    o = two(xres, n)
                    dve.scalar_tensor_tensor(o, YB[(NBLK + v) % 2], 1.0 / PS, o, ALU.mult, ALU.add).then_inc(m.y, 1)

                def combine(f, v, i):
                    dve.wait_ge(m.y, 2 + NBLK + f + 1)
                    dve.wait_ge(m.ygath[v], 64 * (i + 1))
                    for k in range(TOPK):
                        if k:
                            dve.wait_ge(m.half, 2 * f + 2)
                        for c in range(2):
                            t = 2 * f + c
                            o = xres[:, ds(t, 1), :]
                            dve.scalar_tensor_tensor(o, gy[:, v, 2 * c + k, :].unsqueeze(1), wtop[:, k, ds(t, 1)], o,
                                                     ALU.mult, ALU.add).then_inc((m.half, m.last)[k], 1)

                def moments(f):
                    if r == 0:
                        dve.wait_ge(m.last, 2 * f + 2)
                        tile_stats(f)

                dve.wait_ge(Ln.added, (r + 1) * NG)
                for n in range(2):
                    result_shared(n, n)
                    split(NBLK + n + 2, (NBLK + n) % 2)
                with dve.Fori(0, NS // 4 - 1) as i:
                    for v in range(4):
                        n = 4 * i + v + 2
                        result_shared(n, v % 2)
                        split(NBLK + n + 2, (NBLK + v) % 2)
                        combine(n - 2, v, i)
                        moments(n - 2)
                for v in range(4):
                    if v < 2:
                        result_shared(NS - 2 + v, v)
                    combine(NS - 4 + v, v, NS // 4 - 1)
                    moments(NS - 4 + v)

            def attn_full(body, name):
                dve.wait_ge(Att.full, body.filled(name))
                return body.bank(name), ps[:, 6 + body.bank(name), :]

            def qk_lo(body, b):
                _, o = attn_full(body, "QK")
                dve.wait_ge(Att.hi, b + 1)
                for j in range(2):
                    last = dve.scalar_tensor_tensor(qklo[:, j, :], o[:, j * SEQ:(j + 1) * SEQ], qkb[:, j:j + 1],
                                                    qkhi[:, j, :], ALU.add, ALU.subtract)
                last.then_inc(Att.qk, 1)

            def maxima(body, u, jp):
                _, o = attn_full(body, f"maxima{jp}")
                dve.tensor_tensor(qst2[:, 2 * jp:2 * jp + 2, :], o.rearrange("p (j n) -> p j n", j=2),
                                  qst[:, u, 2 * jp:2 * jp + 2, :], ALU.add).then_inc(Att.q2, 1)

            def maximum(b, s):
                jp, c, hh = s // 8, s // 4 % 2, s % 4
                dve.wait_ge(Att.score, 16 * b + s + 1)
                j = 8 * jp + hh
                dve.tensor_reduce(mx[:, c, j:j + 5:4], ps[:, 2 + s % 2, :].rearrange("p (n k) -> p n k", n=2),
                                  AX_X, ALU.max).then_inc(Att.mx, 1)

            def negate(b, jp):
                slots = negmax.rearrange("p c (h s) -> p c h s", s=32)[:, :, 8 * jp:8 * jp + 8, :]
                largest = mx[:, :, 8 * jp:8 * jp + 8]
                dve.wait_ge(Att.mx, 16 * b + 8 * jp + 8)
                dve.tensor_scalar(slots[:, :, :, 24], largest, -1.0 / KX, None, ALU.mult).then_inc(Att.neghi, 1)
                dve.wait_ge(Att.neghi, 2 * b + jp + 1)
                dve.scalar_tensor_tensor(slots[:, :, :, 25], largest, -1.0 / KX, slots[:, :, :, 24],
                                         ALU.mult, ALU.subtract).then_inc(Att.neg, 1)

            def normalise(body, b, jp):
                _, o = attn_full(body, f"back{jp}")
                heads = o.rearrange("p (c h s) -> p c h s", c=CB, s=32)
                sums = rsum[:, :, 8 * jp:8 * jp + 8]
                dve.reciprocal(sums, heads[:, :, :, HD]).then_inc(Att.rsum, 1)
                dve.wait_ge(Att.rsum, 2 * b + jp + 1)
                dve.tensor_tensor(attn.rearrange("p c (h d) -> p c h d", d=HD)[:, :, 8 * jp:8 * jp + 8, :],
                                  heads[:, :, :, 0:HD], over(sums, 3, HD), ALU.mult).then_inc(Att.attn, 1)

            def attn_lo(body, b):
                _, o = attn_full(body, "attn")
                dve.wait_ge(Att.ahi, b + 1)
                dve.scalar_tensor_tensor(alo, o[:, 0:SEQ], XS, ahi, ALU.mult, ALU.subtract).then_inc(Att.alo, 1)

            def add_result(body, b):
                _, o = attn_full(body, "out")
                dve.scalar_tensor_tensor(two(xres, b), o[:, 0:CB * D].rearrange("p (c d) -> p c d", c=CB),
                                         1.0 / PS, two(xres, b), ALU.mult, ALU.add).then_inc(Att.done, 1)

            def moments(b):
                dve.wait_ge(Att.done, b + 1)
                tile_stats(b)

            def attn_body(b, u, body, output, ahead, project2):
                for s in range(16):
                    if ahead:
                        maximum(b + 1, s)
                    if s == 2 and output:
                        normalise(body, b - 1, 0)
                    if s == 3:
                        maxima(body, u, 1)
                    if s == 5 and project2:
                        qk_lo(body, b + 2)
                    if s == 7 and ahead:
                        negate(b + 1, 0)
                    if s == 8 and output:
                        normalise(body, b - 1, 1)
                    if s == 10 and ahead:
                        maxima(body, 1 - u, 0)
                    if s == 11 and output:
                        attn_lo(body, b - 1)
                    if s == 14 and output:
                        add_result(body, b - 1)
                    if s == 15 and output:
                        moments(b - 1)
                if ahead:
                    negate(b + 1, 1)

            def attn_start(body, body1):
                qk_lo(body, 0)
                qk_lo(body1, 1)
                for s in range(16):
                    maximum(0, s)
                    if s == 7:
                        dve.wait_ge(Att.cleared, 1)
                        negate(0, 0)
                    if s == 13:
                        maxima(body1, 0, 0)
                negate(0, 1)

            def attn_end(body, b):
                normalise(body, b, 0)
                normalise(body, b, 1)
                attn_lo(body, b)
                add_result(body, b)
                moments(b)

            norm(0)
            dve.wait_ge(bias_in, 16 * len(BIASES))
            dve.wait_ge(const_made, 2)
            dve.tensor_scalar(bhi[:, 0:NBIAS - 1], bnat[:, 0:NBIAS - 1], WS, None, ALU.mult)
            dve.tensor_scalar(bhi[0:E, NBIAS - 1:NBIAS], bnat[0:E, NBIAS - 1:NBIAS], WS, None, ALU.mult)\
                .then_inc(bias_hi, 1)
            dve.wait_ge(bias_hi, 1)
            dve.scalar_tensor_tensor(blo[:, 0:NBIAS - 1], bnat[:, 0:NBIAS - 1], WS, bhi[:, 0:NBIAS - 1],
                                     ALU.mult, ALU.subtract)
            dve.scalar_tensor_tensor(blo[0:E, NBIAS - 1:NBIAS], bnat[0:E, NBIAS - 1:NBIAS], WS,
                                     bhi[0:E, NBIAS - 1:NBIAS], ALU.mult, ALU.subtract).then_inc(bias_lo, 1)
            dve.wait_ge(qkb_in, 2 * 16)
            dve.tensor_scalar(qkb[:, :], qkb[:, :], PS, None, ALU.mult)
            dve.tensor_scalar(part_i[:, 1:2], part_i[:, 0:1], 31, 3, ALU.bitwise_and, ALU.arith_shift_right)\
                .then_inc(rows_found, 1)
            dve.wait_ge(rows_found, 1)
            dve.tensor_scalar(kxrow[:, :], part_i[:, 1:2], 3.0, KX, ALU.is_equal, ALU.mult)
            dve.wait_ge(wT_hi, 1)
            dve.scalar_tensor_tensor(waT[:, 1, :], ps[:, 0, 0:3 * D], WS, waT[:, 0, :], ALU.mult, ALU.subtract)
            dve.scalar_tensor_tensor(wbT[:, 1, 0:D], ps[:, 0, 3 * D:4 * D], WS, wbT[:, 0, 0:D],
                                     ALU.mult, ALU.subtract)
            dve.scalar_tensor_tensor(wbT[:, 1, D:4 * D], ps[:, 1, 0:3 * D], WS, wbT[:, 0, D:4 * D],
                                     ALU.mult, ALU.subtract)
            dve.scalar_tensor_tensor(gws[:, 1, :], gstage, WS, gws[:, 0, :], ALU.mult, ALU.subtract)\
                .then_inc(wT_lo, 1)
            mix()
            norm(1)
            moe_blocks(0)
            dve.wait_ge(moe[0].last, T)
            norm(2)
            attention(dve, attn_start, attn_body, attn_end)
            norm(3)
            moe_blocks(1)


_INS = ['L0_attn_a_x', 'L0_attn_a_W_q', 'L0_attn_a_W_k', 'L0_attn_a_W_v', 'L0_attn_b_qkv_w', 'L0_attn_b_qkv_b',
        'L0_attn_b_out_w', 'L0_attn_b_out_b', 'L0_ffn_gate_w', 'L0_ffn_gate_b', 'L0_ffn_sh_w1', 'L0_ffn_sh_b1',
        'L0_ffn_sh_w2', 'L0_ffn_sh_b2', 'L0_ffn_ew1', 'L0_ffn_eb1', 'L0_ffn_ew2', 'L0_ffn_eb2']


def kernel(**inputs):
    import numpy as np
    import concourse.bacc as bacc
    from concourse.bass_utils import run_bass_kernel_spmd

    nc = bacc.Bacc("TRN2", target_bir_lowering=False, num_devices=1)
    arrays, args = {}, []
    for name in _INS:
        a = np.ascontiguousarray(inputs[name])
        arrays[f"in_{name}"] = a
        args.append(nc.dram_tensor(f"in_{name}", a.shape, mybir.dt.from_np(a.dtype), kind="ExternalInput").ap())
    shape = inputs['L0_attn_a_x'].shape
    args.append(nc.dram_tensor("out_x", shape, F32, kind="ExternalOutput").ap())
    build(nc, *args)
    r = run_bass_kernel_spmd(nc, [arrays], core_ids=[0])
    return r.results[0]["out_x"]
```
